# Optimizing a Trainium2 kernel written in Bass

```python
import numpy as np
import jax
import jax.numpy as jnp

def _softmax(x, axis=-1):
    return jax.nn.softmax(x, axis=axis)

def _gelu(x):
    return jax.nn.gelu(x, approximate=True)

def _silu(x):
    return jax.nn.silu(x)

def _sigmoid(x):
    return jax.nn.sigmoid(x)

def _layernorm(x, axis=-1, eps=1e-05):
    m = jnp.mean(x, axis=axis, keepdims=True)
    v = jnp.var(x, axis=axis, keepdims=True)
    return (x - m) / jnp.sqrt(v + eps)

def _scatter_add(tgt, idx, src, axis=0):
    return tgt.at[idx].add(src)

def _segment_sum(src, seg, n):
    return jax.ops.segment_sum(src, seg, n)
kernel_name = 'mk_seq_postln_d1_jaxref_r8_a76526'

def setup_inputs(seed: int=0):
    np.random.seed(seed)
    _w = jnp.asarray

    def _L0_attn_setup():
        import jax, jax.numpy as jnp
        import numpy as np
        H_SIZE = 256
        NUM_K_HEADS = 16
        NUM_V_HEADS = 32
        DK = 128
        DV = 128
        KEY_DIM = NUM_K_HEADS * DK
        VALUE_DIM = NUM_V_HEADS * DV
        CONV_DIM = 2 * KEY_DIM + VALUE_DIM
        KERNEL = 4
        EPS = 1e-06
        B, S = (2, 256)

        def _l2norm(x, eps=1e-06):
            return x * jax.lax.rsqrt(jnp.sum(x * x, axis=-1, keepdims=True) + eps)

        def _causal_conv(x, w):
            K = w.shape[-1]
            Sq = x.shape[1]
            xp = jnp.pad(x, ((0, 0), (K - 1, 0), (0, 0)))
            out = xp[:, 0:Sq, :] * w[None, None, :, 0]
            for j in range(1, K):
                out = out + xp[:, j:j + Sq, :] * w[None, None, :, j]
            return out

        def _forward(hidden_states, w_qkv, w_z, w_b, w_a, conv_w, dt_bias, A_log, norm_gamma, w_out):
            Bq, Sq, _ = hidden_states.shape
            mixed = hidden_states @ w_qkv
            z = (hidden_states @ w_z).reshape(Bq, Sq, NUM_V_HEADS, DV)
            b = hidden_states @ w_b
            a = hidden_states @ w_a
            mixed = jax.nn.silu(_causal_conv(mixed, conv_w))
            q, k, v = jnp.split(mixed, [KEY_DIM, 2 * KEY_DIM], axis=-1)
            q = q.reshape(Bq, Sq, NUM_K_HEADS, DK)
            k = k.reshape(Bq, Sq, NUM_K_HEADS, DK)
            v = v.reshape(Bq, Sq, NUM_V_HEADS, DV)
            nrep = NUM_V_HEADS // NUM_K_HEADS
            q = jnp.repeat(q, nrep, axis=2)
            k = jnp.repeat(k, nrep, axis=2)
            beta = jax.nn.sigmoid(b)
            g = -jnp.exp(A_log)[None, None, :] * jax.nn.softplus(a + dt_bias[None, None, :])
            qf = _l2norm(q.astype(jnp.float32)) * DK ** (-0.5)
            kf = _l2norm(k.astype(jnp.float32))
            vf = v.astype(jnp.float32)
            gf = g.astype(jnp.float32)
            bf = beta.astype(jnp.float32)

            def step(state, xs):
                q_t, k_t, v_t, g_t, b_t = xs
                state = state * jnp.exp(g_t)[..., None, None]
                kv = jnp.einsum('bhk,bhkv->bhv', k_t, state)
                delta = (v_t - kv) * b_t[..., None]
                state = state + jnp.einsum('bhk,bhv->bhkv', k_t, delta)
                out = jnp.einsum('bhk,bhkv->bhv', q_t, state)
                return (state, out)
            mv = lambda x: jnp.moveaxis(x, 1, 0)
            xs = (mv(qf), mv(kf), mv(vf), mv(gf), mv(bf))
            state0 = jnp.zeros((Bq, NUM_V_HEADS, DK, DV), jnp.float32)
            _, outs = jax.lax.scan(step, state0, xs)
            o = jnp.moveaxis(outs, 0, 1)
            o = o * jax.nn.silu(z.astype(jnp.float32))
            o = o * jax.lax.rsqrt(jnp.mean(o * o, axis=-1, keepdims=True) + EPS)
            o = o * norm_gamma
            o = o.reshape(Bq, Sq, VALUE_DIM).astype(hidden_states.dtype)
            return o @ w_out
        key = jax.random.key(seed)
        ks = jax.random.split(key, 8)
        w = lambda k, shape, s: jax.random.normal(k, shape, jnp.float32) * s
        return {'hidden_states': jax.random.normal(ks[0], (B, S, H_SIZE), jnp.float32), 'w_qkv': w(ks[1], (H_SIZE, CONV_DIM), 0.02), 'w_z': w(ks[2], (H_SIZE, VALUE_DIM), 0.02), 'w_b': w(ks[3], (H_SIZE, NUM_V_HEADS), 0.02), 'w_a': w(ks[4], (H_SIZE, NUM_V_HEADS), 0.02), 'conv_w': w(ks[5], (CONV_DIM, KERNEL), 0.2), 'dt_bias': jnp.ones((NUM_V_HEADS,), jnp.float32), 'A_log': jnp.zeros((NUM_V_HEADS,), jnp.float32), 'norm_gamma': jnp.ones((DV,), jnp.float32), 'w_out': w(ks[6], (VALUE_DIM, H_SIZE), 0.02)}
    _L0_attn_in = _L0_attn_setup()

    def _L0_ffn_setup():
        import jax, jax.numpy as jnp
        import numpy as np
        B, S, D = (4, 256, 256)
        E, F, K = (8, 128, 2)
        SF = 128
        EPS = 1e-06

        def _rmsnorm(x, w, eps=EPS):
            var = jnp.mean(x * x, axis=-1, keepdims=True)
            return x * jax.lax.rsqrt(var + eps) * w
        key = jax.random.key(seed)
        ks = jax.random.split(key, 9)
        g = lambda k, shape, scale: jax.random.normal(k, shape, jnp.float32) * scale
        return {'x': g(ks[0], (B, S, D), 1.0), 'rms_weight': jnp.ones((D,), jnp.float32), 'router_w': g(ks[1], (D, E), 0.02), 'w_gate': g(ks[2], (E, D, F), 0.02), 'w_up': g(ks[3], (E, D, F), 0.02), 'w_down': g(ks[4], (E, F, D), 0.02), 'sw_gate': g(ks[5], (D, SF), 0.02), 'sw_up': g(ks[6], (D, SF), 0.02), 'sw_down': g(ks[7], (SF, D), 0.02)}
    _L0_ffn_in = _L0_ffn_setup()
    _d = {'L0_attn_hidden_states': _L0_attn_in['hidden_states'], 'L0_attn_w_qkv': _L0_attn_in['w_qkv'], 'L0_attn_w_z': _L0_attn_in['w_z'], 'L0_attn_w_b': _L0_attn_in['w_b'], 'L0_attn_w_a': _L0_attn_in['w_a'], 'L0_attn_conv_w': _L0_attn_in['conv_w'], 'L0_attn_dt_bias': _L0_attn_in['dt_bias'], 'L0_attn_A_log': _L0_attn_in['A_log'], 'L0_attn_norm_gamma': _L0_attn_in['norm_gamma'], 'L0_attn_w_out': _L0_attn_in['w_out'], 'L0_ffn_rms_weight': _L0_ffn_in['rms_weight'], 'L0_ffn_router_w': _L0_ffn_in['router_w'], 'L0_ffn_w_gate': _L0_ffn_in['w_gate'], 'L0_ffn_w_up': _L0_ffn_in['w_up'], 'L0_ffn_w_down': _L0_ffn_in['w_down'], 'L0_ffn_sw_gate': _L0_ffn_in['sw_gate'], 'L0_ffn_sw_up': _L0_ffn_in['sw_up'], 'L0_ffn_sw_down': _L0_ffn_in['sw_down']}
    _x0 = _d['L0_attn_hidden_states']
    _d['L0_attn_hidden_states'] = jax.random.normal(jax.random.fold_in(jax.random.key(seed), 1), (4, 512, 256), dtype=_x0.dtype)
    del _x0
    return _d

def reference(L0_attn_hidden_states, L0_attn_w_qkv, L0_attn_w_z, L0_attn_w_b, L0_attn_w_a, L0_attn_conv_w, L0_attn_dt_bias, L0_attn_A_log, L0_attn_norm_gamma, L0_attn_w_out, L0_ffn_rms_weight, L0_ffn_router_w, L0_ffn_w_gate, L0_ffn_w_up, L0_ffn_w_down, L0_ffn_sw_gate, L0_ffn_sw_up, L0_ffn_sw_down):

    def _L0_attn_ref(hidden_states, w_qkv, w_z, w_b, w_a, conv_w, dt_bias, A_log, norm_gamma, w_out):
        import jax, jax.numpy as jnp
        import numpy as np
        H_SIZE = 256
        NUM_K_HEADS = 16
        NUM_V_HEADS = 32
        DK = 128
        DV = 128
        KEY_DIM = NUM_K_HEADS * DK
        VALUE_DIM = NUM_V_HEADS * DV
        CONV_DIM = 2 * KEY_DIM + VALUE_DIM
        KERNEL = 4
        EPS = 1e-06
        B, S = (2, 256)

        def _l2norm(x, eps=1e-06):
            return x * jax.lax.rsqrt(jnp.sum(x * x, axis=-1, keepdims=True) + eps)

        def _causal_conv(x, w):
            K = w.shape[-1]
            Sq = x.shape[1]
            xp = jnp.pad(x, ((0, 0), (K - 1, 0), (0, 0)))
            out = xp[:, 0:Sq, :] * w[None, None, :, 0]
            for j in range(1, K):
                out = out + xp[:, j:j + Sq, :] * w[None, None, :, j]
            return out

        def _forward(hidden_states, w_qkv, w_z, w_b, w_a, conv_w, dt_bias, A_log, norm_gamma, w_out):
            Bq, Sq, _ = hidden_states.shape
            mixed = hidden_states @ w_qkv
            z = (hidden_states @ w_z).reshape(Bq, Sq, NUM_V_HEADS, DV)
            b = hidden_states @ w_b
            a = hidden_states @ w_a
            mixed = jax.nn.silu(_causal_conv(mixed, conv_w))
            q, k, v = jnp.split(mixed, [KEY_DIM, 2 * KEY_DIM], axis=-1)
            q = q.reshape(Bq, Sq, NUM_K_HEADS, DK)
            k = k.reshape(Bq, Sq, NUM_K_HEADS, DK)
            v = v.reshape(Bq, Sq, NUM_V_HEADS, DV)
            nrep = NUM_V_HEADS // NUM_K_HEADS
            q = jnp.repeat(q, nrep, axis=2)
            k = jnp.repeat(k, nrep, axis=2)
            beta = jax.nn.sigmoid(b)
            g = -jnp.exp(A_log)[None, None, :] * jax.nn.softplus(a + dt_bias[None, None, :])
            qf = _l2norm(q.astype(jnp.float32)) * DK ** (-0.5)
            kf = _l2norm(k.astype(jnp.float32))
            vf = v.astype(jnp.float32)
            gf = g.astype(jnp.float32)
            bf = beta.astype(jnp.float32)

            def step(state, xs):
                q_t, k_t, v_t, g_t, b_t = xs
                state = state * jnp.exp(g_t)[..., None, None]
                kv = jnp.einsum('bhk,bhkv->bhv', k_t, state)
                delta = (v_t - kv) * b_t[..., None]
                state = state + jnp.einsum('bhk,bhv->bhkv', k_t, delta)
                out = jnp.einsum('bhk,bhkv->bhv', q_t, state)
                return (state, out)
            mv = lambda x: jnp.moveaxis(x, 1, 0)
            xs = (mv(qf), mv(kf), mv(vf), mv(gf), mv(bf))
            state0 = jnp.zeros((Bq, NUM_V_HEADS, DK, DV), jnp.float32)
            _, outs = jax.lax.scan(step, state0, xs)
            o = jnp.moveaxis(outs, 0, 1)
            o = o * jax.nn.silu(z.astype(jnp.float32))
            o = o * jax.lax.rsqrt(jnp.mean(o * o, axis=-1, keepdims=True) + EPS)
            o = o * norm_gamma
            o = o.reshape(Bq, Sq, VALUE_DIM).astype(hidden_states.dtype)
            return o @ w_out
        return _forward(hidden_states, w_qkv, w_z, w_b, w_a, conv_w, dt_bias, A_log, norm_gamma, w_out)

    def _L0_ffn_ref(x, rms_weight, router_w, w_gate, w_up, w_down, sw_gate, sw_up, sw_down):
        import jax, jax.numpy as jnp
        import numpy as np
        B, S, D = (4, 256, 256)
        E, F, K = (8, 128, 2)
        SF = 128
        EPS = 1e-06

        def _rmsnorm(x, w, eps=EPS):
            var = jnp.mean(x * x, axis=-1, keepdims=True)
            return x * jax.lax.rsqrt(var + eps) * w
        b, s, d = x.shape
        e = router_w.shape[1]
        h = _rmsnorm(x, rms_weight)
        ht = h.reshape(-1, d)
        t = ht.shape[0]
        logits = ht @ router_w
        probs = jax.nn.softmax(logits, axis=-1)
        topv, topi = jax.lax.top_k(probs, K)
        topv = topv / jnp.sum(topv, axis=-1, keepdims=True)
        w_dense = jnp.zeros((t, e), ht.dtype).at[jnp.arange(t)[:, None], topi].set(topv)
        g = jnp.einsum('td,edf->tef', ht, w_gate)
        u = jnp.einsum('td,edf->tef', ht, w_up)
        eo = jnp.einsum('tef,efd->ted', jax.nn.silu(g) * u, w_down)
        moe = jnp.einsum('te,ted->td', w_dense, eo)
        sh = jax.nn.silu(ht @ sw_gate) * (ht @ sw_up) @ sw_down
        return (moe + sh).reshape(b, s, d)
    x = L0_attn_hidden_states
    x = _layernorm(x + _L0_attn_ref(x, L0_attn_w_qkv, L0_attn_w_z, L0_attn_w_b, L0_attn_w_a, L0_attn_conv_w, L0_attn_dt_bias, L0_attn_A_log, L0_attn_norm_gamma, L0_attn_w_out), axis=-1)
    x = _layernorm(x + _L0_ffn_ref(x, L0_ffn_rms_weight, L0_ffn_router_w, L0_ffn_w_gate, L0_ffn_w_up, L0_ffn_w_down, L0_ffn_sw_gate, L0_ffn_sw_up, L0_ffn_sw_down), axis=-1)
    return x

_drawn_inputs = setup_inputs


def setup_inputs(seed=0):
    import zlib

    import numpy as np

    out = dict(_drawn_inputs(seed))
    spreads = {'L0_attn_dt_bias': (1.0, 0.6),
     'L0_attn_A_log': (0.0, 0.8),
     'L0_attn_norm_gamma': (1.0, 0.6),
     'L0_ffn_rms_weight': (1.0, 0.6)}
    factors = {'L0_attn_w_b': 6.199,
     'L0_attn_w_a': 8.0,
     'L0_ffn_router_w': 7.125,
     'L0_ffn_w_gate': 6.239,
     'L0_ffn_w_up': 6.16,
     'L0_ffn_w_down': 6.185,
     'L0_ffn_sw_gate': 4.491,
     'L0_ffn_sw_up': 4.392,
     'L0_ffn_sw_down': 4.421}
    for name, (base, spread) in spreads.items():
        noise = np.random.default_rng([zlib.crc32(name.encode()), seed]).standard_normal(out[name].shape)
        drawn = base * np.exp(spread * noise) if base else spread * noise
        out[name] = jnp.asarray(drawn.astype(out[name].dtype))
    for name, factor in factors.items():
        out[name] = (out[name] * factor).astype(out[name].dtype)
    return out
```

```python
from contextlib import ExitStack

import concourse.bass as bass
from concourse import mybir

F32 = mybir.dt.float32
F16 = mybir.dt.float16
BF16 = mybir.dt.bfloat16
U32 = mybir.dt.uint32
ALU = mybir.AluOpType
ACT = mybir.ActivationFunctionType
AX = mybir.AxisListType.X

P = 128
B, SEQ, D = 4, 512, 256
CH = SEQ // P
KT = D // P
KH, VH = 16, 2
TILES = B * CH
CELLS = CH * VH
BODIES = KH * B
TAPS = 4
GROUPS = 4
SCALE = float(P) ** -0.5
LEVELS = [2, 4, 8, 16, 32, 64]
NE, TOPS = 8, 8
NX = NE + 1
NQ = 6
Q_G, Q_BETA, Q_EG, Q_ESUF, Q_EEND, Q_NEG_EG = range(NQ)

SCHEDULE = [
    ("F", "scalars", 0),
    ("level", 0), ("F", "proj", 0), ("level", 1), ("F", "proj", 1), ("level", 2), ("F", "proj", 2),
    ("level", 3), ("F", "proj", 3), ("level", 4), ("F", "gate", 0), ("level", 5), ("F", "gate", 1),
    ("newton", 0), ("F", "norms", 0), ("chain", 0), ("F", "keys", 0), ("chain", 1),
    ("F", "values", 0), ("F", "values", 1), ("chain", 2), ("F", "products", 0), ("chain", 3),
    ("F", "decay", 0), ("F", "decay", 1), ("F", "system", 0), ("out", 0), ("gated", 0), ("F", "start", 0),
    ("project", 0),
]


def build_kernel(nc, x_rows, x_cols, w_heads, w_ab, conv_w, dt_bias, a_log, gamma, w_out,
                 rms_w, router_w, gate_up, down, tri, levels16, neg_mask, ident16, iota8, out):
    ctx = ExitStack()
    with ctx:
        def sb(name, shape, dt=F32):
            return ctx.enter_context(nc.sbuf_tensor(name, shape, dt))

        def sem(name):
            return ctx.enter_context(nc.semaphore(name))

        bank = [ctx.enter_context(nc.psum_tensor(f"bank{i}", [P, 512], F32)) for i in range(8)]
        F0, F1, F2, B0, B1, B2, B3, B4 = bank

        tri_sb = sb("tri_sb", [P, 4, P])
        upto, after, ident, ones = (tri_sb[:, i, :] for i in range(4))
        lev = sb("lev", [P, 1 + len(LEVELS), P], F16)
        negm = sb("negm", [P, 512], BF16)
        identb = sb("identb", [P, P], BF16)
        identh = sb("identh", [P, P], F16)
        iota_sb = sb("iota_sb", [P, NE])
        xT = sb("xT", [P, KT, TILES * P])
        wab = sb("wab", [P, KT, 64])
        vec32 = sb("vec32", [P, 2, 32])
        gam = sb("gam", [P, 1])
        cw_all = sb("cw_all", [P, KH, GROUPS * TAPS])
        sc_all = sb("sc_all", [P, BODIES, NQ * CELLS])
        acc = sb("acc", [P, TILES, D])
        w_kh = sb("w_kh", [P, KT, 768])
        wo_raw = sb("wo_raw", [P, VH, D])
        wo = sb("wo", [P, VH, D])
        cw = sb("cw", [P, 2, GROUPS * TAPS])
        sc = sb("sc", [P, 2, NQ * CELLS])
        conv = sb("conv", [P, GROUPS, SEQ])
        zone = sb("zone", [P, 5, 2048])

        def zoned(i, pattern, **sizes):
            return zone[:, i, :].rearrange(pattern, **sizes)

        qkT = zoned(0, "p (x a n) -> p x a n", x=2, a=2)
        vT = sb("vT", [P, VH, SEQ])
        sq = sb("sq", [P, 2 * SEQ])
        zs = zoned(1, "p (x c n) -> p x c n", x=2, c=CH)
        ss = sb("ss", [P, 2 * CH])
        lnss = sb("lnss", [P, 2 * CH])
        rqk = sb("rqk", [P, 2 * CH])
        nk = sb("nk", [P, CH])
        rk2 = sb("rk2", [P, CH])
        rqs = sb("rqs", [P, CH])
        cj = sb("cj", [P, CELLS])
        kfac = sb("kfac", [P, CELLS])
        keys = zoned(2, "p (x c n) -> p x c n", x=2, c=CELLS)
        vals = zoned(3, "p (x c n) -> p x c n", x=2, c=CELLS)
        gseg = sb("gseg", [P, CELLS, P])
        dec = sb("dec", [P, CELLS, P])
        decc = sb("decc", [P, CELLS, P])
        m32T = sb("m32T", [P, CELLS, P])
        mhiT = sb("mhiT", [P, 2, CELLS, P], F16)
        mloT = sb("mloT", [P, 2, CELLS, P], F16)
        pT = zoned(4, "p (x c n) -> p x c n", x=2, c=CELLS)
        X = sb("X", [P, 2, CELLS, P], F16)
        XT = sb("XT", [P, 2, CELLS, P], F16)
        N = sb("N", [P, CELLS, P], F16)
        TT = sb("TT", [P, CELLS, P])
        rhs = sb("rhs", [P, CELLS, P])
        U = sb("U", [P, CELLS, P])
        S = sb("S", [P, CH, VH * P])
        qs = sb("qs", [P, CELLS, P])
        og = sb("og", [P, CELLS, P])
        og2 = sb("og2", [P, CELLS, P])
        ms = sb("ms", [P, 3, CELLS])
        ogT = sb("ogT", [P, CELLS, P])

        s_const = sem("s_const")
        s_w = sem("s_w")
        s_wo = sem("s_wo")
        s_zero = sem("s_zero")
        s_abp = sem("s_abp")
        s_gates = sem("s_gates")
        s_gact = sem("s_gact")
        s_cum = sem("s_cum")
        s_scall = sem("s_scall")
        s_sc = sem("s_sc")
        s_proj = sem("s_proj")
        s_tap = sem("s_tap")
        s_conv = sem("s_conv")
        s_silu = sem("s_silu")
        s_zp = sem("s_zp")
        s_zs = sem("s_zs")
        s_sq = sem("s_sq")
        s_ssp = sem("s_ssp")
        s_ss = sem("s_ss")
        s_ln = sem("s_ln")
        s_rqk = sem("s_rqk")
        s_small = sem("s_small")
        s_zq = sem("s_zq")
        s_ktp = sem("s_ktp")
        s_keys = sem("s_keys")
        s_vtp = sem("s_vtp")
        s_vals = sem("s_vals")
        s_kq = sem("s_kq")
        s_seg = sem("s_seg")
        s_decp = sem("s_decp")
        s_dec = sem("s_dec")
        s_decc = sem("s_decc")
        s_m = sem("s_m")
        s_p = sem("s_p")
        s_fill = sem("s_fill")
        s_mhi = sem("s_mhi")
        s_mlo = sem("s_mlo")
        s_pair = sem("s_pair")
        s_xp = sem("s_xp")
        s_x0 = sem("s_x0")
        s_np = sem("s_np")
        s_n = sem("s_n")
        s_xyp = sem("s_xyp")
        s_xy = sem("s_xy")
        s_resp = sem("s_resp")
        s_res = sem("s_res")
        s_newp = sem("s_newp")
        s_new = sem("s_new")
        s_ksp = sem("s_ksp")
        s_r = sem("s_r")
        s_up = sem("s_up")
        s_u = sem("s_u")
        s_stp = sem("s_stp")
        s_st = sem("s_st")
        s_qsp = sem("s_qsp")
        s_qs = sem("s_qs")
        s_pup = sem("s_pup")
        s_o = sem("s_o")
        s_og = sem("s_og")
        s_og2 = sem("s_og2")
        s_ms = sem("s_ms")
        s_msl = sem("s_msl")
        s_on = sem("s_on")
        s_gtp = sem("s_gtp")
        s_gt = sem("s_gt")
        s_opp = sem("s_opp")
        s_acc = sem("s_acc")
        s_wog = sem("s_wog")
        s_attn = sem("s_attn")
        s_mw = sem("s_mw")
        s_xg = sem("s_xg")
        s_x1 = sem("s_x1")
        s_ln1 = sem("s_ln1")
        s_sqx = sem("s_sqx")
        s_x2 = sem("s_x2")
        s_h = sem("s_h")
        s_htp = sem("s_htp")
        s_ht = sem("s_ht")
        s_rtp = sem("s_rtp")
        s_rt = sem("s_rt")
        s_e2 = sem("s_e2")
        s_gup = sem("s_gup")
        s_sg = sem("s_sg")
        s_a = sem("s_a")
        s_dnp = sem("s_dnp")
        s_y = sem("s_y")
        s_ln2 = sem("s_ln2")
        s_out = sem("s_out")

        CONSTS = 12 * 16

        def body_steps(kh, last):
            for b in range(B):
                for step in SCHEDULE:
                    if step[0] == "F":
                        if not (last and b == B - 1):
                            yield step[1:], kh * B + b + 1, b + 1, kh + (b + 1) // B
                    else:
                        yield step, kh * B + b, b, kh

        def past_first(n):
            return not (isinstance(n, int) and n == 0)

        FRONT = [s[1:] for s in SCHEDULE if s[0] == "F"]

        def half(t, h):
            return t[:, CELLS // 2 * h:CELLS // 2 * (h + 1)]

        def bank4(t):
            return t[:, :].rearrange("p (x n) -> p x n", x=4)

        def scal(p, what, a, n=1):
            return sc[:, p, what * CELLS + a:what * CELLS + a + n]

        NG = BODIES * CELLS

        def gate_buffer(t, i):
            return t[:, :, :].rearrange("p a n -> p (a n)")[:, NG * i:NG * (i + 1)]

        a_in, b_in, al, a_abs = (gate_buffer(conv, i) for i in range(4))
        b_abs, gall = (gate_buffer(gseg, i) for i in range(2))
        e_a, e_b = (gate_buffer(dec, i) for i in range(2))
        ln_a, e_al = (gate_buffer(decc, i) for i in range(2))
        b_den, b_num = (gate_buffer(m32T, i) for i in range(2))

        def by_body(t):
            return t.rearrange("p (n x) -> p n x", x=CELLS)

        def by_tile(t, tile):
            b, c = tile // CH, tile % CH
            return t.rearrange("p (h b x) -> p h b x", b=B, x=CELLS)[:, :, b, c * VH:(c + 1) * VH]

        def scalars_of(what):
            return sc_all[:, :, what * CELLS:(what + 1) * CELLS]

        def gates_vector(dve):
            for t in range(TILES):
                dve.wait_ge(s_abp, 8 * (t // 8 + 1))
                src = bank[t // 8][:, 64 * (t % 8):64 * (t % 8) + 64].rearrange("p (a h v) -> p a h v", a=2, v=VH)
                dve.tensor_tensor(by_tile(a_in, t), src[:, 0], vec32[:, 0, :].rearrange("p (h v) -> p h v", v=VH),
                                  ALU.add).then_inc(s_gates, 1)
                dve.tensor_copy(by_tile(b_in, t), src[:, 1]).then_inc(s_gates, 1)
            dve.tensor_copy(al.rearrange("p (h y v) -> p h y v", y=B * CH, v=VH),
                            vec32[:, 1, :].rearrange("p (h v) -> p h v", v=VH).unsqueeze(2)
                            .broadcast_to([P, KH, B * CH, VH])).then_inc(s_gates, 1)
            dve.wait_ge(s_gates, 2 * TILES + 1)
            dve.scalar_tensor_tensor(a_abs, a_in, -1.0, a_in, op0=ALU.mult, op1=ALU.max).then_inc(s_gates, 1)
            dve.scalar_tensor_tensor(b_abs, b_in, -1.0, b_in, op0=ALU.mult, op1=ALU.max).then_inc(s_gates, 1)
            dve.wait_ge(s_gact, 3)
            dve.tensor_scalar(e_a, e_a, 1.0, None, ALU.add).then_inc(s_gates, 1)
            dve.tensor_scalar(b_den, e_b, 1.0, None, ALU.add).then_inc(s_gates, 1)
            dve.scalar_tensor_tensor(b_num, b_in, 0.0, e_b, op0=ALU.is_ge, op1=ALU.max).then_inc(s_gates, 1)
            dve.wait_ge(s_gates, 2 * TILES + 6)
            dve.reciprocal(b_den, b_den).then_inc(s_gates, 1)
            dve.wait_ge(s_gates, 2 * TILES + 7)
            dve.tensor_tensor(scalars_of(Q_BETA), by_body(b_num), by_body(b_den), ALU.mult).then_inc(s_gates, 1)
            dve.wait_ge(s_gact, 4)
            dve.scalar_tensor_tensor(ln_a, a_in, 0.0, ln_a, op0=ALU.max, op1=ALU.add).then_inc(s_gates, 1)
            dve.wait_ge(s_gates, 2 * TILES + 9)
            dve.scalar_tensor_tensor(gall, e_al, -1.0, ln_a, op0=ALU.mult, op1=ALU.mult).then_inc(s_gates, 1)
            dve.wait_ge(s_gates, GATES)
            dve.tensor_copy(scalars_of(Q_G), by_body(gall)).then_inc(s_scall, 1)
            dve.wait_ge(s_gact, 5)
            dve.tensor_scalar(scalars_of(Q_NEG_EG), scalars_of(Q_EG), -1.0, None, ALU.mult).then_inc(s_scall, 1)

        GATES = 2 * TILES + 10
        GACT = 7

        def gates_scalar(act):
            act.wait_ge(s_gates, 2 * TILES + 3)
            act.activation(e_a, a_abs, ACT.Exp, scale=-1.0).then_inc(s_gact, 1)
            act.activation(e_b, b_abs, ACT.Exp, scale=-1.0).then_inc(s_gact, 1)
            act.activation(e_al, al, ACT.Exp).then_inc(s_gact, 1)
            act.wait_ge(s_gates, 2 * TILES + 4)
            act.activation(ln_a, e_a, ACT.Ln).then_inc(s_gact, 1)
            for i, what in enumerate((Q_EG, Q_ESUF, Q_EEND)):
                act.wait_ge(s_cum, i + 1)
                act.activation(scalars_of(what), bank[2 + i][:, :].rearrange("p (n x) -> p n x", x=CELLS),
                               ACT.Exp).then_inc(s_gact, 1)

        gu_w = zone[:, :, :].rearrange("p a n -> p (a n)")[:, 0:NX * KT * 256].rearrange("p (e k n) -> p e k n", e=NX, k=KT)
        dn_w = zone[:, :, :].rearrange("p a n -> p (a n)")[:, NX * KT * 256:NX * (KT + 1) * 256].rearrange("p (e n) -> p e n", e=NX)
        rt_w = sb("rt_w", [P, KT, NE])
        rms_sb = sb("rms_sb", [P, KT])

        def wide(t, n=D):
            return t[:, :, :].rearrange("p a n -> p (a n)").rearrange("p (c n) -> p c n", n=n)

        xg = wide(gseg)
        x1 = wide(dec)
        hrow = wide(decc)
        sqx = wide(m32T)
        hT = wide(rhs, SEQ)
        sg = wide(TT, SEQ)[:, 0:2]
        aT = wide(U, SEQ)[:, 0:2]
        y = wide(qs)
        outrow = wide(og)
        bn = sb("bn", [P, CH, 6])
        mv = sb("mv", [P, CH, 2])
        st1 = sb("st1", [P, 4, CH])
        lg = sb("lg", [P, CH, NE])
        top = sb("top", [P, CH, TOPS])
        ti = sb("ti", [P, CH, TOPS], U32)
        tif = sb("tif", [P, CH, TOPS])
        tw = sb("tw", [P, 4, CH])
        pick = sb("pick", [P, 2, CH, NE])
        wd = sb("wd", [P, CH, NE])

        def moe_loads(sp):
            sp.wait_ge(s_acc, 2 * BODIES)
            sp.dma_start(gu_w, gate_up).then_inc(s_mw, 16)
            sp.dma_start(dn_w, down).then_inc(s_mw, 16)
            sp.dma_start(rt_w[:, :, :], router_w).then_inc(s_mw, 16)
            sp.dma_start(rms_sb[:, :], rms_w).then_inc(s_mw, 16)
            sp.dma_start(xg, x_rows[0:SEQ, :].rearrange("(c p) n -> p c n", p=P)).then_inc(s_xg, 16)
            for gi in range(B):
                if gi + 1 < B:
                    sp.wait_ge(s_x1, gi + 1)
                    sp.dma_start(xg, x_rows[SEQ * (gi + 1):SEQ * (gi + 2), :].rearrange("(c p) n -> p c n", p=P)).then_inc(s_xg, 16)
                sp.wait_ge(s_ln2, (gi + 1) * LN2)
                sp.dma_start(out[SEQ * gi:SEQ * (gi + 1), :].rearrange("(c p) n -> p c n", p=P), outrow).then_inc(s_out, 16)
            sp.wait_ge(s_out, 16 * B)

        def moe_pool(pool):
            pass

        LN1 = LN2 = 3 * CH + 1
        RT = 2 * CH + 10

        def moe_tensor(pe):
            pe.wait_ge(s_mw, 64)
            for g in range(B):
                for c in range(CH):
                    pe.wait_ge(s_h, g * (CH + 1) + 1 + c + 1)
                    for k in range(KT):
                        mm = pe.transpose((F0, F1)[k][:, c * P:(c + 1) * P], hrow[:, c, k * P:(k + 1) * P], ident)
                mm.then_inc(s_htp, 1)
                pe.wait_ge(s_ht, 2 * g + 2)
                if g > 0:
                    pe.wait_ge(s_rt, (g - 1) * RT + 1)
                for c in range(CH):
                    for k in range(KT):
                        mm = pe.matmul(F2[:, c * NE:(c + 1) * NE], hT[:, k, c * P:(c + 1) * P], rt_w[:, k, :],
                                       start=(k == 0), stop=(k == KT - 1))
                mm.then_inc(s_rtp, 1)

                def into(e):
                    i = g * NX + e
                    for a, dst in enumerate(((B0, B1), (B2, F0))[e % 2]):
                        if i > 1:
                            pe.wait_ge(s_a, i - 1)
                        for k in range(KT):
                            mm = pe.matmul(dst[:, :], gu_w[:, e, k, a * P:(a + 1) * P], hT[:, k, :],
                                           start=(k == 0), stop=(k == KT - 1))
                        mm.then_inc(s_gup, 1)

                def outof(e):
                    i = g * NX + e
                    pe.wait_ge(s_a, i + 1)
                    for h, dst in enumerate((B3, B4)):
                        if i > 0:
                            pe.wait_ge(s_y, (i - 1) * CH + 2 * h + 2)
                        for c in range(2):
                            mm = pe.matmul(dst[:, 256 * c:256 * c + 256], aT[:, e % 2, (2 * h + c) * P:(2 * h + c + 1) * P],
                                           dn_w[:, e, :], start=True, stop=True)
                        mm.then_inc(s_dnp, 1)

                into(0)
                for e in range(1, NX):
                    into(e)
                    outof(e - 1)
                outof(NX - 1)

        def moe_scalar(act):
            act.wait_ge(s_mw, 64)
            for g in range(B):
                act.wait_ge(s_ln1, g * LN1 + 2 * CH + 1)
                act.activation(st1[:, 1, :], st1[:, 0, :], ACT.Ln).then_inc(s_sqx, 1)
                act.wait_ge(s_sqx, g * 7 + 1)
                act.activation(st1[:, 2, :], st1[:, 1, :], ACT.Exp, scale=-0.5).then_inc(s_sqx, 1)
                act.wait_ge(s_ln1, (g + 1) * LN1)
                act.activation(sqx, x1, ACT.Square).then_inc(s_sqx, 1)
                act.wait_ge(s_h, g * (CH + 1) + 1)
                act.activation(st1[:, 1, :], st1[:, 0, :], ACT.Ln).then_inc(s_sqx, 1)
                act.wait_ge(s_sqx, g * 7 + 4)
                act.activation(st1[:, 2, :], st1[:, 1, :], ACT.Exp, scale=-0.5).then_inc(s_sqx, 1)
                act.wait_ge(s_htp, g + 1)
                for k in range(KT):
                    act.activation(hT[:, k, :], (F0, F1)[k][:, :], ACT.Copy, scale=rms_sb[:, k:k + 1]).then_inc(s_ht, 1)
                act.wait_ge(s_e2, 2 * g + 1)
                act.activation(tw[:, 1, :], tw[:, 0, :], ACT.Exp).then_inc(s_e2, 1)
                for e in range(NX):
                    i = g * NX + e
                    act.wait_ge(s_gup, 2 * i + 1)
                    if i > 1:
                        act.wait_ge(s_a, i - 1)
                    act.activation(sg[:, e % 2], (B0, B2)[e % 2][:, :], ACT.Silu).then_inc(s_sg, 1)
                act.wait_ge(s_ln2, g * LN2 + 2 * CH + 1)
                act.activation(st1[:, 1, :], st1[:, 0, :], ACT.Ln).then_inc(s_sqx, 1)
                act.wait_ge(s_sqx, g * 7 + 6)
                act.activation(st1[:, 2, :], st1[:, 1, :], ACT.Exp, scale=-0.5).then_inc(s_sqx, 1)

        def moe_vector(dve):
            dve.wait_ge(s_acc, 2 * BODIES)

            def norm_stats(src, s, base):
                for c in range(CH):
                    dve.bn_stats(bn[:, c, :], src[:, c, :]).then_inc(s, 1)
                for c in range(CH):
                    dve.wait_ge(s, base + c + 1)
                    dve.bn_aggr(mv[:, c, :], bn[:, c, :]).then_inc(s, 1)
                dve.wait_ge(s, base + 2 * CH)
                dve.tensor_scalar(st1[:, 0, :], mv[:, :, 1], 1e-5, None, ALU.add).then_inc(s, 1)

            def normalise(dst, src, s):
                for c in range(CH):
                    dve.tensor_scalar(dst[:, c, :], src[:, c, :], mv[:, c, 0:1], st1[:, 2, c:c + 1],
                                      ALU.subtract, ALU.mult).then_inc(s, 1)

            for g in range(B):
                dve.wait_ge(s_xg, 16 * (g + 1))
                if g > 0:
                    dve.wait_ge(s_ln2, g * LN2)
                dve.tensor_tensor(y, xg, acc[:, g * CH:(g + 1) * CH, :], ALU.add).then_inc(s_x1, 1)
                dve.wait_ge(s_x1, g + 1)
                norm_stats(y, s_ln1, g * LN1)
                dve.wait_ge(s_sqx, g * 7 + 2)
                normalise(x1, y, s_ln1)
                dve.wait_ge(s_sqx, g * 7 + 3)
                dve.tensor_reduce(st1[:, 3, :], sqx, AX, ALU.add).then_inc(s_x2, 1)
                dve.wait_ge(s_x2, g + 1)
                dve.tensor_scalar(st1[:, 0, :], st1[:, 3, :], 1.0 / D, 1e-6, ALU.mult, ALU.add).then_inc(s_h, 1)
                dve.wait_ge(s_sqx, g * 7 + 5)
                for c in range(CH):
                    dve.tensor_scalar(hrow[:, c, :], x1[:, c, :], st1[:, 2, c:c + 1], None, ALU.mult).then_inc(s_h, 1)
                dve.wait_ge(s_rtp, g + 1)
                r = g * RT
                dve.tensor_copy(lg[:, :, :], F2[:, 0:CH * NE].rearrange("p (c e) -> p c e", e=NE)).then_inc(s_rt, 1)
                dve.wait_ge(s_rt, r + 1)
                for c in range(CH):
                    dve.max(top[:, c, :], lg[:, c, :]).then_inc(s_rt, 1)
                for c in range(CH):
                    dve.wait_ge(s_rt, r + 2 + c)
                    dve.max_index(ti[:, c, :], top[:, c, :], lg[:, c, :]).then_inc(s_rt, 1)
                dve.tensor_tensor(tw[:, 0, :], top[:, :, 1], top[:, :, 0], ALU.subtract).then_inc(s_e2, 1)
                dve.wait_ge(s_rt, r + 1 + 2 * CH)
                dve.tensor_copy(tif[:, :, :], ti[:, :, :]).then_inc(s_rt, 1)
                dve.wait_ge(s_e2, 2 * g + 2)
                dve.tensor_scalar(tw[:, 2, :], tw[:, 1, :], 1.0, None, ALU.add).then_inc(s_rt, 1)
                dve.wait_ge(s_rt, r + 3 + 2 * CH)
                dve.reciprocal(tw[:, 2, :], tw[:, 2, :]).then_inc(s_rt, 1)
                dve.wait_ge(s_rt, r + 4 + 2 * CH)
                dve.tensor_tensor(tw[:, 3, :], tw[:, 1, :], tw[:, 2, :], ALU.mult).then_inc(s_rt, 1)
                for j in range(2):
                    dve.tensor_tensor(pick[:, j], iota_sb[:, :].unsqueeze(1).broadcast_to([P, CH, NE]),
                                      tif[:, :, j:j + 1].broadcast_to([P, CH, NE]), ALU.is_equal).then_inc(s_rt, 1)
                dve.wait_ge(s_rt, r + 7 + 2 * CH)
                for j in range(2):
                    dve.tensor_tensor(pick[:, j], pick[:, j], tw[:, 2 + j, :].unsqueeze(2).broadcast_to([P, CH, NE]),
                                      ALU.mult).then_inc(s_rt, 1)
                dve.wait_ge(s_rt, r + 9 + 2 * CH)
                dve.tensor_tensor(wd[:, :, :], pick[:, 0], pick[:, 1], ALU.add).then_inc(s_rt, 1)
                dve.wait_ge(s_rt, r + 10 + 2 * CH)

                def gated(e):
                    i = g * NX + e
                    dve.wait_ge(s_sg, i + 1)
                    dve.wait_ge(s_gup, 2 * i + 2)
                    if i > 1:
                        dve.wait_ge(s_dnp, 2 * (i - 1))
                    dve.tensor_tensor(aT[:, e % 2], sg[:, e % 2], (B1, F0)[e % 2][:, :], ALU.mult).then_inc(s_a, 1)

                def added(e):
                    i = g * NX + e
                    for c in range(CH):
                        dve.wait_ge(s_dnp, 2 * i + c // 2 + 1)
                        if e > 0:
                            dve.wait_ge(s_y, (i - 1) * CH + c + 1)
                        src = (B3, B4)[c // 2][:, 256 * (c % 2):256 * (c % 2) + 256]
                        dve.scalar_tensor_tensor(y[:, c, :], src, wd[:, c, e:e + 1] if e < NE else 1.0,
                                                 (y if e else x1)[:, c, :], op0=ALU.mult, op1=ALU.add).then_inc(s_y, 1)

                gated(0)
                for e in range(1, NX):
                    gated(e)
                    added(e - 1)
                added(NX - 1)
                dve.wait_ge(s_y, (g + 1) * NX * CH)
                norm_stats(y, s_ln2, g * LN2)
                dve.wait_ge(s_sqx, g * 7 + 7)
                if g > 0:
                    dve.wait_ge(s_out, 16 * g)
                normalise(outrow, y, s_ln2)

        block = ctx.enter_context(nc.Block())

        @block.sync
        def _(sp):
            sp.dma_start(w_kh[:, :, :], w_heads[0].rearrange("p (t n) -> p t n", t=KT)).then_inc(s_w, 16)
            for dst, src in (
                (xT[:, :, :], x_cols.rearrange("(t p) n -> p t n", p=P)),
                (tri_sb[:, :, :], tri), (wab[:, :, :], w_ab.rearrange("(t p) n -> p t n", p=P)),
                (vec32[:, 0, :], dt_bias), (vec32[:, 1, :], a_log),
                (negm[:, :], neg_mask[:, 0:512]), (identb[:, :], neg_mask[:, 512:640]),
                (lev[:, :, :], levels16), (identh[:, :], ident16), (iota_sb[:, :], iota8),
                (gam[:, :], gamma), (cw_all[:, :, :], conv_w),
            ):
                sp.dma_start(dst, src).then_inc(s_const, 16)
            sp.dma_start(wo_raw[:, :, :], w_out[0]).then_inc(s_wo, 16)

            def weights(kh):
                sp.wait_ge(s_zp, (kh * B + B) * 2)
                sp.dma_start(w_kh[:, :, :], w_heads[bass.ds(kh + 1, 1)].rearrange("o p (t n) -> (o p) t n", t=KT)).then_inc(s_w, 16)
                sp.wait_ge(s_wog, kh + 1)
                sp.dma_start(wo_raw[:, :, :], w_out[bass.ds(kh + 1, 1)].rearrange("o p v n -> (o p) v n")).then_inc(s_wo, 16)

            sp.wait_ge(s_const, CONSTS)
            with sp.Fori(0, KH - 1) as kh:
                weights(kh)
            moe_loads(sp)

        @block.gpsimd
        def _(pool):
            pool.memset(acc[:, :, :], 0.0).then_inc(s_zero, 1)
            pool.wait_ge(s_const, CONSTS)

            def scale_wo(kh):
                pool.wait_ge(s_wo, 16 * (kh + 1))
                pool.tensor_tensor(wo[:, :, :], wo_raw[:, :, :], gam[:, 0:1].unsqueeze(2).broadcast_to([P, VH, D]), ALU.mult).then_inc(s_wog, 1)

            def run(step, n, b, head):
                p = b % 2
                if step == ("scalars", 0):
                    pool.wait_ge(s_sc, n * 2 + 2)
                    if past_first(n):
                        pool.wait_ge(s_decp, n * 2)
                    pool.tensor_tensor(gseg[:, :, :], after.unsqueeze(1).broadcast_to([P, CELLS, P]),
                                       scal(p, Q_G, 0, CELLS).unsqueeze(2).broadcast_to([P, CELLS, P]),
                                       ALU.mult).then_inc(s_seg, 1)
                elif step == ("norms", 0):
                    pool.wait_ge(s_rqk, n * 2 + 1)
                    if past_first(n):
                        pool.wait_ge(s_keys, n)
                    pool.tensor_tensor(rk2[:, :], rqk[:, CH:], rqk[:, CH:], ALU.mult).then_inc(s_small, 1)
                    pool.tensor_scalar(rqs[:, :], rqk[:, 0:CH], SCALE, None, ALU.mult).then_inc(s_small, 1)
                    pool.wait_ge(s_small, n * 4 + 2)
                    pool.tensor_tensor(cj[:, :].rearrange("p (c v) -> p c v", v=VH),
                                       scal(p, Q_BETA, 0, CELLS).rearrange("p (c v) -> p c v", v=VH),
                                       rk2[:, :].unsqueeze(2).broadcast_to([P, CH, VH]), ALU.mult).then_inc(s_small, 1)
                    pool.wait_ge(s_small, n * 4 + 3)
                    pool.tensor_tensor(kfac[:, :], cj[:, :], scal(p, Q_ESUF, 0, CELLS), ALU.mult).then_inc(s_small, 1)
                    pool.wait_ge(s_zs, n * 2 + 2)
                    pool.tensor_tensor(zs[:, p, :, :], zs[:, p, :, :],
                                       rqs[:, :].unsqueeze(2).broadcast_to([P, CH, VH * P]), ALU.mult).then_inc(s_zq, 1)
                elif step[0] == "decay":
                    h = step[1]
                    pool.wait_ge(s_dec, n * 2 + h + 1)
                    if past_first(n):
                        pool.wait_ge(s_p, n * 2)
                    pool.tensor_tensor(half(decc, h), half(dec, h),
                                       cj[:, 4 * h:4 * h + 4].unsqueeze(2).broadcast_to([P, 4, P]), ALU.mult).then_inc(s_decc, 1)
                elif step == ("system", 0):
                    for h in range(2):
                        pool.wait_ge(s_const, CONSTS)
                        pool.wait_ge(s_m, n * 2 + h + 1)
                        pool.affine_select(out=half(m32T, h), in_=half(m32T, h), compare_op=ALU.not_equal, fill=1.0,
                                           base=0, pattern=[[0, 4], [-1, P]], channel_multiplier=1).then_inc(s_fill, 1)
                    pool.wait_ge(s_mhi, n + 1)
                    pool.tensor_tensor(mloT[:, p], m32T[:, :, :], mhiT[:, p], ALU.subtract).then_inc(s_mlo, 1)
                elif step == ("gated", 0):
                    for h in range(2):
                        pool.wait_ge(s_msl, n * 2 + 2)
                        pool.tensor_tensor(half(og, h), half(og, h),
                                           ms[:, 2, 4 * h:4 * h + 4].unsqueeze(2).broadcast_to([P, 4, P]),
                                           ALU.mult).then_inc(s_on, 1)

            for step in FRONT:
                run(step, 0, 0, 0)

            def key_head(kh, last):
                for step, n, b, head in body_steps(kh, last):
                    run(step, n, b, head)
                    if step == ("project", 0) and b == B - 1 and not last:
                        pool.wait_ge(s_opp, (kh * B + B) * 2)
                        scale_wo(kh + 1)

            scale_wo(0)
            with pool.Fori(0, KH - 1) as kh:
                key_head(kh, False)
            key_head(KH - 1, True)
            moe_pool(pool)

        @block.tensor
        def _(pe):
            pe.wait_ge(s_const, CONSTS)
            for t in range(TILES):
                for k in range(KT):
                    mm = pe.matmul(bank[t // 8][:, 64 * (t % 8):64 * (t % 8) + 64], xT[:, k, t * P:(t + 1) * P],
                                   wab[:, k, :], start=(k == 0), stop=(k == KT - 1))
                mm.then_inc(s_abp, 1)
            pe.wait_ge(s_gates, GATES)
            for i, m in enumerate((upto, after, ones)):
                pe.matmul(bank[2 + i][:, :], m, gall, start=True, stop=True).then_inc(s_cum, 1)
            pe.wait_ge(s_gact, GACT)

            def run(step, n, b, head):
                p = b % 2
                later = past_first(n)
                name, i = step
                if name == "proj":
                    dst = (F0, F1, F2, F0)[i]
                    if i == 0:
                        if b % B == 0:
                            pe.wait_ge(s_w, 16 * (head + 1))
                        if later:
                            pe.wait_ge(s_dec, n * 2)
                    if later and i == 1:
                        pe.wait_ge(s_x0, n)
                    if later and i == 2:
                        pe.wait_ge(s_p, n * 2)
                    if i == 3:
                        pe.wait_ge(s_conv, n * 12 + 3)
                        pe.wait_ge(s_tap, n * 4 + 1)
                    for k in range(KT):
                        mm = pe.matmul(dst[:, :], w_kh[:, k, i * P:(i + 1) * P], xT[:, k, bass.ts(b % B, SEQ)],
                                       start=(k == 0), stop=(k == KT - 1))
                    mm.then_inc(s_proj, 1)
                elif name == "gate":
                    dst = (F1, F2)[i]
                    pe.wait_ge(s_conv, n * 12 + 6 + 3 * i)
                    for c in range(2):
                        t = (b % B) * CH + 2 * i + c
                        for k in range(KT):
                            mm = pe.matmul(dst[:, 256 * c:256 * c + 256], xT[:, k, t * P:(t + 1) * P], w_kh[:, k, 512:768],
                                           start=(k == 0), stop=(k == KT - 1))
                    mm.then_inc(s_zp, 1)
                elif name == "norms":
                    pe.wait_ge(s_sq, n + 1)
                    pe.wait_ge(s_conv, n * 12 + 12)
                    for c in range(2 * CH):
                        mm = pe.matmul(F0[:, c:c + 1], sq[:, c * P:(c + 1) * P], ones[:, 0:1], start=True, stop=True)
                    mm.then_inc(s_ssp, 1)
                elif name == "keys":
                    pe.wait_ge(s_zs, n * 2 + 1)
                    for c in range(CH):
                        mm = pe.transpose(F1[:, c * P:(c + 1) * P], qkT[:, p, 1, c * P:(c + 1) * P], ident)
                    mm.then_inc(s_ktp, 1)
                elif name == "values":
                    if i == 0:
                        pe.wait_ge(s_silu, n * 4 + 4)
                        pe.wait_ge(s_zs, n * 2 + 2)
                    else:
                        pe.wait_ge(s_ss, n + 1)
                    for c in range(2):
                        for v in range(VH):
                            o = (c * VH + v) * P
                            t = (2 * i + c) * P
                            mm = pe.transpose((F2, F0)[i][:, o:o + P], vT[:, v, t:t + P], ident)
                    mm.then_inc(s_vtp, 1)
                elif name == "products":
                    for a, dst, free in ((1, F1, (s_keys, 1, 1)), (0, F2, (s_vals, 2, 1))):
                        pe.wait_ge(free[0], n * free[1] + free[2])
                        for c in range(CH):
                            mm = pe.matmul(dst[:, c * P:(c + 1) * P], qkT[:, p, 1, c * P:(c + 1) * P],
                                           qkT[:, p, a, c * P:(c + 1) * P], start=True, stop=True)
                        mm.then_inc(s_kq, 1)
                elif name == "decay":
                    if i == 0:
                        pe.wait_ge(s_seg, n + 1)
                        pe.wait_ge(s_vals, n * 2 + 2)
                    else:
                        pe.wait_ge(s_dec, n * 2 + 1)
                    pe.matmul(F0[:, :], identb[:, :], negm[:, :], start=True, stop=False, skip_group_check=True)
                    for x in range(4):
                        mm = pe.matmul(F0[:, x * P:(x + 1) * P], gseg[:, 4 * i + x, :], upto, start=False,
                                       stop=(x == 3), skip_group_check=True)
                    mm.then_inc(s_decp, 1)
                elif name == "start":
                    pe.wait_ge(s_pair, n + 1)
                    pe.wait_ge(s_m, n * 2 + 2)
                    f1h = F1[:, :].bitcast(F16)
                    for x in range(CELLS):
                        mm = pe.transpose(f1h[:, x * P:(x + 1) * P], XT[:, 0, x, :], identh[:, :])
                    mm.then_inc(s_xp, 1)
                elif name == "level":
                    old, base = i % 2, n * 12 + 2 * i
                    for h, dst in ((0, B0), (1, B1)):
                        if i == 0:
                            if h == 0:
                                pe.wait_ge(s_x0, n + 1)
                        else:
                            pe.wait_ge(s_xy, n * 24 + 4 * (i - 1) + 2 * h + 1)
                        for x in range(4):
                            mm = pe.matmul(dst[:, x * P:(x + 1) * P], mhiT[:, p, 4 * h + x, :], X[:, old, 4 * h + x, :],
                                           start=True, stop=True)
                        mm.then_inc(s_np, 1)
                    for h in range(2):
                        pe.wait_ge(s_n, base + h + 1)
                        if i > 0:
                            pe.wait_ge(s_xy, n * 24 + 4 * (i - 1) + 2 * h + 2 + (2 if h == 0 else 0))
                        for j, dst in enumerate(((B2, B3), (B4, B2))[h]):
                            if h == 1 and j == 1:
                                pe.wait_ge(s_xy, n * 24 + 4 * i + 1)
                            for x in range(4):
                                c = 4 * h + x
                                if j == 0:
                                    mm = pe.matmul(dst[:, x * P:(x + 1) * P], XT[:, old, c, :], N[:, c, :], start=True, stop=True)
                                else:
                                    mm = pe.matmul(dst[:, x * P:(x + 1) * P], N[:, c, :], XT[:, old, c, :], start=True, stop=True)
                            mm.then_inc(s_xyp, 1)
                elif name == "newton":
                    for h, dst in ((0, B0), (1, B1)):
                        pe.wait_ge(s_xy, n * 24 + 20 + 2 * h + 1)
                        if h == 0:
                            pe.wait_ge(s_mlo, n + 1)
                        for x in range(4):
                            c = 4 * h + x
                            pe.matmul(dst[:, x * P:(x + 1) * P], mhiT[:, p, c, :], X[:, 0, c, :], start=True, stop=False)
                            mm = pe.matmul(dst[:, x * P:(x + 1) * P], mloT[:, p, c, :], X[:, 0, c, :], start=False, stop=True)
                        mm.then_inc(s_resp, 1)
                    for h, dst in ((0, B3), (1, B4)):
                        pe.wait_ge(s_res, n * 2 + h + 1)
                        pe.wait_ge(s_xy, n * 24 + 20 + 2 * h + 2)
                        for x in range(4):
                            c = 4 * h + x
                            mm = pe.matmul(dst[:, x * P:(x + 1) * P], N[:, c, :], XT[:, 0, c, :], start=True, stop=True)
                        mm.then_inc(s_newp, 1)
                elif name == "chain":
                    c = i
                    qT, kT = (qkT[:, p, a, c * P:(c + 1) * P] for a in range(2))
                    if c > 0:
                        pe.wait_ge(s_st, n * 6 + 2 * c)
                        pe.matmul(B0[:, 0:256], kT, S[:, c, :], start=True, stop=True).then_inc(s_ksp, 1)
                        if c == 1:
                            pe.wait_ge(s_new, n * 2 + 2)
                        mm = pe.matmul((B3, B3, B4, B4)[c][:, 256 * (c % 2):256 * (c % 2) + 256], qT, S[:, c, :],
                                       start=True, stop=True)
                        if c in (1, 3):
                            mm.then_inc(s_qsp, 1)
                    if c == 0:
                        pe.wait_ge(s_new, n * 2 + 1)
                        pe.wait_ge(s_vals, n * 2 + 1)
                    elif c == 2:
                        pe.wait_ge(s_new, n * 2 + 2)
                    for v in range(VH):
                        x = c * VH + v
                        if c > 0:
                            pe.wait_ge(s_r, n * 6 + 2 * c - 2 + v + 1)
                        mm = pe.matmul(B1[:, v * P:(v + 1) * P], TT[:, x, :], rhs[:, x, :] if c else vals[:, p, x, :],
                                       start=True, stop=True)
                    mm.then_inc(s_up, 1)
                    pe.wait_ge(s_u, n * 4 + c + 1)
                    if c < CH - 1:
                        if c == 0:
                            pe.wait_ge(s_xy, n * 24 + 24)
                            pe.wait_ge(s_keys, n + 1)
                        for v in range(VH):
                            x = c * VH + v
                            mm = pe.matmul(B2[:, v * P:(v + 1) * P], keys[:, p, x, :], U[:, x, :], start=True, stop=True)
                        mm.then_inc(s_stp, 1)
                elif name == "out":
                    pe.wait_ge(s_p, n * 2 + 2)
                    for h, dst in ((0, B0), (1, B1)):
                        for x in range(4):
                            c = 4 * h + x
                            mm = pe.matmul(dst[:, x * P:(x + 1) * P], pT[:, p, c, :], U[:, c, :], start=True, stop=True)
                        mm.then_inc(s_pup, 1)
                elif name == "project":
                    for h, dst in ((0, B2), (1, B3)):
                        pe.wait_ge(s_on, n * 2 + h + 1)
                        if h == 0:
                            pe.wait_ge(s_st, n * 6 + 6)
                        for x in range(4):
                            mm = pe.transpose(dst[:, x * P:(x + 1) * P], og[:, 4 * h + x, :], ident)
                        mm.then_inc(s_gtp, 1)
                    if b == 0:
                        pe.wait_ge(s_wog, head + 1)
                    for h, dst in ((0, B4), (1, B0)):
                        pe.wait_ge(s_gt, n * 2 + h + 1)
                        for c in range(2):
                            for v in range(VH):
                                mm = pe.matmul(dst[:, 256 * c:256 * c + 256], ogT[:, 4 * h + 2 * c + v, :], wo[:, v, :],
                                               start=(v == 0), stop=(v == VH - 1))
                        mm.then_inc(s_opp, 1)
                    pe.wait_ge(s_acc, n * 2 + 2)

            for step in FRONT:
                run(step, 0, 0, 0)
            with pe.Fori(0, KH - 1) as kh:
                for step, n, b, head in body_steps(kh, False):
                    run(step, n, b, head)
            for step, n, b, head in body_steps(KH - 1, True):
                run(step, n, b, head)
            moe_tensor(pe)

        @block.scalar
        def _(act):
            act.wait_ge(s_const, CONSTS)
            gates_scalar(act)

            def run(step, n, b, head):
                p = b % 2
                later = past_first(n)
                name, i = step
                if name == "proj":
                    if i == 0:
                        act.wait_ge(s_sc, n * 2 + 1)
                    act.wait_ge(s_proj, n * 4 + i + 1)
                    act.activation(conv[:, i, :], (F0, F1, F2, F0)[i][:, :], ACT.Copy,
                                   scale=cw[:, p, i * TAPS + 3:i * TAPS + 4]).then_inc(s_tap, 1)
                elif name == "gate":
                    for g in (2 * i, 2 * i + 1):
                        act.wait_ge(s_conv, n * 12 + 3 * g + 3)
                        dst = qkT[:, p, g, :] if g < 2 else vT[:, g - 2, :]
                        act.activation(dst, conv[:, g, :], ACT.Silu).then_inc(s_silu, 1)
                    act.wait_ge(s_zp, n * 2 + i + 1)
                    act.activation(zs[:, p, 2 * i:2 * i + 2, :], (F1, F2)[i][:, :].rearrange("p (c n) -> p c n", c=2),
                                   ACT.Silu).then_inc(s_zs, 1)
                    if i == 0:
                        act.wait_ge(s_silu, n * 4 + 2)
                        act.activation(sq[:, :], qkT[:, p, :, :].rearrange("p a n -> p (a n)"), ACT.Square).then_inc(s_sq, 1)
                elif name == "norms":
                    act.wait_ge(s_ss, n + 1)
                    act.activation(lnss[:, :], ss[:, :], ACT.Ln).then_inc(s_ln, 1)
                    act.wait_ge(s_ln, n + 1)
                    act.activation(rqk[:, :], lnss[:, :], ACT.Exp, scale=-0.5).then_inc(s_rqk, 1)
                    act.activation(nk[:, :], lnss[:, CH:], ACT.Exp, scale=0.5).then_inc(s_rqk, 1)
                elif name == "decay":
                    act.wait_ge(s_decp, n * 2 + i + 1)
                    act.activation(half(dec, i), bank4(F0), ACT.Exp).then_inc(s_dec, 1)
                elif name == "system":
                    act.wait_ge(s_fill, n * 2 + 2)
                    act.activation(mhiT[:, p], m32T[:, :, :], ACT.Copy).then_inc(s_mhi, 1)
                elif name == "start":
                    act.wait_ge(s_xp, n + 1)
                    act.activation(X[:, 0], F1[:, :].bitcast(F16).rearrange("p (x n) -> p x n", x=CELLS), ACT.Copy).then_inc(s_x0, 1)
                elif name == "level":
                    new = (i + 1) % 2
                    for h in range(2):
                        for j, (dst, src) in enumerate(((X, (B2, B4)[h]), (XT, (B3, B2)[h]))):
                            act.wait_ge(s_xyp, n * 24 + 4 * i + 2 * h + j + 1)
                            act.activation(half(dst[:, new], h), bank4(src), ACT.Copy).then_inc(s_xy, 1)
                elif name == "chain":
                    act.wait_ge(s_up, n * 4 + i + 1)
                    act.activation(U[:, 2 * i:2 * i + 2, :], B1[:, 0:256].rearrange("p (v n) -> p v n", v=VH),
                                   ACT.Copy).then_inc(s_u, 1)
                elif name == "gated":
                    for h in range(2):
                        act.wait_ge(s_og, n * 2 + h + 1)
                        act.activation(half(og2, h), half(og, h), ACT.Square).then_inc(s_og2, 1)
                    act.wait_ge(s_ms, n * 3 + 3)
                    act.activation(ms[:, 1, :], ms[:, 1, :], ACT.Ln).then_inc(s_msl, 1)
                    act.wait_ge(s_msl, n * 2 + 1)
                    act.activation(ms[:, 2, :], ms[:, 1, :], ACT.Exp, scale=-0.5).then_inc(s_msl, 1)
                elif name == "project":
                    for h in range(2):
                        act.wait_ge(s_gtp, n * 2 + h + 1)
                        act.activation(half(ogT, h), bank4((B2, B3)[h]), ACT.Copy).then_inc(s_gt, 1)

            for step in FRONT:
                run(step, 0, 0, 0)
            with act.Fori(0, KH - 1) as kh:
                for step, n, b, head in body_steps(kh, False):
                    run(step, n, b, head)
            for step, n, b, head in body_steps(KH - 1, True):
                run(step, n, b, head)
            moe_scalar(act)

        @block.vector
        def _(dve):
            dve.wait_ge(s_const, CONSTS)
            gates_vector(dve)

            def run(step, n, b, head):
                p = b % 2
                later = past_first(n)
                name, i = step
                if name == "scalars":
                    if later:
                        dve.wait_ge(s_tap, (n - 1) * GROUPS)
                        dve.wait_ge(s_seg, n)
                    else:
                        dve.wait_ge(s_scall, 2)
                        dve.wait_ge(s_gact, GACT)
                    dve.tensor_scalar(cw[:, p, :], cw_all[:, bass.ds(head, 1), :].rearrange("p o n -> p (o n)"),
                                      1.0, None, ALU.mult).then_inc(s_sc, 1)
                    dve.tensor_scalar(sc[:, p, :], sc_all[:, bass.ds(n, 1), :].rearrange("p o n -> p (o n)"),
                                      1.0, None, ALU.mult).then_inc(s_sc, 1)
                elif name == "proj":
                    src = (F0, F1, F2, F0)[i]
                    for j in (1, 2, 3):
                        dve.wait_ge(s_tap, n * 4 + i + 1) if j == 1 else dve.wait_ge(s_conv, n * 12 + 3 * i + j - 1)
                        dve.scalar_tensor_tensor(conv[:, i, j:], src[:, 0:SEQ - j], cw[:, p, i * TAPS + 3 - j:i * TAPS + 4 - j],
                                                 conv[:, i, j:], op0=ALU.mult, op1=ALU.add).then_inc(s_conv, 1)
                elif name == "norms":
                    dve.wait_ge(s_ssp, n + 1)
                    dve.tensor_scalar(ss[:, :], F0[:, 0:2 * CH], 1e-6, None, ALU.add).then_inc(s_ss, 1)
                elif name == "keys":
                    dve.wait_ge(s_ktp, n + 1)
                    dve.wait_ge(s_small, n * 4 + 4)
                    dve.tensor_tensor(keys[:, p].rearrange("p (c v) n -> p c v n", v=VH),
                                      F1[:, :].rearrange("p (c n) -> p c n", c=CH).unsqueeze(2).broadcast_to([P, CH, VH, P]),
                                      kfac[:, :].rearrange("p (c v) -> p c v", v=VH).unsqueeze(3).broadcast_to([P, CH, VH, P]),
                                      ALU.mult).then_inc(s_keys, 1)
                elif name == "values":
                    dve.wait_ge(s_vtp, n * 2 + i + 1)
                    dve.wait_ge(s_rqk, n * 2 + 2)
                    dve.tensor_tensor(half(vals[:, p], i).rearrange("p (c v) n -> p c (v n)", v=VH),
                                      (F2, F0)[i][:, :].rearrange("p (c n) -> p c n", c=2),
                                      nk[:, 2 * i:2 * i + 2].unsqueeze(2).broadcast_to([P, 2, VH * P]),
                                      ALU.mult).then_inc(s_vals, 1)
                elif name == "system":
                    for h in range(2):
                        dve.wait_ge(s_decc, n * 2 + h + 1)
                        dve.wait_ge(s_kq, n * 2 + 1)
                        if h == 0 and later:
                            dve.wait_ge(s_mlo, n)
                        for dst, src, done in ((m32T[:, :, :], F1, s_m), (pT[:, p], F2, s_p)):
                            if done is s_p:
                                dve.wait_ge(s_kq, n * 2 + 2)
                            dve.tensor_tensor(half(dst, h).rearrange("p (c v) n -> p c v n", v=VH),
                                              src[:, :].rearrange("p (c n) -> p c n", c=CH)[:, 2 * h:2 * h + 2]
                                              .unsqueeze(2).broadcast_to([P, 2, VH, P]),
                                              half(decc, h).rearrange("p (c v) n -> p c v n", v=VH),
                                              ALU.mult).then_inc(done, 1)
                    dve.wait_ge(s_mhi, n + 1)
                    dve.tensor_tensor(XT[:, 0], mhiT[:, p], lev[:, 0, :].unsqueeze(1).broadcast_to([P, CELLS, P]),
                                      ALU.mult).then_inc(s_pair, 1)
                elif name == "level":
                    for h in range(2):
                        dve.wait_ge(s_np, n * 12 + 2 * i + h + 1)
                        if i > 0:
                            dve.wait_ge(s_xyp, n * 24 + 4 * (i - 1) + 2 * h + 2)
                        dve.tensor_tensor(half(N, h), bank4((B0, B1)[h]),
                                          lev[:, 1 + i, :].unsqueeze(1).broadcast_to([P, 4, P]), ALU.mult).then_inc(s_n, 1)
                elif name == "newton":
                    for h in range(2):
                        dve.wait_ge(s_resp, n * 2 + h + 1)
                        dve.tensor_tensor(half(N, h), ident.unsqueeze(1).broadcast_to([P, 4, P]), bank4((B0, B1)[h]),
                                          ALU.subtract).then_inc(s_res, 1)
                    for h in range(2):
                        dve.wait_ge(s_newp, n * 2 + h + 1)
                        dve.tensor_tensor(half(TT, h), bank4((B3, B4)[h]), half(XT[:, 0], h), ALU.add).then_inc(s_new, 1)
                elif name == "chain":
                    c = i
                    if c == 0:
                        dve.wait_ge(s_sc, n * 2 + 2)
                    if c > 0:
                        dve.wait_ge(s_ksp, n * 3 + c)
                        for v in range(VH):
                            x = c * VH + v
                            dve.scalar_tensor_tensor(rhs[:, x, :], B0[:, v * P:(v + 1) * P], scal(p, Q_NEG_EG, x),
                                                     vals[:, p, x, :], op0=ALU.mult, op1=ALU.add).then_inc(s_r, 1)
                    if c < CH - 1:
                        dve.wait_ge(s_stp, n * 3 + c + 1)
                        for v in range(VH):
                            x = c * VH + v
                            new, got = S[:, c + 1, v * P:(v + 1) * P], B2[:, v * P:(v + 1) * P]
                            if c == 0:
                                dve.tensor_copy(new, got).then_inc(s_st, 1)
                            else:
                                dve.scalar_tensor_tensor(new, S[:, c, v * P:(v + 1) * P], scal(p, Q_EEND, x), got,
                                                         op0=ALU.mult, op1=ALU.add).then_inc(s_st, 1)
                elif name == "out":
                    for h in range(2):
                        dve.wait_ge(s_qsp, n * 2 + h + 1)
                        a = 2 if h == 0 else 0
                        dve.tensor_tensor(qs[:, 4 * h + a:4 * h + 4, :], bank4((B3, B4)[h])[:, a:4],
                                          scal(p, Q_EG, 4 * h + a, 4 - a).unsqueeze(2).broadcast_to([P, 4 - a, P]),
                                          ALU.mult).then_inc(s_qs, 1)
                elif name == "gated":
                    for h in range(2):
                        dve.wait_ge(s_pup, n * 2 + h + 1)
                        dve.wait_ge(s_qs, n * 2 + h + 1)
                        src = bank4((B0, B1)[h])
                        if h == 0:
                            dve.wait_ge(s_zq, n + 1)
                            dve.tensor_tensor(og[:, 0:2, :], src[:, 0:2], zs[:, p, 0, :].rearrange("p (v n) -> p v n", v=VH),
                                              ALU.mult).then_inc(s_o, 1)
                            dve.tensor_tensor(qs[:, 2:4, :], src[:, 2:4], qs[:, 2:4, :], ALU.add).then_inc(s_o, 1)
                            dve.wait_ge(s_o, n * 3 + 2)
                            dve.tensor_tensor(og[:, 2:4, :], qs[:, 2:4, :], zs[:, p, 1, :].rearrange("p (v n) -> p v n", v=VH),
                                              ALU.mult).then_inc(s_og, 1)
                        else:
                            dve.tensor_tensor(qs[:, 4:8, :], src, qs[:, 4:8, :], ALU.add).then_inc(s_o, 1)
                            dve.wait_ge(s_o, n * 3 + 3)
                            dve.tensor_tensor(og[:, 4:8, :], qs[:, 4:8, :],
                                              zs[:, p, 2:4, :].rearrange("p c (v n) -> p (c v) n", v=VH),
                                              ALU.mult).then_inc(s_og, 1)
                    for h in range(2):
                        dve.wait_ge(s_og2, n * 2 + h + 1)
                        dve.tensor_reduce(ms[:, 0, 4 * h:4 * h + 4], half(og2, h), AX, ALU.add).then_inc(s_ms, 1)
                    dve.wait_ge(s_ms, n * 3 + 2)
                    dve.tensor_scalar(ms[:, 1, :], ms[:, 0, :], 1.0 / P, 1e-6, ALU.mult, ALU.add).then_inc(s_ms, 1)
                elif name == "project":
                    for h in range(2):
                        dve.wait_ge(s_opp, n * 2 + h + 1)
                        a = acc[:, b * CH + 2 * h:b * CH + 2 * h + 2, :]
                        dve.tensor_tensor(a, (B4, B0)[h][:, :].rearrange("p (c n) -> p c n", c=2), a,
                                          ALU.add).then_inc(s_acc, 1)

            dve.wait_ge(s_zero, 1)
            for step in FRONT:
                run(step, 0, 0, 0)
            with dve.Fori(0, KH - 1) as kh:
                for step, n, b, head in body_steps(kh, False):
                    run(step, n, b, head)
            for step, n, b, head in body_steps(KH - 1, True):
                run(step, n, b, head)
            moe_vector(dve)


def kernel(**inputs):
    import ml_dtypes
    import numpy as np
    import concourse.bacc as bacc
    from concourse.bass_utils import run_bass_kernel_spmd

    def arr(name):
        return np.asarray(inputs["L0_" + name])

    x = arr("attn_hidden_states").reshape(TILES * P, D)
    w_qkv, w_z = arr("attn_w_qkv"), arr("attn_w_z")
    kdim = KH * P
    q, k = (w_qkv[:, i * kdim:(i + 1) * kdim].reshape(KT, P, KH, P) for i in range(2))
    v, z = (w.reshape(KT, P, KH, VH * P) for w in (w_qkv[:, 2 * kdim:], w_z))
    heads = np.concatenate([q, k, v, z], axis=3).transpose(2, 1, 0, 3).reshape(KH, P, -1)
    cw = arr("attn_conv_w")
    cq, ck = (cw[i * kdim:(i + 1) * kdim].reshape(KH, 1, P, TAPS) for i in range(2))
    cv = cw[2 * kdim:].reshape(KH, VH, P, TAPS)
    conv_w = np.concatenate([cq, ck, cv], axis=1).transpose(2, 0, 1, 3).reshape(P, KH, GROUPS * TAPS)
    i, j = np.arange(P)[:, None], np.arange(P)[None, :]
    eye = np.eye(P, dtype=np.float32)
    levels = [eye - ((j == i + 1) & (i % 2 == 0))]
    levels += [eye - ((i // (2 * s) == j // (2 * s)) & (i // s == j // s + 1)) for s in LEVELS]
    late = np.where(j < i, -30000.0, 0.0)
    gate, up = (np.concatenate([arr("ffn_w_" + n), arr("ffn_sw_" + n)[None]]) for n in ("gate", "up"))
    down = np.concatenate([arr("ffn_w_down"), arr("ffn_sw_down")[None]])
    arrays = {
        "x_rows": x,
        "x_cols": x.T,
        "w_heads": heads,
        "w_ab": np.concatenate([arr("attn_w_a"), arr("attn_w_b")], axis=1),
        "conv_w": conv_w,
        "dt_bias": np.broadcast_to(arr("attn_dt_bias"), (P, KH * VH)),
        "a_log": np.broadcast_to(arr("attn_A_log"), (P, KH * VH)),
        "gamma": arr("attn_norm_gamma").reshape(P, 1),
        "w_out": arr("attn_w_out").reshape(KH, VH, P, D).transpose(0, 2, 1, 3),
        "rms_w": arr("ffn_rms_weight").reshape(KT, P).T,
        "router_w": arr("ffn_router_w").reshape(KT, P, NE).transpose(1, 0, 2),
        "gate_up": np.concatenate([gate, up], axis=2).reshape(NX, KT, P, 2 * P).transpose(2, 0, 1, 3),
        "down": down.transpose(1, 0, 2),
        "tri": np.stack([i <= j, i > j, i == j, i == i + 0 * j], axis=1).astype(np.float32),
        "levels16": np.stack(levels, axis=1).astype(np.float16),
        "neg_mask": np.concatenate([late] * 4 + [eye], axis=1).astype(ml_dtypes.bfloat16),
        "ident16": eye.astype(np.float16),
        "iota8": np.broadcast_to(np.arange(NE, dtype=np.float32), (P, NE)),
    }
    nc = bacc.Bacc("TRN2", target_bir_lowering=False, num_devices=1)
    args, data = [], {}
    for name, a in arrays.items():
        data[name] = np.ascontiguousarray(a)
        args.append(nc.dram_tensor(name, a.shape, mybir.dt.from_np(a.dtype), kind="ExternalInput").ap())
    args.append(nc.dram_tensor("out", (TILES * P, D), F32, kind="ExternalOutput").ap())
    build_kernel(nc, *args)
    r = run_bass_kernel_spmd(nc, [data], core_ids=[0])
    return r.results[0]["out"].reshape(B, SEQ, D)
```

```python
from contextlib import ExitStack

import concourse.bass as bass
from concourse import mybir

F32 = mybir.dt.float32
F16 = mybir.dt.float16
BF16 = mybir.dt.bfloat16
U32 = mybir.dt.uint32
ALU = mybir.AluOpType
ACT = mybir.ActivationFunctionType
AX = mybir.AxisListType.X

P = 128
B, SEQ, D = 4, 512, 256
CH = SEQ // P
KT = D // P
KH, VH = 16, 2
TILES = B * CH
CELLS = CH * VH
BODIES = KH * B
TAPS = 4
GROUPS = 4
SCALE = float(P) ** -0.5
LEVELS = [2, 4, 8, 16, 32, 64]
NE, TOPS = 8, 8
NX = NE + 1
NQ = 6
Q_G, Q_BETA, Q_EG, Q_ESUF, Q_EEND, Q_NEG_EG = range(NQ)

SCHEDULE = [
    ("F", "scalars", 0), ("F", "proj", 0), ("F", "proj", 1),
    ("solve", 0), ("F", "conv", 0), ("F", "proj", 2),
    ("write", 0), ("F", "conv", 1), ("F", "proj", 3),
    ("read", 1), ("F", "conv", 2), ("F", "decay", 0),
    ("solve", 1), ("F", "conv", 3), ("F", "decay", 1),
    ("write", 1), ("F", "conv", 4), ("F", "proj", 4),
    ("read", 2), ("F", "conv", 5), ("F", "silu", 0), ("F", "proj", 5),
    ("solve", 2), ("F", "squares", 0), ("F", "proj", 6),
    ("write", 2), ("F", "conv", 6), ("F", "proj", 7),
    ("read", 3), ("F", "conv", 7), ("F", "conv", 8), ("F", "norms", 0),
    ("solve", 3), ("F", "conv", 9), ("F", "keys", 0), ("F", "conv", 10), ("F", "conv", 11),
    ("out", 0), ("F", "silu", 1), ("F", "products", 0), ("F", "system", 0), ("F", "values", 0),
    ("gated", 0), ("F", "values", 1), ("F", "gate", 0), ("F", "pairs", 0), ("F", "gate", 1),
    ("gated", 1), ("F", "start", 0), ("F", "join", 0), ("gated", 2), ("F", "grow", 0),
    ("F", "join", 1), ("turn", 0), ("F", "grow", 1), ("F", "join", 2), ("turn", 1), ("F", "grow", 2),
    ("F", "join", 3), ("project", 0), ("F", "grow", 3), ("F", "join", 4), ("project", 1), ("F", "grow", 4),
    ("F", "join", 5), ("F", "grow", 5), ("F", "newton", 0),
]


def build_kernel(nc, x_rows, x_cols, w_heads, w_ab, conv_w, dt_bias, a_log, gamma, w_out,
                 rms_w, router_w, gate_up, down, tri, levels16, neg_mask, ident16, iota8, exponents, out):
    ctx = ExitStack()
    with ctx:
        def sb(name, shape, dt=F32):
            return ctx.enter_context(nc.sbuf_tensor(name, shape, dt))

        def sem(name):
            return ctx.enter_context(nc.semaphore(name))

        bank = [ctx.enter_context(nc.psum_tensor(f"bank{i}", [P, 512], F32)) for i in range(8)]
        F0, F1, F2, F3, B0, B1, B2, B3 = bank
        FB = bank[:4]

        tri_sb = sb("tri_sb", [P, 4, P])
        upto, after, ident, ones = (tri_sb[:, i, :] for i in range(4))
        lev = sb("lev", [P, 1 + len(LEVELS), P], F16)
        negm = sb("negm", [P, 512], BF16)
        identb = sb("identb", [P, P], BF16)
        identh = sb("identh", [P, P], F16)
        iota_sb = sb("iota_sb", [P, NE])
        xT = sb("xT", [P, KT, TILES * P])
        wab = sb("wab", [P, KT, 64])
        vec32 = sb("vec32", [P, 2, 32])
        gam = sb("gam", [P, 1])
        cw_all = sb("cw_all", [P, KH, GROUPS * TAPS])
        sc_all = sb("sc_all", [P, BODIES, NQ * CELLS])
        acc = sb("acc", [P, TILES, D])
        w_kh = sb("w_kh", [P, KT, 768])
        wo_raw = sb("wo_raw", [P, VH, D])
        wo = sb("wo", [P, VH, D])
        cw = sb("cw", [P, 2, GROUPS * TAPS])
        sc = sb("sc", [P, 2, NQ * CELLS])
        conv = sb("conv", [P, GROUPS, SEQ])
        zone = sb("zone", [P, 5, 2048])

        def zoned(i, pattern, **sizes):
            return zone[:, i, :].rearrange(pattern, **sizes)

        qkT = zoned(0, "p (x a n) -> p x a n", x=2, a=2)
        vT = sb("vT", [P, VH, SEQ])
        sq = sb("sq", [P, 2 * SEQ])
        zs = zoned(1, "p (x c n) -> p x c n", x=2, c=CH)
        ss = sb("ss", [P, 2 * CH])
        nk = sb("nk", [P, CH])
        rk2 = sb("rk2", [P, CH])
        rqs = sb("rqs", [P, CH])
        cj = sb("cj", [P, CELLS])
        kfac = sb("kfac", [P, CELLS])
        keys = zoned(2, "p (x c n) -> p x c n", x=2, c=CELLS)
        vals = zoned(3, "p (x c n) -> p x c n", x=2, c=CELLS)
        gseg = sb("gseg", [P, CELLS, P])
        dec = sb("dec", [P, CELLS, P])
        decc = sb("decc", [P, CELLS, P])
        m32T = sb("m32T", [P, CELLS, P])
        mhiT = sb("mhiT", [P, CELLS, P], F16)
        mloT = sb("mloT", [P, CELLS, P], F16)
        pT = zoned(4, "p (x c n) -> p x c n", x=2, c=CELLS)
        X = sb("X", [P, 2, CELLS, P], F16)
        XT = sb("XT", [P, 2, CELLS, P], F16)
        N = sb("N", [P, CELLS, P], F16)
        TT = sb("TT", [P, 2, CELLS, P])
        rhs = sb("rhs", [P, CELLS, P])
        U = sb("U", [P, CELLS, P])
        S = sb("S", [P, CH, VH * P])
        qs = sb("qs", [P, CELLS, P])
        og = sb("og", [P, CELLS, P])
        og2 = sb("og2", [P, CELLS, P])
        ms = sb("ms", [P, 3, CELLS])
        expo = sb("expo", [P, 2])
        ogT = sb("ogT", [P, CELLS, P])

        s_const = sem("s_const")
        s_w = sem("s_w")
        s_wo = sem("s_wo")
        s_zero = sem("s_zero")
        s_abp = sem("s_abp")
        s_gates = sem("s_gates")
        s_gact = sem("s_gact")
        s_cum = sem("s_cum")
        s_scall = sem("s_scall")
        s_sc = sem("s_sc")
        s_proj = sem("s_proj")
        s_tap = sem("s_tap")
        s_conv = sem("s_conv")
        s_silu = sem("s_silu")
        s_zp = sem("s_zp")
        s_zs = sem("s_zs")
        s_sq = sem("s_sq")
        s_ssp = sem("s_ssp")
        s_ss = sem("s_ss")
        s_small = sem("s_small")
        s_zq = sem("s_zq")
        s_ktp = sem("s_ktp")
        s_keys = sem("s_keys")
        s_vtp = sem("s_vtp")
        s_vals = sem("s_vals")
        s_kq = sem("s_kq")
        s_seg = sem("s_seg")
        s_decp = sem("s_decp")
        s_dec = sem("s_dec")
        s_decc = sem("s_decc")
        s_m = sem("s_m")
        s_p = sem("s_p")
        s_fill = sem("s_fill")
        s_mhi = sem("s_mhi")
        s_mlo = sem("s_mlo")
        s_pair = sem("s_pair")
        s_xp = sem("s_xp")
        s_x0 = sem("s_x0")
        s_np = sem("s_np")
        s_n = sem("s_n")
        s_xp4 = sem("s_xp4")
        s_x = sem("s_x")
        s_xt1 = sem("s_xt1")
        s_resp = sem("s_resp")
        s_res = sem("s_res")
        s_newp = sem("s_newp")
        s_new = sem("s_new")
        s_ksp = sem("s_ksp")
        s_r = sem("s_r")
        s_up = sem("s_up")
        s_u = sem("s_u")
        s_stp = sem("s_stp")
        s_st = sem("s_st")
        s_qsp = sem("s_qsp")
        s_qs = sem("s_qs")
        s_pup = sem("s_pup")
        s_o = sem("s_o")
        s_og = sem("s_og")
        s_og2 = sem("s_og2")
        s_ms = sem("s_ms")
        s_msl = sem("s_msl")
        s_on = sem("s_on")
        s_gtp = sem("s_gtp")
        s_gt = sem("s_gt")
        s_opp = sem("s_opp")
        s_acc = sem("s_acc")
        s_wog = sem("s_wog")
        s_attn = sem("s_attn")
        s_mw = sem("s_mw")
        s_xg = sem("s_xg")
        s_x1 = sem("s_x1")
        s_ln1 = sem("s_ln1")
        s_sqx = sem("s_sqx")
        s_x2 = sem("s_x2")
        s_h = sem("s_h")
        s_htp = sem("s_htp")
        s_ht = sem("s_ht")
        s_rtp = sem("s_rtp")
        s_rt = sem("s_rt")
        s_e2 = sem("s_e2")
        s_gup = sem("s_gup")
        s_sg = sem("s_sg")
        s_a = sem("s_a")
        s_dnp = sem("s_dnp")
        s_y = sem("s_y")
        s_ln2 = sem("s_ln2")
        s_out = sem("s_out")

        CONSTS = 13 * 16

        def body_steps(kh, last):
            for b in range(B):
                for step in SCHEDULE:
                    if step[0] == "F":
                        if not (last and b == B - 1):
                            yield step[1:], kh * B + b + 1, b + 1, kh + (b + 1) // B
                    else:
                        yield step, kh * B + b, b, kh

        def past_first(n):
            return not (isinstance(n, int) and n == 0)

        FRONT = [s[1:] for s in SCHEDULE if s[0] == "F"]

        def level_banks(i):
            return (FB[:2], FB[2:]) if i % 2 == 0 else (FB[2:], FB[:2])

        def half(t, h):
            return t[:, CELLS // 2 * h:CELLS // 2 * (h + 1)]

        def bank4(t):
            return t[:, :].rearrange("p (x n) -> p x n", x=4)

        def scal(p, what, a, n=1):
            return sc[:, p, what * CELLS + a:what * CELLS + a + n]

        NG = BODIES * CELLS

        def gate_buffer(t, i):
            return t[:, :, :].rearrange("p a n -> p (a n)")[:, NG * i:NG * (i + 1)]

        a_in, b_in, al, a_abs = (gate_buffer(conv, i) for i in range(4))
        b_abs, gall = (gate_buffer(gseg, i) for i in range(2))
        e_a, e_b = (gate_buffer(dec, i) for i in range(2))
        ln_a, e_al = (gate_buffer(decc, i) for i in range(2))
        b_den, b_num = (gate_buffer(m32T, i) for i in range(2))

        def by_body(t):
            return t.rearrange("p (n x) -> p n x", x=CELLS)

        def by_tile(t, tile):
            b, c = tile // CH, tile % CH
            return t.rearrange("p (h b x) -> p h b x", b=B, x=CELLS)[:, :, b, c * VH:(c + 1) * VH]

        def scalars_of(what):
            return sc_all[:, :, what * CELLS:(what + 1) * CELLS]

        def gates_vector(dve):
            for t in range(TILES):
                dve.wait_ge(s_abp, 8 * (t // 8 + 1))
                src = bank[t // 8][:, 64 * (t % 8):64 * (t % 8) + 64].rearrange("p (a h v) -> p a h v", a=2, v=VH)
                dve.tensor_tensor(by_tile(a_in, t), src[:, 0], vec32[:, 0, :].rearrange("p (h v) -> p h v", v=VH),
                                  ALU.add).then_inc(s_gates, 1)
                dve.tensor_copy(by_tile(b_in, t), src[:, 1]).then_inc(s_gates, 1)
            dve.tensor_copy(al.rearrange("p (h y v) -> p h y v", y=B * CH, v=VH),
                            vec32[:, 1, :].rearrange("p (h v) -> p h v", v=VH).unsqueeze(2)
                            .broadcast_to([P, KH, B * CH, VH])).then_inc(s_gates, 1)
            dve.wait_ge(s_gates, 2 * TILES + 1)
            dve.scalar_tensor_tensor(a_abs, a_in, -1.0, a_in, op0=ALU.mult, op1=ALU.max).then_inc(s_gates, 1)
            dve.scalar_tensor_tensor(b_abs, b_in, -1.0, b_in, op0=ALU.mult, op1=ALU.max).then_inc(s_gates, 1)
            dve.wait_ge(s_gact, 3)
            dve.tensor_scalar(e_a, e_a, 1.0, None, ALU.add).then_inc(s_gates, 1)
            dve.tensor_scalar(b_den, e_b, 1.0, None, ALU.add).then_inc(s_gates, 1)
            dve.scalar_tensor_tensor(b_num, b_in, 0.0, e_b, op0=ALU.is_ge, op1=ALU.max).then_inc(s_gates, 1)
            dve.wait_ge(s_gates, 2 * TILES + 6)
            dve.reciprocal(b_den, b_den).then_inc(s_gates, 1)
            dve.wait_ge(s_gates, 2 * TILES + 7)
            dve.tensor_tensor(scalars_of(Q_BETA), by_body(b_num), by_body(b_den), ALU.mult).then_inc(s_gates, 1)
            dve.wait_ge(s_gact, 4)
            dve.scalar_tensor_tensor(ln_a, a_in, 0.0, ln_a, op0=ALU.max, op1=ALU.add).then_inc(s_gates, 1)
            dve.wait_ge(s_gates, 2 * TILES + 9)
            dve.scalar_tensor_tensor(gall, e_al, -1.0, ln_a, op0=ALU.mult, op1=ALU.mult).then_inc(s_gates, 1)
            dve.wait_ge(s_gates, GATES)
            dve.tensor_copy(scalars_of(Q_G), by_body(gall)).then_inc(s_scall, 1)
            dve.wait_ge(s_gact, 5)
            dve.tensor_scalar(scalars_of(Q_NEG_EG), scalars_of(Q_EG), -1.0, None, ALU.mult).then_inc(s_scall, 1)

        GATES = 2 * TILES + 10
        GACT = 7

        def gates_scalar(act):
            act.wait_ge(s_gates, 2 * TILES + 3)
            act.activation(e_a, a_abs, ACT.Exp, scale=-1.0).then_inc(s_gact, 1)
            act.activation(e_b, b_abs, ACT.Exp, scale=-1.0).then_inc(s_gact, 1)
            act.activation(e_al, al, ACT.Exp).then_inc(s_gact, 1)
            act.wait_ge(s_gates, 2 * TILES + 4)
            act.activation(ln_a, e_a, ACT.Ln).then_inc(s_gact, 1)
            for i, what in enumerate((Q_EG, Q_ESUF, Q_EEND)):
                act.wait_ge(s_cum, i + 1)
                act.activation(scalars_of(what), bank[2 + i][:, :].rearrange("p (n x) -> p n x", x=CELLS),
                               ACT.Exp).then_inc(s_gact, 1)

        gu_w = zone[:, :, :].rearrange("p a n -> p (a n)")[:, 0:NX * KT * 256].rearrange("p (e k n) -> p e k n", e=NX, k=KT)
        dn_w = zone[:, :, :].rearrange("p a n -> p (a n)")[:, NX * KT * 256:NX * (KT + 1) * 256].rearrange("p (e n) -> p e n", e=NX)
        rt_w = sb("rt_w", [P, KT, NE])
        rms_sb = sb("rms_sb", [P, KT])

        def wide(t, n=D):
            return t[:, :, :].rearrange("p a n -> p (a n)").rearrange("p (c n) -> p c n", n=n)

        xg = wide(gseg)
        x1 = wide(dec)
        hrow = wide(decc)
        sqx = wide(m32T)
        hT = wide(rhs, SEQ)
        sg = wide(TT[:, 0], SEQ)[:, 0:2]
        aT = wide(U, SEQ)[:, 0:2]
        y = wide(qs)
        outrow = wide(og)
        bn = sb("bn", [P, CH, 6])
        mv = sb("mv", [P, CH, 2])
        st1 = sb("st1", [P, 4, CH])
        lg = sb("lg", [P, CH, NE])
        top = sb("top", [P, CH, TOPS])
        ti = sb("ti", [P, CH, TOPS], U32)
        tif = sb("tif", [P, CH, TOPS])
        tw = sb("tw", [P, 4, CH])
        pick = sb("pick", [P, 2, CH, NE])
        wd = sb("wd", [P, CH, NE])

        def moe_loads(sp):
            sp.wait_ge(s_acc, 2 * BODIES)
            sp.dma_start(gu_w, gate_up).then_inc(s_mw, 16)
            sp.dma_start(dn_w, down).then_inc(s_mw, 16)
            sp.dma_start(rt_w[:, :, :], router_w).then_inc(s_mw, 16)
            sp.dma_start(rms_sb[:, :], rms_w).then_inc(s_mw, 16)
            sp.dma_start(xg, x_rows[0:SEQ, :].rearrange("(c p) n -> p c n", p=P)).then_inc(s_xg, 16)
            for gi in range(B):
                if gi + 1 < B:
                    sp.wait_ge(s_x1, gi + 1)
                    sp.dma_start(xg, x_rows[SEQ * (gi + 1):SEQ * (gi + 2), :].rearrange("(c p) n -> p c n", p=P)).then_inc(s_xg, 16)
                sp.wait_ge(s_ln2, (gi + 1) * LN2)
                sp.dma_start(out[SEQ * gi:SEQ * (gi + 1), :].rearrange("(c p) n -> p c n", p=P), outrow).then_inc(s_out, 16)
            sp.wait_ge(s_out, 16 * B)

        def moe_pool(pool):
            pass

        LN1 = LN2 = 3 * CH + 1
        RT = 2 * CH + 10

        def moe_tensor(pe):
            pe.wait_ge(s_mw, 64)
            for g in range(B):
                for c in range(CH):
                    pe.wait_ge(s_h, g * (CH + 1) + 1 + c + 1)
                    for k in range(KT):
                        mm = pe.transpose((F0, F1)[k][:, c * P:(c + 1) * P], hrow[:, c, k * P:(k + 1) * P], ident)
                mm.then_inc(s_htp, 1)
                pe.wait_ge(s_ht, 2 * g + 2)
                if g > 0:
                    pe.wait_ge(s_rt, (g - 1) * RT + 1)
                for c in range(CH):
                    for k in range(KT):
                        mm = pe.matmul(F2[:, c * NE:(c + 1) * NE], hT[:, k, c * P:(c + 1) * P], rt_w[:, k, :],
                                       start=(k == 0), stop=(k == KT - 1))
                mm.then_inc(s_rtp, 1)

                def into(e):
                    i = g * NX + e
                    for a, dst in enumerate(((B0, B1), (F3, F0))[e % 2]):
                        if i > 1:
                            pe.wait_ge(s_a, i - 1)
                        for k in range(KT):
                            mm = pe.matmul(dst[:, :], gu_w[:, e, k, a * P:(a + 1) * P], hT[:, k, :],
                                           start=(k == 0), stop=(k == KT - 1))
                        mm.then_inc(s_gup, 1)

                def outof(e):
                    i = g * NX + e
                    pe.wait_ge(s_a, i + 1)
                    for h, dst in enumerate((B2, B3)):
                        if i > 0:
                            pe.wait_ge(s_y, (i - 1) * CH + 2 * h + 2)
                        for c in range(2):
                            mm = pe.matmul(dst[:, 256 * c:256 * c + 256], aT[:, e % 2, (2 * h + c) * P:(2 * h + c + 1) * P],
                                           dn_w[:, e, :], start=True, stop=True)
                        mm.then_inc(s_dnp, 1)

                into(0)
                for e in range(1, NX):
                    into(e)
                    outof(e - 1)
                outof(NX - 1)

        def moe_scalar(act):
            act.wait_ge(s_mw, 64)
            for g in range(B):
                act.wait_ge(s_ln1, g * LN1 + 2 * CH + 1)
                act.activation(st1[:, 1, :], st1[:, 0, :], ACT.Ln).then_inc(s_sqx, 1)
                act.wait_ge(s_sqx, g * 7 + 1)
                act.activation(st1[:, 2, :], st1[:, 1, :], ACT.Exp, scale=-0.5).then_inc(s_sqx, 1)
                act.wait_ge(s_ln1, (g + 1) * LN1)
                act.activation(sqx, x1, ACT.Square).then_inc(s_sqx, 1)
                act.wait_ge(s_h, g * (CH + 1) + 1)
                act.activation(st1[:, 1, :], st1[:, 0, :], ACT.Ln).then_inc(s_sqx, 1)
                act.wait_ge(s_sqx, g * 7 + 4)
                act.activation(st1[:, 2, :], st1[:, 1, :], ACT.Exp, scale=-0.5).then_inc(s_sqx, 1)
                act.wait_ge(s_htp, g + 1)
                for k in range(KT):
                    act.activation(hT[:, k, :], (F0, F1)[k][:, :], ACT.Copy, scale=rms_sb[:, k:k + 1]).then_inc(s_ht, 1)
                act.wait_ge(s_e2, 2 * g + 1)
                act.activation(tw[:, 1, :], tw[:, 0, :], ACT.Exp).then_inc(s_e2, 1)
                for e in range(NX):
                    i = g * NX + e
                    act.wait_ge(s_gup, 2 * i + 1)
                    if i > 1:
                        act.wait_ge(s_a, i - 1)
                    act.activation(sg[:, e % 2], (B0, F3)[e % 2][:, :], ACT.Silu).then_inc(s_sg, 1)
                act.wait_ge(s_ln2, g * LN2 + 2 * CH + 1)
                act.activation(st1[:, 1, :], st1[:, 0, :], ACT.Ln).then_inc(s_sqx, 1)
                act.wait_ge(s_sqx, g * 7 + 6)
                act.activation(st1[:, 2, :], st1[:, 1, :], ACT.Exp, scale=-0.5).then_inc(s_sqx, 1)

        def moe_vector(dve):
            dve.wait_ge(s_acc, 2 * BODIES)

            def norm_stats(src, s, base):
                for c in range(CH):
                    dve.bn_stats(bn[:, c, :], src[:, c, :]).then_inc(s, 1)
                for c in range(CH):
                    dve.wait_ge(s, base + c + 1)
                    dve.bn_aggr(mv[:, c, :], bn[:, c, :]).then_inc(s, 1)
                dve.wait_ge(s, base + 2 * CH)
                dve.tensor_scalar(st1[:, 0, :], mv[:, :, 1], 1e-5, None, ALU.add).then_inc(s, 1)

            def normalise(dst, src, s):
                for c in range(CH):
                    dve.tensor_scalar(dst[:, c, :], src[:, c, :], mv[:, c, 0:1], st1[:, 2, c:c + 1],
                                      ALU.subtract, ALU.mult).then_inc(s, 1)

            for g in range(B):
                dve.wait_ge(s_xg, 16 * (g + 1))
                if g > 0:
                    dve.wait_ge(s_ln2, g * LN2)
                dve.tensor_tensor(y, xg, acc[:, g * CH:(g + 1) * CH, :], ALU.add).then_inc(s_x1, 1)
                dve.wait_ge(s_x1, g + 1)
                norm_stats(y, s_ln1, g * LN1)
                dve.wait_ge(s_sqx, g * 7 + 2)
                normalise(x1, y, s_ln1)
                dve.wait_ge(s_sqx, g * 7 + 3)
                dve.tensor_reduce(st1[:, 3, :], sqx, AX, ALU.add).then_inc(s_x2, 1)
                dve.wait_ge(s_x2, g + 1)
                dve.tensor_scalar(st1[:, 0, :], st1[:, 3, :], 1.0 / D, 1e-6, ALU.mult, ALU.add).then_inc(s_h, 1)
                dve.wait_ge(s_sqx, g * 7 + 5)
                for c in range(CH):
                    dve.tensor_scalar(hrow[:, c, :], x1[:, c, :], st1[:, 2, c:c + 1], None, ALU.mult).then_inc(s_h, 1)
                dve.wait_ge(s_rtp, g + 1)
                r = g * RT
                dve.tensor_copy(lg[:, :, :], F2[:, 0:CH * NE].rearrange("p (c e) -> p c e", e=NE)).then_inc(s_rt, 1)
                dve.wait_ge(s_rt, r + 1)
                for c in range(CH):
                    dve.max(top[:, c, :], lg[:, c, :]).then_inc(s_rt, 1)
                for c in range(CH):
                    dve.wait_ge(s_rt, r + 2 + c)
                    dve.max_index(ti[:, c, :], top[:, c, :], lg[:, c, :]).then_inc(s_rt, 1)
                dve.tensor_tensor(tw[:, 0, :], top[:, :, 1], top[:, :, 0], ALU.subtract).then_inc(s_e2, 1)
                dve.wait_ge(s_rt, r + 1 + 2 * CH)
                dve.tensor_copy(tif[:, :, :], ti[:, :, :]).then_inc(s_rt, 1)
                dve.wait_ge(s_e2, 2 * g + 2)
                dve.tensor_scalar(tw[:, 2, :], tw[:, 1, :], 1.0, None, ALU.add).then_inc(s_rt, 1)
                dve.wait_ge(s_rt, r + 3 + 2 * CH)
                dve.reciprocal(tw[:, 2, :], tw[:, 2, :]).then_inc(s_rt, 1)
                dve.wait_ge(s_rt, r + 4 + 2 * CH)
                dve.tensor_tensor(tw[:, 3, :], tw[:, 1, :], tw[:, 2, :], ALU.mult).then_inc(s_rt, 1)
                for j in range(2):
                    dve.tensor_tensor(pick[:, j], iota_sb[:, :].unsqueeze(1).broadcast_to([P, CH, NE]),
                                      tif[:, :, j:j + 1].broadcast_to([P, CH, NE]), ALU.is_equal).then_inc(s_rt, 1)
                dve.wait_ge(s_rt, r + 7 + 2 * CH)
                for j in range(2):
                    dve.tensor_tensor(pick[:, j], pick[:, j], tw[:, 2 + j, :].unsqueeze(2).broadcast_to([P, CH, NE]),
                                      ALU.mult).then_inc(s_rt, 1)
                dve.wait_ge(s_rt, r + 9 + 2 * CH)
                dve.tensor_tensor(wd[:, :, :], pick[:, 0], pick[:, 1], ALU.add).then_inc(s_rt, 1)
                dve.wait_ge(s_rt, r + 10 + 2 * CH)

                def gated(e):
                    i = g * NX + e
                    dve.wait_ge(s_sg, i + 1)
                    dve.wait_ge(s_gup, 2 * i + 2)
                    if i > 1:
                        dve.wait_ge(s_dnp, 2 * (i - 1))
                    dve.tensor_tensor(aT[:, e % 2], sg[:, e % 2], (B1, F0)[e % 2][:, :], ALU.mult).then_inc(s_a, 1)

                def added(e):
                    i = g * NX + e
                    for c in range(CH):
                        dve.wait_ge(s_dnp, 2 * i + c // 2 + 1)
                        if e > 0:
                            dve.wait_ge(s_y, (i - 1) * CH + c + 1)
                        src = (B2, B3)[c // 2][:, 256 * (c % 2):256 * (c % 2) + 256]
                        dve.scalar_tensor_tensor(y[:, c, :], src, wd[:, c, e:e + 1] if e < NE else 1.0,
                                                 (y if e else x1)[:, c, :], op0=ALU.mult, op1=ALU.add).then_inc(s_y, 1)

                gated(0)
                for e in range(1, NX):
                    gated(e)
                    added(e - 1)
                added(NX - 1)
                dve.wait_ge(s_y, (g + 1) * NX * CH)
                norm_stats(y, s_ln2, g * LN2)
                dve.wait_ge(s_sqx, g * 7 + 7)
                if g > 0:
                    dve.wait_ge(s_out, 16 * g)
                normalise(outrow, y, s_ln2)

        block = ctx.enter_context(nc.Block())

        @block.sync
        def _(sp):
            sp.dma_start(w_kh[:, :, :], w_heads[0].rearrange("p (t n) -> p t n", t=KT)).then_inc(s_w, 16)
            for dst, src in (
                (xT[:, :, :], x_cols.rearrange("(t p) n -> p t n", p=P)),
                (tri_sb[:, :, :], tri), (wab[:, :, :], w_ab.rearrange("(t p) n -> p t n", p=P)),
                (vec32[:, 0, :], dt_bias), (vec32[:, 1, :], a_log),
                (negm[:, :], neg_mask[:, 0:512]), (identb[:, :], neg_mask[:, 512:640]),
                (lev[:, :, :], levels16), (identh[:, :], ident16), (iota_sb[:, :], iota8),
                (gam[:, :], gamma), (expo[:, :], exponents), (cw_all[:, :, :], conv_w),
            ):
                sp.dma_start(dst, src).then_inc(s_const, 16)
            sp.dma_start(wo_raw[:, :, :], w_out[0]).then_inc(s_wo, 16)

            def weights(kh):
                sp.wait_ge(s_zp, (kh * B + B) * 2)
                sp.dma_start(w_kh[:, :, :], w_heads[bass.ds(kh + 1, 1)].rearrange("o p (t n) -> (o p) t n", t=KT)).then_inc(s_w, 16)
                sp.wait_ge(s_wog, kh + 1)
                sp.dma_start(wo_raw[:, :, :], w_out[bass.ds(kh + 1, 1)].rearrange("o p v n -> (o p) v n")).then_inc(s_wo, 16)

            sp.wait_ge(s_const, CONSTS)
            with sp.Fori(0, KH - 1) as kh:
                weights(kh)
            moe_loads(sp)

        @block.gpsimd
        def _(pool):
            pool.memset(acc[:, :, :], 0.0).then_inc(s_zero, 1)
            pool.wait_ge(s_const, CONSTS)

            def scale_wo(kh):
                pool.wait_ge(s_wo, 16 * (kh + 1))
                pool.tensor_tensor(wo[:, :, :], wo_raw[:, :, :], gam[:, 0:1].unsqueeze(2).broadcast_to([P, VH, D]), ALU.mult).then_inc(s_wog, 1)

            def run(step, n, b, head):
                p = b % 2
                if step == ("scalars", 0):
                    pool.wait_ge(s_sc, n * 2 + 2)
                    if past_first(n):
                        pool.wait_ge(s_decp, n * 2)
                    pool.tensor_tensor(gseg[:, :, :], after.unsqueeze(1).broadcast_to([P, CELLS, P]),
                                       scal(p, Q_G, 0, CELLS).unsqueeze(2).broadcast_to([P, CELLS, P]),
                                       ALU.mult).then_inc(s_seg, 1)
                elif step == ("norms", 0):
                    pool.wait_ge(s_ss, n * 3 + 3)
                    if past_first(n):
                        pool.wait_ge(s_keys, n)
                    pool.tensor_tensor(cj[:, :].rearrange("p (c v) -> p c v", v=VH),
                                       scal(p, Q_BETA, 0, CELLS).rearrange("p (c v) -> p c v", v=VH),
                                       rk2[:, :].unsqueeze(2).broadcast_to([P, CH, VH]), ALU.mult).then_inc(s_small, 1)
                    pool.wait_ge(s_small, n * 4 + 1)
                    pool.tensor_tensor(kfac[:, :], cj[:, :], scal(p, Q_ESUF, 0, CELLS), ALU.mult).then_inc(s_small, 1)
                    for h in range(2):
                        pool.wait_ge(s_dec, n * 2 + h + 1)
                        if h == 0 and past_first(n):
                            pool.wait_ge(s_p, n * 2)
                        pool.tensor_tensor(half(decc, h), half(dec, h),
                                           cj[:, 4 * h:4 * h + 4].unsqueeze(2).broadcast_to([P, 4, P]), ALU.mult).then_inc(s_decc, 1)
                    pool.tensor_tensor(nk[:, :], ss[:, CH:], expo[:, 1:2].broadcast_to([P, CH]), ALU.pow).then_inc(s_small, 1)
                    pool.tensor_tensor(rqs[:, :], ss[:, 0:CH], expo[:, 0:1].broadcast_to([P, CH]), ALU.pow).then_inc(s_small, 1)
                elif step == ("start", 0):
                    pool.wait_ge(s_zs, n * 2 + 2)
                    pool.wait_ge(s_small, n * 4 + 4)
                    pool.tensor_tensor(zs[:, p, :, :], zs[:, p, :, :],
                                       rqs[:, :].unsqueeze(2).broadcast_to([P, CH, VH * P]), ALU.mult).then_inc(s_zq, 1)
                elif step == ("system", 0):
                    for h in range(2):
                        pool.wait_ge(s_const, CONSTS)
                        pool.wait_ge(s_m, n * 2 + h + 1)
                        pool.affine_select(out=half(m32T, h), in_=half(m32T, h), compare_op=ALU.not_equal, fill=1.0,
                                           base=0, pattern=[[0, 4], [-1, P]], channel_multiplier=1).then_inc(s_fill, 1)
                    pool.wait_ge(s_mhi, n * 2 + 2)
                    pool.tensor_tensor(mloT[:, :, :], m32T[:, :, :], mhiT[:, :, :], ALU.subtract).then_inc(s_mlo, 1)
                elif step == ("gated", 2):
                    pool.wait_ge(s_ms, n * 3 + 3)
                    pool.tensor_tensor(ms[:, 2, :], ms[:, 1, :], expo[:, 0:1].broadcast_to([P, CELLS]),
                                       ALU.pow).then_inc(s_msl, 1)
                    for h in range(2):
                        pool.wait_ge(s_msl, n + 1)
                        pool.tensor_tensor(half(og, h), half(og, h),
                                           ms[:, 2, 4 * h:4 * h + 4].unsqueeze(2).broadcast_to([P, 4, P]),
                                           ALU.mult).then_inc(s_on, 1)

            for step in FRONT:
                run(step, 0, 0, 0)

            def key_head(kh, last):
                for step, n, b, head in body_steps(kh, last):
                    run(step, n, b, head)
                    if step == ("project", 1) and b == B - 1 and not last:
                        pool.wait_ge(s_opp, (kh * B + B) * 2)
                        scale_wo(kh + 1)

            scale_wo(0)
            with pool.Fori(0, KH - 1) as kh:
                key_head(kh, False)
            key_head(KH - 1, True)
            moe_pool(pool)

        @block.tensor
        def _(pe):
            pe.wait_ge(s_const, CONSTS)
            for t in range(TILES):
                for k in range(KT):
                    mm = pe.matmul(bank[t // 8][:, 64 * (t % 8):64 * (t % 8) + 64], xT[:, k, t * P:(t + 1) * P],
                                   wab[:, k, :], start=(k == 0), stop=(k == KT - 1))
                mm.then_inc(s_abp, 1)
            pe.wait_ge(s_gates, GATES)
            for i, m in enumerate((upto, after, ones)):
                pe.matmul(bank[2 + i][:, :], m, gall, start=True, stop=True).then_inc(s_cum, 1)
            pe.wait_ge(s_gact, GACT)

            def run(step, n, b, head):
                p = b % 2
                later = past_first(n)
                name, i = step
                if name == "proj":
                    g, k = divmod(i, KT)
                    if i == 0 and b % B == 0:
                        pe.wait_ge(s_w, 16 * (head + 1))
                    if g >= 2 and k == 0:
                        pe.wait_ge(s_dec, n * 2 + g - 1)
                    mm = pe.matmul(FB[g][:, :], w_kh[:, k, g * P:(g + 1) * P], xT[:, k, bass.ts(b % B, SEQ)],
                                   start=(k == 0), stop=(k == KT - 1))
                    if k == KT - 1:
                        mm.then_inc(s_proj, 1)
                elif name == "decay":
                    if i == 0:
                        pe.wait_ge(s_seg, n + 1)
                    if later:
                        pe.wait_ge(s_new, (n - 1) * 2 + i + 1)
                    pe.matmul(FB[2 + i][:, :], identb[:, :], negm[:, :], start=True, stop=False, skip_group_check=True)
                    for x in range(4):
                        mm = pe.matmul(FB[2 + i][:, x * P:(x + 1) * P], gseg[:, 4 * i + x, :], upto, start=False,
                                       stop=(x == 3), skip_group_check=True)
                    mm.then_inc(s_decp, 1)
                elif name == "gate":
                    pe.wait_ge(s_vals, n * 2 + i + 1)
                    for c in range(2):
                        t = (b % B) * CH + 2 * i + c
                        for k in range(KT):
                            mm = pe.matmul(FB[2 + i][:, 256 * c:256 * c + 256], xT[:, k, t * P:(t + 1) * P], w_kh[:, k, 512:768],
                                           start=(k == 0), stop=(k == KT - 1))
                    mm.then_inc(s_zp, 1)
                elif name == "norms":
                    pe.wait_ge(s_sq, n + 1)
                    for c in range(2 * CH):
                        mm = pe.matmul(F0[:, c:c + 1], sq[:, c * P:(c + 1) * P], ones[:, 0:1], start=True, stop=True)
                    mm.then_inc(s_ssp, 1)
                elif name == "keys":
                    for c in range(CH):
                        mm = pe.transpose(F1[:, c * P:(c + 1) * P], qkT[:, p, 1, c * P:(c + 1) * P], ident)
                    mm.then_inc(s_ktp, 1)
                elif name == "values":
                    if i == 0:
                        pe.wait_ge(s_silu, n * 4 + 4)
                    for c in range(2):
                        for v in range(VH):
                            o = (c * VH + v) * P
                            t = (2 * i + c) * P
                            mm = pe.transpose(FB[2 + i][:, o:o + P], vT[:, v, t:t + P], ident)
                    mm.then_inc(s_vtp, 1)
                elif name == "products":
                    pe.wait_ge(s_ss, n * 3 + 2)
                    for a, dst in ((1, F0), (0, F1)):
                        if a == 0:
                            pe.wait_ge(s_keys, n + 1)
                        for c in range(CH):
                            mm = pe.matmul(dst[:, c * P:(c + 1) * P], qkT[:, p, 1, c * P:(c + 1) * P],
                                           qkT[:, p, a, c * P:(c + 1) * P], start=True, stop=True)
                        mm.then_inc(s_kq, 1)
                elif name == "start":
                    pe.wait_ge(s_pair, n * 2 + 2)
                    f0h = F0[:, :].bitcast(F16)
                    for x in range(CELLS):
                        mm = pe.transpose(f0h[:, x * P:(x + 1) * P], XT[:, 0, x, :], identh[:, :])
                    mm.then_inc(s_xp, 1)
                elif name == "join":
                    for h in range(2):
                        if i == 0:
                            if h == 0:
                                pe.wait_ge(s_x0, n + 1)
                                pe.wait_ge(s_p, n * 2 + 2)
                        else:
                            pe.wait_ge(s_x, n * 18 + 3 * (i - 1) + h + 1)
                        for x in range(4):
                            mm = pe.matmul(level_banks(i)[0][h][:, x * P:(x + 1) * P], mhiT[:, 4 * h + x, :],
                                           X[:, i % 2, 4 * h + x, :], start=True, stop=True)
                        mm.then_inc(s_np, 1)
                elif name == "grow":
                    mxb, xb = level_banks(i)
                    for t in range(2):
                        for h in range(2):
                            if t == 0:
                                if i == 0:
                                    if h == 0:
                                        pe.wait_ge(s_zs, n * 2 + 2)
                                elif h == 0:
                                    pe.wait_ge(s_x, n * 18 + 3 * i)
                                else:
                                    pe.wait_ge(s_xt1, n * 6 + i)
                                pe.wait_ge(s_n, n * 12 + 2 * i + h + 1)
                            for x in range(4):
                                c = 4 * h + x
                                if t == 0:
                                    mm = pe.matmul(xb[h][:, x * P:(x + 1) * P], XT[:, i % 2, c, :], N[:, c, :], start=True, stop=True)
                                else:
                                    mm = pe.matmul(mxb[h][:, x * P:(x + 1) * P], N[:, c, :], XT[:, i % 2, c, :], start=True, stop=True)
                            mm.then_inc(s_xp4, 1)
                elif name == "newton":
                    for h in range(2):
                        pe.wait_ge(s_x, n * 18 + 15 + h + 1)
                        if h == 0:
                            pe.wait_ge(s_mlo, n + 1)
                        for x in range(4):
                            c = 4 * h + x
                            pe.matmul(FB[h][:, x * P:(x + 1) * P], mhiT[:, c, :], X[:, 0, c, :], start=True, stop=False)
                            mm = pe.matmul(FB[h][:, x * P:(x + 1) * P], mloT[:, c, :], X[:, 0, c, :], start=False, stop=True)
                        mm.then_inc(s_resp, 1)
                    for h in range(2):
                        if h == 0:
                            pe.wait_ge(s_x, n * 18 + 18)
                        else:
                            pe.wait_ge(s_xt1, n * 6 + 6)
                        pe.wait_ge(s_res, n * 2 + h + 1)
                        for x in range(4):
                            c = 4 * h + x
                            mm = pe.matmul(FB[2 + h][:, x * P:(x + 1) * P], N[:, c, :], XT[:, 0, c, :], start=True, stop=True)
                        mm.then_inc(s_newp, 1)
                elif name == "read":
                    c = i
                    qT, kT = (qkT[:, p, a, c * P:(c + 1) * P] for a in range(2))
                    pe.wait_ge(s_st, n * 6 + 2 * c)
                    pe.matmul(B0[:, 0:256], kT, S[:, c, :], start=True, stop=True).then_inc(s_ksp, 1)
                    mm = pe.matmul((B2, B2, B3, B3)[c][:, 256 * (c % 2):256 * (c % 2) + 256], qT, S[:, c, :],
                                   start=True, stop=True)
                    if c % 2:
                        mm.then_inc(s_qsp, 1)
                elif name == "solve":
                    c = i
                    if c == 0:
                        pe.wait_ge(s_new, n * 2 + 2)
                        pe.wait_ge(s_vals, n * 2 + 1)
                        pe.wait_ge(s_acc, n * 2)
                    for v in range(VH):
                        x = c * VH + v
                        if c > 0:
                            pe.wait_ge(s_r, n * 6 + 2 * c - 2 + v + 1)
                        mm = pe.matmul(B1[:, v * P:(v + 1) * P], TT[:, p, x, :], rhs[:, x, :] if c else vals[:, p, x, :],
                                       start=True, stop=True)
                    mm.then_inc(s_up, 1)
                elif name == "write":
                    c = i
                    pe.wait_ge(s_u, n * 4 + c + 1)
                    if c == 0:
                        pe.wait_ge(s_keys, n + 1)
                    for v in range(VH):
                        x = c * VH + v
                        mm = pe.matmul(B0[:, v * P:(v + 1) * P], keys[:, p, x, :], U[:, x, :], start=True, stop=True)
                    mm.then_inc(s_stp, 1)
                elif name == "out":
                    pe.wait_ge(s_p, n * 2 + 2)
                    pe.wait_ge(s_u, n * 4 + 4)
                    for h, dst in ((0, B0), (1, B1)):
                        for x in range(4):
                            c = 4 * h + x
                            mm = pe.matmul(dst[:, x * P:(x + 1) * P], pT[:, p, c, :], U[:, c, :], start=True, stop=True)
                        mm.then_inc(s_pup, 1)
                elif name == "turn":
                    pe.wait_ge(s_on, n * 2 + i + 1)
                    for x in range(4):
                        mm = pe.transpose((B2, B3)[i][:, x * P:(x + 1) * P], og[:, 4 * i + x, :], ident)
                    mm.then_inc(s_gtp, 1)
                elif name == "project":
                    if b == 0 and i == 0:
                        pe.wait_ge(s_wog, head + 1)
                    pe.wait_ge(s_gt, n * 2 + i + 1)
                    for c in range(2):
                        for v in range(VH):
                            mm = pe.matmul((B0, B1)[i][:, 256 * c:256 * c + 256], ogT[:, 4 * i + 2 * c + v, :], wo[:, v, :],
                                           start=(v == 0), stop=(v == VH - 1))
                    mm.then_inc(s_opp, 1)

            for step in FRONT:
                run(step, 0, 0, 0)
            with pe.Fori(0, KH - 1) as kh:
                for step, n, b, head in body_steps(kh, False):
                    run(step, n, b, head)
            for step, n, b, head in body_steps(KH - 1, True):
                run(step, n, b, head)
            moe_tensor(pe)

        @block.scalar
        def _(act):
            act.wait_ge(s_const, CONSTS)
            gates_scalar(act)

            def run(step, n, b, head):
                p = b % 2
                later = past_first(n)
                name, i = step
                if name == "proj":
                    if i == 0:
                        act.wait_ge(s_sc, n * 2 + 1)
                    g, k = divmod(i, KT)
                    if k == KT - 1:
                        act.wait_ge(s_proj, n * 4 + g + 1)
                        act.activation(conv[:, g, :], FB[g][:, :], ACT.Copy,
                                       scale=cw[:, p, g * TAPS + 3:g * TAPS + 4]).then_inc(s_tap, 1)
                elif name == "silu":
                    for g in (2 * i, 2 * i + 1):
                        act.wait_ge(s_conv, n * 12 + 3 * g + 3)
                        dst = qkT[:, p, g, :] if g < 2 else vT[:, g - 2, :]
                        act.activation(dst, conv[:, g, :], ACT.Silu).then_inc(s_silu, 1)
                elif name == "gate":
                    act.wait_ge(s_zp, n * 2 + i + 1)
                    act.activation(zs[:, p, 2 * i:2 * i + 2, :], FB[2 + i][:, :].rearrange("p (c n) -> p c n", c=2),
                                   ACT.Silu).then_inc(s_zs, 1)
                elif name == "squares":
                    act.wait_ge(s_silu, n * 4 + 2)
                    act.activation(sq[:, :], qkT[:, p, :, :].rearrange("p a n -> p (a n)"), ACT.Square).then_inc(s_sq, 1)
                elif name == "decay":
                    act.wait_ge(s_decp, n * 2 + i + 1)
                    act.activation(half(dec, i), bank4(FB[2 + i]), ACT.Exp).then_inc(s_dec, 1)
                elif name == "system":
                    for h in range(2):
                        act.wait_ge(s_fill, n * 2 + h + 1)
                        act.activation(half(mhiT, h), half(m32T, h), ACT.Copy).then_inc(s_mhi, 1)
                elif name == "start":
                    act.wait_ge(s_xp, n + 1)
                    act.activation(X[:, 0], F0[:, :].bitcast(F16).rearrange("p (x n) -> p x n", x=CELLS), ACT.Copy).then_inc(s_x0, 1)
                elif name == "grow":
                    mxb, xb = level_banks(i)
                    for t, (dst, h, src) in enumerate(((X, 0, xb[0]), (X, 1, xb[1]), (XT, 0, mxb[0]))):
                        act.wait_ge(s_xp4, n * 24 + 4 * i + t + 1)
                        act.activation(half(dst[:, (i + 1) % 2], h), bank4(src), ACT.Copy).then_inc(s_x, 1)
                elif name == "solve":
                    act.wait_ge(s_up, n * 4 + i + 1)
                    act.activation(U[:, 2 * i:2 * i + 2, :], B1[:, 0:256].rearrange("p (v n) -> p v n", v=VH),
                                   ACT.Copy).then_inc(s_u, 1)
                elif name == "gated" and i == 1:
                    for h in range(2):
                        act.wait_ge(s_og, n * 2 + h + 1)
                        act.activation(half(og2, h), half(og, h), ACT.Square).then_inc(s_og2, 1)
                elif name == "turn":
                    act.wait_ge(s_gtp, n * 2 + i + 1)
                    act.activation(half(ogT, i), bank4((B2, B3)[i]), ACT.Copy).then_inc(s_gt, 1)

            for step in FRONT:
                run(step, 0, 0, 0)
            with act.Fori(0, KH - 1) as kh:
                for step, n, b, head in body_steps(kh, False):
                    run(step, n, b, head)
            for step, n, b, head in body_steps(KH - 1, True):
                run(step, n, b, head)
            moe_scalar(act)

        @block.vector
        def _(dve):
            dve.wait_ge(s_const, CONSTS)
            gates_vector(dve)

            def run(step, n, b, head):
                p = b % 2
                later = past_first(n)
                name, i = step
                if name == "scalars":
                    if later:
                        dve.wait_ge(s_tap, (n - 1) * GROUPS)
                        dve.wait_ge(s_seg, n)
                    else:
                        dve.wait_ge(s_scall, 2)
                        dve.wait_ge(s_gact, GACT)
                    dve.tensor_scalar(cw[:, p, :], cw_all[:, bass.ds(head, 1), :].rearrange("p o n -> p (o n)"),
                                      1.0, None, ALU.mult).then_inc(s_sc, 1)
                    dve.tensor_scalar(sc[:, p, :], sc_all[:, bass.ds(n, 1), :].rearrange("p o n -> p (o n)"),
                                      1.0, None, ALU.mult).then_inc(s_sc, 1)
                elif name == "conv":
                    g, j = i // 3, i % 3 + 1
                    if j == 1:
                        dve.wait_ge(s_tap, n * 4 + g + 1)
                    else:
                        dve.wait_ge(s_conv, n * 12 + i)
                    dve.scalar_tensor_tensor(conv[:, g, j:], FB[g][:, 0:SEQ - j], cw[:, p, g * TAPS + 3 - j:g * TAPS + 4 - j],
                                             conv[:, g, j:], op0=ALU.mult, op1=ALU.add).then_inc(s_conv, 1)
                elif name == "norms":
                    dve.wait_ge(s_ssp, n + 1)
                    dve.tensor_scalar(ss[:, CH:], F0[:, CH:2 * CH], 1e-6, None, ALU.add).then_inc(s_ss, 1)
                    dve.tensor_scalar(ss[:, 0:CH], F0[:, 0:CH], float(P), P * 1e-6, ALU.mult, ALU.add).then_inc(s_ss, 1)
                    dve.wait_ge(s_ss, n * 3 + 1)
                    dve.reciprocal(rk2[:, :], ss[:, CH:]).then_inc(s_ss, 1)
                elif name == "keys":
                    dve.wait_ge(s_ktp, n + 1)
                    dve.wait_ge(s_small, n * 4 + 2)
                    dve.tensor_tensor(keys[:, p].rearrange("p (c v) n -> p c v n", v=VH),
                                      F1[:, :].rearrange("p (c n) -> p c n", c=CH).unsqueeze(2).broadcast_to([P, CH, VH, P]),
                                      kfac[:, :].rearrange("p (c v) -> p c v", v=VH).unsqueeze(3).broadcast_to([P, CH, VH, P]),
                                      ALU.mult).then_inc(s_keys, 1)
                elif name == "values":
                    dve.wait_ge(s_vtp, n * 2 + i + 1)
                    dve.wait_ge(s_small, n * 4 + 3)
                    dve.tensor_tensor(half(vals[:, p], i).rearrange("p (c v) n -> p c (v n)", v=VH),
                                      FB[2 + i][:, :].rearrange("p (c n) -> p c n", c=2),
                                      nk[:, 2 * i:2 * i + 2].unsqueeze(2).broadcast_to([P, 2, VH * P]),
                                      ALU.mult).then_inc(s_vals, 1)
                elif name == "system":
                    for dst, src, done in ((m32T[:, :, :], F0, s_m), (pT[:, p], F1, s_p)):
                        dve.wait_ge(s_kq, n * 2 + (1 if done is s_m else 2))
                        for h in range(2):
                            if done is s_m:
                                dve.wait_ge(s_decc, n * 2 + h + 1)
                                if h == 0 and later:
                                    dve.wait_ge(s_mlo, n)
                            dve.tensor_tensor(half(dst, h).rearrange("p (c v) n -> p c v n", v=VH),
                                              src[:, :].rearrange("p (c n) -> p c n", c=CH)[:, 2 * h:2 * h + 2]
                                              .unsqueeze(2).broadcast_to([P, 2, VH, P]),
                                              half(decc, h).rearrange("p (c v) n -> p c v n", v=VH),
                                              ALU.mult).then_inc(done, 1)
                elif name == "pairs":
                    for h in range(2):
                        dve.wait_ge(s_mhi, n * 2 + h + 1)
                        dve.tensor_tensor(half(XT[:, 0], h), half(mhiT, h), lev[:, 0, :].unsqueeze(1).broadcast_to([P, 4, P]),
                                          ALU.mult).then_inc(s_pair, 1)
                elif name == "join":
                    for h in range(2):
                        dve.wait_ge(s_np, n * 12 + 2 * i + h + 1)
                        if i > 0:
                            dve.wait_ge(s_xp4, n * 24 + 4 * (i - 1) + 3 + h)
                        dve.tensor_tensor(half(N, h), bank4(level_banks(i)[0][h]),
                                          lev[:, 1 + i, :].unsqueeze(1).broadcast_to([P, 4, P]), ALU.mult).then_inc(s_n, 1)
                elif name == "grow":
                    dve.wait_ge(s_xp4, n * 24 + 4 * i + 4)
                    dve.tensor_copy(half(XT[:, (i + 1) % 2], 1), bank4(level_banks(i)[0][1])).then_inc(s_xt1, 1)
                elif name == "newton":
                    for h in range(2):
                        dve.wait_ge(s_resp, n * 2 + h + 1)
                        dve.tensor_tensor(half(N, h), ident.unsqueeze(1).broadcast_to([P, 4, P]), bank4(FB[h]),
                                          ALU.subtract).then_inc(s_res, 1)
                    for h in range(2):
                        dve.wait_ge(s_newp, n * 2 + h + 1)
                        dve.tensor_tensor(half(TT[:, p], h), bank4(FB[2 + h]), half(XT[:, 0], h), ALU.add).then_inc(s_new, 1)
                elif name == "read":
                    dve.wait_ge(s_ksp, n * 3 + i)
                    for v in range(VH):
                        x = i * VH + v
                        dve.scalar_tensor_tensor(rhs[:, x, :], B0[:, v * P:(v + 1) * P], scal(p, Q_NEG_EG, x),
                                                 vals[:, p, x, :], op0=ALU.mult, op1=ALU.add).then_inc(s_r, 1)
                elif name == "write":
                    dve.wait_ge(s_stp, n * 3 + i + 1)
                    for v in range(VH):
                        x = i * VH + v
                        new, got = S[:, i + 1, v * P:(v + 1) * P], B0[:, v * P:(v + 1) * P]
                        if i == 0:
                            dve.tensor_copy(new, got).then_inc(s_st, 1)
                        else:
                            dve.scalar_tensor_tensor(new, S[:, i, v * P:(v + 1) * P], scal(p, Q_EEND, x), got,
                                                     op0=ALU.mult, op1=ALU.add).then_inc(s_st, 1)
                elif name == "out":
                    for h in range(2):
                        dve.wait_ge(s_qsp, n * 2 + h + 1)
                        a = 2 if h == 0 else 0
                        dve.tensor_tensor(qs[:, 4 * h + a:4 * h + 4, :], bank4((B2, B3)[h])[:, a:4],
                                          scal(p, Q_EG, 4 * h + a, 4 - a).unsqueeze(2).broadcast_to([P, 4 - a, P]),
                                          ALU.mult).then_inc(s_qs, 1)
                elif name == "gated" and i == 0:
                    for h in range(2):
                        dve.wait_ge(s_pup, n * 2 + h + 1)
                        dve.wait_ge(s_qs, n * 2 + h + 1)
                        src = bank4((B0, B1)[h])
                        if h == 0:
                            dve.wait_ge(s_zq, n + 1)
                            dve.tensor_tensor(og[:, 0:2, :], src[:, 0:2], zs[:, p, 0, :].rearrange("p (v n) -> p v n", v=VH),
                                              ALU.mult).then_inc(s_o, 1)
                            dve.tensor_tensor(qs[:, 2:4, :], src[:, 2:4], qs[:, 2:4, :], ALU.add).then_inc(s_o, 1)
                            dve.wait_ge(s_o, n * 3 + 2)
                            dve.tensor_tensor(og[:, 2:4, :], qs[:, 2:4, :], zs[:, p, 1, :].rearrange("p (v n) -> p v n", v=VH),
                                              ALU.mult).then_inc(s_og, 1)
                        else:
                            dve.tensor_tensor(qs[:, 4:8, :], src, qs[:, 4:8, :], ALU.add).then_inc(s_o, 1)
                            dve.wait_ge(s_o, n * 3 + 3)
                            dve.tensor_tensor(og[:, 4:8, :], qs[:, 4:8, :],
                                              zs[:, p, 2:4, :].rearrange("p c (v n) -> p (c v) n", v=VH),
                                              ALU.mult).then_inc(s_og, 1)
                elif name == "gated" and i == 1:
                    for h in range(2):
                        dve.wait_ge(s_og2, n * 2 + h + 1)
                        dve.tensor_reduce(ms[:, 0, 4 * h:4 * h + 4], half(og2, h), AX, ALU.add).then_inc(s_ms, 1)
                    dve.wait_ge(s_ms, n * 3 + 2)
                    dve.tensor_scalar(ms[:, 1, :], ms[:, 0, :], 1.0 / P, 1e-6, ALU.mult, ALU.add).then_inc(s_ms, 1)
                elif name == "project":
                    dve.wait_ge(s_opp, n * 2 + i + 1)
                    a = acc[:, b * CH + 2 * i:b * CH + 2 * i + 2, :]
                    dve.tensor_tensor(a, (B0, B1)[i][:, :].rearrange("p (c n) -> p c n", c=2), a,
                                      ALU.add).then_inc(s_acc, 1)

            dve.wait_ge(s_zero, 1)
            for step in FRONT:
                run(step, 0, 0, 0)
            with dve.Fori(0, KH - 1) as kh:
                for step, n, b, head in body_steps(kh, False):
                    run(step, n, b, head)
            for step, n, b, head in body_steps(KH - 1, True):
                run(step, n, b, head)
            moe_vector(dve)


def kernel(**inputs):
    import ml_dtypes
    import numpy as np
    import concourse.bacc as bacc
    from concourse.bass_utils import run_bass_kernel_spmd

    def arr(name):
        return np.asarray(inputs["L0_" + name])

    x = arr("attn_hidden_states").reshape(TILES * P, D)
    w_qkv, w_z = arr("attn_w_qkv"), arr("attn_w_z")
    kdim = KH * P
    q, k = (w_qkv[:, i * kdim:(i + 1) * kdim].reshape(KT, P, KH, P) for i in range(2))
    v, z = (w.reshape(KT, P, KH, VH * P) for w in (w_qkv[:, 2 * kdim:], w_z))
    heads = np.concatenate([q, k, v, z], axis=3).transpose(2, 1, 0, 3).reshape(KH, P, -1)
    cw = arr("attn_conv_w")
    cq, ck = (cw[i * kdim:(i + 1) * kdim].reshape(KH, 1, P, TAPS) for i in range(2))
    cv = cw[2 * kdim:].reshape(KH, VH, P, TAPS)
    conv_w = np.concatenate([cq, ck, cv], axis=1).transpose(2, 0, 1, 3).reshape(P, KH, GROUPS * TAPS)
    i, j = np.arange(P)[:, None], np.arange(P)[None, :]
    eye = np.eye(P, dtype=np.float32)
    levels = [eye - ((j == i + 1) & (i % 2 == 0))]
    levels += [eye - ((i // (2 * s) == j // (2 * s)) & (i // s == j // s + 1)) for s in LEVELS]
    late = np.where(j < i, -30000.0, 0.0)
    gate, up = (np.concatenate([arr("ffn_w_" + n), arr("ffn_sw_" + n)[None]]) for n in ("gate", "up"))
    down = np.concatenate([arr("ffn_w_down"), arr("ffn_sw_down")[None]])
    arrays = {
        "x_rows": x,
        "x_cols": x.T,
        "w_heads": heads,
        "w_ab": np.concatenate([arr("attn_w_a"), arr("attn_w_b")], axis=1),
        "conv_w": conv_w,
        "dt_bias": np.broadcast_to(arr("attn_dt_bias"), (P, KH * VH)),
        "a_log": np.broadcast_to(arr("attn_A_log"), (P, KH * VH)),
        "gamma": arr("attn_norm_gamma").reshape(P, 1),
        "w_out": arr("attn_w_out").reshape(KH, VH, P, D).transpose(0, 2, 1, 3),
        "rms_w": arr("ffn_rms_weight").reshape(KT, P).T,
        "router_w": arr("ffn_router_w").reshape(KT, P, NE).transpose(1, 0, 2),
        "gate_up": np.concatenate([gate, up], axis=2).reshape(NX, KT, P, 2 * P).transpose(2, 0, 1, 3),
        "down": down.transpose(1, 0, 2),
        "tri": np.stack([i <= j, i > j, i == j, i == i + 0 * j], axis=1).astype(np.float32),
        "levels16": np.stack(levels, axis=1).astype(np.float16),
        "neg_mask": np.concatenate([late] * 4 + [eye], axis=1).astype(ml_dtypes.bfloat16),
        "ident16": eye.astype(np.float16),
        "iota8": np.broadcast_to(np.arange(NE, dtype=np.float32), (P, NE)),
        "exponents": np.broadcast_to(np.array([-0.5, 0.5], np.float32), (P, 2)),
    }
    nc = bacc.Bacc("TRN2", target_bir_lowering=False, num_devices=1)
    args, data = [], {}
    for name, a in arrays.items():
        data[name] = np.ascontiguousarray(a)
        args.append(nc.dram_tensor(name, a.shape, mybir.dt.from_np(a.dtype), kind="ExternalInput").ap())
    args.append(nc.dram_tensor("out", (TILES * P, D), F32, kind="ExternalOutput").ap())
    build_kernel(nc, *args)
    r = run_bass_kernel_spmd(nc, [data], core_ids=[0])
    return r.results[0]["out"].reshape(B, SEQ, D)
```

```python
from contextlib import ExitStack

import concourse.bass as bass
from concourse import mybir

F32 = mybir.dt.float32
F16 = mybir.dt.float16
BF16 = mybir.dt.bfloat16
F32R = mybir.dt.float32r
U32 = mybir.dt.uint32
ALU = mybir.AluOpType
ACT = mybir.ActivationFunctionType
AX = mybir.AxisListType.X

P = 128
B, SEQ, D = 4, 512, 256
CH = SEQ // P
KT = D // P
KH, VH = 16, 2
TILES = B * CH
CELLS = CH * VH
BODIES = KH * B
TAPS = 4
GROUPS = 4
LEVELS = [2, 4, 8, 16, 32, 64]
NE, TOPS = 8, 8
NX = NE + 1
NQ = 6
Q_G, Q_G_REST, Q_BETA, Q_EG, Q_KEYS, Q_EEND = range(NQ)

SCHEDULE = [
    ("F", "scalars", 0), ("finish", 0), ("F", "proj", 0), ("F", "proj", 1), ("finish", 1), ("F", "conv", 0),
    ("F", "proj", 2), ("F", "proj", 3), ("solve", 0), ("F", "conv", 1), ("F", "proj", 4), ("F", "conv", 2),
    ("F", "conv", 3), ("write", 0), ("F", "proj", 5), ("F", "proj", 6), ("F", "conv", 4), ("F", "conv", 5),
    ("F", "conv", 6), ("F", "silu", 0), ("read", 1), ("F", "proj", 7), ("solve", 1), ("F", "conv", 7),
    ("F", "conv", 8), ("F", "squares", 0), ("F", "conv", 9), ("write", 1), ("F", "decay", 0),
    ("F", "conv", 10), ("read", 2), ("F", "decay", 1), ("F", "conv", 11), ("F", "norms", 0), ("solve", 2),
    ("F", "keys", 0), ("F", "products", 0), ("write", 2), ("F", "silu", 1), ("recall", 1), ("recall", 2),
    ("recalled", 0), ("F", "products", 1), ("F", "system", 0), ("read", 3), ("recall", 3),
    ("F", "values", 0), ("F", "gate", 0), ("F", "pairs", 0), ("F", "system", 1), ("solve", 3), ("out", 0),
    ("F", "start", 0), ("F", "values", 1), ("out", 1), ("recalled", 1), ("F", "join", 0), ("F", "gate", 1),
    ("gated", 0), ("F", "join", 1), ("F", "grow", 0), ("out", 2), ("power", 0), ("out", 3),
    ("F", "join", 2), ("F", "grow", 1), ("gated", 1), ("F", "gate", 2), ("F", "grow", 2), ("F", "join", 3),
    ("power", 1), ("factor", 0), ("F", "join", 4), ("F", "grow", 3), ("F", "gate", 3), ("F", "join", 5),
    ("F", "grow", 4), ("F", "grow", 5), ("F", "join", 6), ("F", "join", 7), ("F", "scale", 0),
    ("F", "grow", 6), ("F", "grow", 7), ("F", "join", 8), ("turn", 0), ("F", "join", 9), ("F", "grow", 8),
    ("turn", 1), ("F", "grow", 9), ("F", "join", 10), ("project", 0), ("F", "grow", 10), ("F", "join", 11),
    ("project", 1), ("F", "newton", 0), ("F", "grow", 11), ("project", 2), ("F", "newton", 1),
    ("project", 3),
]


def build_kernel(nc, x_rows, x_cols, w_heads, w_ab, conv_w, dt_bias, a_log, gamma, w_out,
                 rms_w, router_w, gate_up, down, tri, levels16, neg_mask, ident16, iota8, exponents, out):
    ctx = ExitStack()
    with ctx:
        def sb(name, shape, dt=F32):
            return ctx.enter_context(nc.sbuf_tensor(name, shape, dt))

        def sem(name):
            return ctx.enter_context(nc.semaphore(name))

        bank = [ctx.enter_context(nc.psum_tensor(f"bank{i}", [P, 512], F32)) for i in range(8)]
        F0, F1, F2, F3, B0, B1, B2, B3 = bank
        FB = bank[:4]

        tri_sb = sb("tri_sb", [P, 4, P])
        upto, after, ident, ones = (tri_sb[:, i, :] for i in range(4))
        lev = sb("lev", [P, 1 + len(LEVELS), P], F16)
        negm = sb("negm", [P, 512], BF16)
        identb = sb("identb", [P, P], BF16)
        identh = sb("identh", [P, P], F16)
        iota_sb = sb("iota_sb", [P, NE])
        xT = sb("xT", [P, KT, TILES * P])
        wab = sb("wab", [P, KT, 64])
        vec32 = sb("vec32", [P, 2, 32])
        after_r = sb("after_r", [P, P], F32R)
        gam = sb("gam", [P, 1])
        cw_all = sb("cw_all", [P, KH, GROUPS * TAPS])
        sc_all = sb("sc_all", [P, BODIES, NQ * CELLS])
        acc = sb("acc", [P, TILES, D])
        rt_w = sb("rt_w", [P, KT, NE])
        rms_sb = sb("rms_sb", [P, KT])
        w_kh = sb("w_kh", [P, KT, 768])
        wo_raw = sb("wo_raw", [P, VH, D])
        wo = sb("wo", [P, VH, D])
        cw = sb("cw", [P, 2, GROUPS * TAPS])
        sc = sb("sc", [P, 2, NQ * CELLS])
        conv = sb("conv", [P, GROUPS, SEQ])
        zone = sb("zone", [P, 5, 2048])

        def zoned(i, pattern, **sizes):
            return zone[:, i, :].rearrange(pattern, **sizes)

        qkT = zoned(0, "p (x a n) -> p x a n", x=2, a=2)
        vT = sb("vT", [P, VH, SEQ])
        ssum = sb("ssum", [P, 2 * CH])
        zs = zoned(1, "p (x c n) -> p x c n", x=2, c=CH)
        ss = sb("ss", [P, 2 * CH])
        nk = sb("nk", [P, CH])
        rk2 = sb("rk2", [P, CH])
        rqs = sb("rqs", [P, CH])
        kfac = sb("kfac", [P, CELLS])
        keys = zoned(2, "p (x c n) -> p x c n", x=2, c=CELLS)
        vals = zoned(3, "p (x c n) -> p x c n", x=2, c=CELLS)
        gseg = sb("gseg", [P, 2, CELLS, P], F32R)
        dec = sb("dec", [P, CELLS, P])
        decb = sb("decb", [P, CELLS, P])
        m32T = sb("m32T", [P, CELLS, P])
        mhiT = sb("mhiT", [P, CELLS, P], F16)
        mloT = sb("mloT", [P, CELLS, P], F16)
        pT = zoned(4, "p (x c n) -> p x c n", x=2, c=CELLS)
        X = sb("X", [P, CELLS, P], F16)
        XT = sb("XT", [P, CELLS, P], F16)
        N = sb("N", [P, len(LEVELS), CELLS, P], F16)
        res = mloT
        TT = sb("TT", [P, 2, CELLS, P])
        rhs = sb("rhs", [P, CELLS, P])
        U = sb("U", [P, CELLS, P])
        S = sb("S", [P, CH, VH * P])
        qs = sb("qs", [P, CELLS, P])
        og = sb("og", [P, CELLS, P])
        og2 = sb("og2", [P, CELLS, P])
        ms = sb("ms", [P, 3, CELLS])
        expo = sb("expo", [P, 3])
        ogT = sb("ogT", [P, CELLS, P])

        s_const = sem("s_const")
        s_early = sem("s_early")
        s_xin = [sem(f"s_xin{b}") for b in range(B)]
        s_w = sem("s_w")
        s_wo = sem("s_wo")
        s_zero = sem("s_zero")
        s_abp = sem("s_abp")
        s_gates = sem("s_gates")
        s_gact = sem("s_gact")
        s_cum = sem("s_cum")
        s_scall = sem("s_scall")
        s_first = sem("s_first")
        s_sc = sem("s_sc")
        s_proj = sem("s_proj")
        s_tap = sem("s_tap")
        s_conv = sem("s_conv")
        s_silu = sem("s_silu")
        s_zp = sem("s_zp")
        s_zs = sem("s_zs")
        s_sq = sem("s_sq")
        s_ss = sem("s_ss")
        s_small = sem("s_small")
        s_kfac = sem("s_kfac")
        s_zq = sem("s_zq")
        s_ktp = sem("s_ktp")
        s_keys = sem("s_keys")
        s_vtp = sem("s_vtp")
        s_vals = sem("s_vals")
        s_kq = sem("s_kq")
        s_seg = sem("s_seg")
        s_decp = sem("s_decp")
        s_dec = sem("s_dec")
        s_decb = sem("s_decb")
        s_m = sem("s_m")
        s_p = sem("s_p")
        s_fill = sem("s_fill")
        s_mhi = sem("s_mhi")
        s_mlo = sem("s_mlo")
        s_pair = sem("s_pair")
        s_xp = sem("s_xp")
        s_x0 = sem("s_x0")
        s_np = sem("s_np")
        s_ident = sem("s_ident")
        s_n = sem("s_n")
        s_xp4 = sem("s_xp4")
        s_x = sem("s_x")
        s_xt0 = sem("s_xt0")
        s_resp = sem("s_resp")
        s_res = sem("s_res")
        s_newp = sem("s_newp")
        s_new = sem("s_new")
        s_ksp = sem("s_ksp")
        s_r = sem("s_r")
        s_up = sem("s_up")
        s_u = sem("s_u")
        s_stp = sem("s_stp")
        s_st = sem("s_st")
        s_qsp = sem("s_qsp")
        s_qs = sem("s_qs")
        s_pup = sem("s_pup")
        s_o = sem("s_o")
        s_og = sem("s_og")
        s_ms = sem("s_ms")
        s_mse = sem("s_mse")
        s_msl = sem("s_msl")
        s_on = sem("s_on")
        s_gtp = sem("s_gtp")
        s_gt = sem("s_gt")
        s_opp = sem("s_opp")
        s_acc = sem("s_acc")
        s_wog = sem("s_wog")
        s_mw = sem("s_mw")
        s_xg = sem("s_xg")
        s_x1 = sem("s_x1")
        s_ln1 = sem("s_ln1")
        s_sqx = sem("s_sqx")
        s_pw = sem("s_pw")
        s_pw2 = sem("s_pw2")
        s_h = sem("s_h")
        s_htp = sem("s_htp")
        s_ht = sem("s_ht")
        s_rtp = sem("s_rtp")
        s_rt = sem("s_rt")
        s_e2 = sem("s_e2")
        s_gup = sem("s_gup")
        s_sg = sem("s_sg")
        s_a = sem("s_a")
        s_dnp = sem("s_dnp")
        s_y = sem("s_y")
        s_ln2 = sem("s_ln2")
        s_out = sem("s_out")

        CONSTS = 10 * 16
        EARLY_LOADS = 4 * 16

        def body_steps(kh, last):
            for b in range(B):
                for step in SCHEDULE:
                    if step[0] == "F":
                        if not (last and b == B - 1):
                            yield step[1:], kh * B + b + 1, b + 1, kh + (b + 1) // B
                    else:
                        yield step, kh * B + b, b, kh
                        if last and b == B - 1:
                            for k in AFTER_STEP.get(step, ()):
                                yield ("prepare", k), 0, 0, 0

        def past_first(n):
            return not (isinstance(n, int) and n == 0)

        def before_last(n):
            return not (isinstance(n, int) and n == BODIES - 1)

        FRONT = [s[1:] for s in SCHEDULE if s[0] == "F"]

        def level_banks(i):
            return (FB[:2], FB[2:]) if i % 2 == 0 else (FB[2:], FB[:2])

        def half(t, h):
            return t[:, CELLS // 2 * h:CELLS // 2 * (h + 1)]

        def blocks(t, i, odd):
            s = LEVELS[i]
            return t.rearrange("p x (b two s) -> p x b two s", two=2, s=s)[:, :, :, odd]

        def packed(t, i):
            return t[:, 0:256].rearrange("p (x b s) -> p x b s", x=4, s=LEVELS[i])

        def bank4(t):
            return t[:, :].rearrange("p (x n) -> p x n", x=4)

        def scal(p, what, a, n=1):
            return sc[:, p, what * CELLS + a:what * CELLS + a + n]

        NG = BODIES * CELLS

        def gate_buffer(t, i):
            return t[:, :, :].rearrange("p a n -> p (a n)")[:, NG * i:NG * (i + 1)]

        a_in, b_in, al, a_abs = (gate_buffer(conv, i) for i in range(4))
        b_abs, gall = (gate_buffer(qs, i) for i in range(2))
        g_first = gseg[:, 0].rearrange("p a n -> p (a n)")[:, 0:NG]
        e_a, e_b = (gate_buffer(dec, i) for i in range(2))
        ln_a, e_al = (gate_buffer(decb, i) for i in range(2))
        b_den, b_num = (gate_buffer(m32T, i) for i in range(2))

        def by_body(t):
            return t.rearrange("p (n x) -> p n x", x=CELLS)

        def by_tile(t, tile):
            b, c = tile // CH, tile % CH
            return t.rearrange("p (h b x) -> p h b x", b=B, x=CELLS)[:, :, b, c * VH:(c + 1) * VH]

        def scalars_of(what):
            return sc_all[:, :, what * CELLS:(what + 1) * CELLS]

        def gates_vector(dve):
            for t in range(TILES):
                dve.wait_ge(s_abp, 8 * (t // 8 + 1))
                src = bank[t // 8][:, 64 * (t % 8):64 * (t % 8) + 64].rearrange("p (a h v) -> p a h v", a=2, v=VH)
                dve.tensor_tensor(by_tile(a_in, t), src[:, 0], vec32[:, 0, :].rearrange("p (h v) -> p h v", v=VH),
                                  ALU.add).then_inc(s_gates, 1)
                dve.tensor_copy(by_tile(b_in, t), src[:, 1]).then_inc(s_gates, 1)
            dve.tensor_copy(al.rearrange("p (h y v) -> p h y v", y=B * CH, v=VH),
                            vec32[:, 1, :].rearrange("p (h v) -> p h v", v=VH).unsqueeze(2)
                            .broadcast_to([P, KH, B * CH, VH])).then_inc(s_gates, 1)
            dve.wait_ge(s_gates, 2 * TILES + 1)
            dve.scalar_tensor_tensor(a_abs, a_in, -1.0, a_in, op0=ALU.mult, op1=ALU.max).then_inc(s_gates, 1)
            dve.scalar_tensor_tensor(b_abs, b_in, -1.0, b_in, op0=ALU.mult, op1=ALU.max).then_inc(s_gates, 1)
            dve.wait_ge(s_gact, 3)
            dve.tensor_scalar(e_a, e_a, 1.0, None, ALU.add).then_inc(s_gates, 1)
            dve.tensor_scalar(b_den, e_b, 1.0, None, ALU.add).then_inc(s_gates, 1)
            dve.scalar_tensor_tensor(b_num, b_in, 0.0, e_b, op0=ALU.is_ge, op1=ALU.max).then_inc(s_gates, 1)
            dve.wait_ge(s_gates, 2 * TILES + 6)
            dve.reciprocal(b_den, b_den).then_inc(s_gates, 1)
            dve.wait_ge(s_gates, 2 * TILES + 7)
            dve.tensor_tensor(scalars_of(Q_BETA), by_body(b_num), by_body(b_den), ALU.mult).then_inc(s_gates, 1)
            dve.wait_ge(s_gact, 4)
            dve.scalar_tensor_tensor(ln_a, a_in, 0.0, ln_a, op0=ALU.max, op1=ALU.add).then_inc(s_gates, 1)
            dve.wait_ge(s_gates, 2 * TILES + 9)
            dve.scalar_tensor_tensor(gall, e_al, -1.0, ln_a, op0=ALU.mult, op1=ALU.mult).then_inc(s_gates, 1)
            dve.wait_ge(s_gates, GATES)
            dve.tensor_copy(g_first, gall).then_inc(s_first, 1)
            dve.tensor_copy(after_r[:, :], after).then_inc(s_first, 1)
            dve.wait_ge(s_first, 2)
            dve.tensor_copy(scalars_of(Q_G), by_body(g_first.bitcast(F32))).then_inc(s_scall, 1)
            dve.tensor_tensor(scalars_of(Q_G_REST), by_body(gall), by_body(g_first.bitcast(F32)), ALU.subtract).then_inc(s_scall, 1)
            dve.wait_ge(s_gact, 6)
            dve.tensor_tensor(scalars_of(Q_KEYS), scalars_of(Q_KEYS), scalars_of(Q_BETA), ALU.mult).then_inc(s_scall, 1)

        GATES = 2 * TILES + 10
        GACT = 7

        def gates_scalar(act):
            act.wait_ge(s_gates, 2 * TILES + 3)
            act.activation(e_a, a_abs, ACT.Exp, scale=-1.0).then_inc(s_gact, 1)
            act.activation(e_b, b_abs, ACT.Exp, scale=-1.0).then_inc(s_gact, 1)
            act.activation(e_al, al, ACT.Exp).then_inc(s_gact, 1)
            act.wait_ge(s_gates, 2 * TILES + 4)
            act.activation(ln_a, e_a, ACT.Ln).then_inc(s_gact, 1)
            for i, what in enumerate((Q_EG, Q_KEYS, Q_EEND)):
                act.wait_ge(s_cum, i + 1)
                act.activation(scalars_of(what), bank[2 + i][:, :].rearrange("p (n x) -> p n x", x=CELLS),
                               ACT.Exp).then_inc(s_gact, 1)

        def flat(t):
            return t[:, :, :].rearrange("p a n -> p (a n)")

        gu_routed = flat(xT).rearrange("p (e k n) -> p e k n", e=NE, k=KT)
        dn_routed = flat(conv).rearrange("p (e n) -> p e n", e=NE)
        gu_shared = flat(w_kh)[:, 0:KT * 2 * P].rearrange("p (e k n) -> p e k n", e=1, k=KT)
        dn_shared = flat(w_kh)[:, KT * 2 * P:KT * 2 * P + D].rearrange("p (e n) -> p e n", e=1)

        def gate_up_of(e):
            return gu_routed[:, e] if e < NE else gu_shared[:, 0]

        def down_of(e):
            return dn_routed[:, e] if e < NE else dn_shared[:, 0]

        def wide(t, n=D):
            return flat(t).rearrange("p (c n) -> p c n", n=n)

        xg = zone[:, 0, 0:CH * D].rearrange("p (c n) -> p c n", n=D)
        x1 = [wide(t) for t in (dec, decb)]
        hrow = wide(m32T)
        sqx = wide(og2)
        hT = [wide(t, SEQ) for t in (vT, rhs)]
        sg = wide(TT[:, 0], SEQ)[:, 0:2]
        aT = wide(U, SEQ)[:, 0:2]
        y = wide(qs)
        outrow = wide(og)
        bn = sb("bn", [P, 2, CH, 6])
        mv = sb("mv", [P, 2, CH, 2])
        st1 = sb("st1", [P, 2, 2, CH])
        rs = sb("rs", [P, 3, CH])
        lg = sb("lg", [P, CH, NE])
        top = sb("top", [P, CH, TOPS])
        ti = sb("ti", [P, CH, TOPS], U32)
        tif = sb("tif", [P, CH, TOPS])
        tw = sb("tw", [P, 4, CH])
        pick = sb("pick", [P, 2, CH, NE])
        wd = sb("wd", [P, 2, CH, NE])

        NORM = 3 * CH + 1
        RT = 2 * CH + 10

        AFTER_EXPERT = {
            "vector": {1: (0,), 2: (2,), 3: (4,), 4: (6,), 6: (8,), 7: (10,)},
            "scalar": {2: (3,), 5: (7,)},
            "tensor": {5: (7,), 6: (8,)},
        }
        AFTER_STEP = {("solve", 0): (0, 1), ("write", 0): (2, 3), ("solve", 1): (4, 5), ("write", 1): (6,),
                      ("read", 2): (7,), ("write", 2): (8, 9), ("out", 3): (10,), ("gated", 1): (12,)}

        def moe_loads(sp):
            sp.wait_ge(s_qsp, 2 * (BODIES - 1))
            sp.wait_ge(s_ksp, 3 * (BODIES - 1))
            sp.dma_start(xg, x_rows[0:SEQ, :].rearrange("(c p) n -> p c n", p=P)).then_inc(s_xg, 16)
            sp.wait_ge(s_silu, 4 * BODIES)
            sp.wait_ge(s_zp, 2 * BODIES)
            sp.dma_start(gu_routed, gate_up[:, 0:NE]).then_inc(s_mw, 16)
            sp.dma_start(dn_routed, down[:, 0:NE]).then_inc(s_mw, 16)
            sp.dma_start(gu_shared, gate_up[:, NE:NX]).then_inc(s_mw, 16)
            sp.dma_start(dn_shared, down[:, NE:NX]).then_inc(s_mw, 16)

            def rows(g):
                sp.wait_ge(s_ln1, g * NORM)
                sp.dma_start(xg, x_rows[SEQ * g:SEQ * (g + 1), :].rearrange("(c p) n -> p c n", p=P)).then_inc(s_xg, 16)

            rows(1)
            for g in range(B):
                if g + 2 < B:
                    rows(g + 2)
                sp.wait_ge(s_ln2, (g + 1) * NORM)
                sp.dma_start(out[SEQ * g:SEQ * (g + 1), :].rearrange("(c p) n -> p c n", p=P), outrow).then_inc(s_out, 16)
            sp.wait_ge(s_out, 16 * B)

        def prepare_pool(pool, k, g):
            if k == 1:
                pool.wait_ge(s_ln1, g * NORM + 2 * CH + 1)
                pool.tensor_tensor(st1[:, 0, 1, :], st1[:, 0, 0, :], expo[:, 0:1].broadcast_to([P, CH]), ALU.pow).then_inc(s_pw, 1)
            elif k == 5:
                pool.wait_ge(s_h, g * (CH + 1) + 1)
                pool.tensor_tensor(rs[:, 2, :], rs[:, 1, :], expo[:, 0:1].broadcast_to([P, CH]), ALU.pow).then_inc(s_pw, 1)
            elif k == 9:
                pool.wait_ge(s_e2, g + 1)
                pool.tensor_tensor(tw[:, 1, :], expo[:, 2:3].broadcast_to([P, CH]), tw[:, 0, :], ALU.pow).then_inc(s_pw, 1)

        def moe_pool(pool):
            for g in range(B):
                if g + 1 < B:
                    for k in range(11):
                        prepare_pool(pool, k, g + 1)
                pool.wait_ge(s_ln2, g * NORM + 2 * CH + 1)
                pool.tensor_tensor(st1[:, 1, 1, :], st1[:, 1, 0, :], expo[:, 0:1].broadcast_to([P, CH]), ALU.pow).then_inc(s_pw2, 1)

        def into(pe, g, e):
            i = g * NX + e
            for a, dst in enumerate(((F2, F3), (B0, B1))[i % 2]):
                if i > 1:
                    pe.wait_ge(s_a, i - 1)
                for k in range(KT):
                    mm = pe.matmul(dst[:, :], gate_up_of(e)[:, k, a * P:(a + 1) * P], hT[g % 2][:, k, :],
                                   start=(k == 0), stop=(k == KT - 1))
                mm.then_inc(s_gup, 1)

        def prepare_tensor(pe, k, g):
            if k == 7:
                if g > 0:
                    pe.wait_ge(s_rt, (g - 1) * RT + 1)
                for c in range(CH):
                    pe.wait_ge(s_h, g * (CH + 1) + 1 + c + 1)
                    for t in range(KT):
                        mm = pe.transpose((F0, F1)[t][:, c * P:(c + 1) * P], hrow[:, c, t * P:(t + 1) * P], ident)
                mm.then_inc(s_htp, 1)
            elif k == 8:
                pe.wait_ge(s_ht, 2 * g + 2)
                for c in range(CH):
                    for t in range(KT):
                        mm = pe.matmul(F0[:, c * NE:(c + 1) * NE], hT[g % 2][:, t, c * P:(c + 1) * P], rt_w[:, t, :],
                                       start=(t == 0), stop=(t == KT - 1))
                mm.then_inc(s_rtp, 1)
            elif k == 12:
                pe.wait_ge(s_mw, 64)
                into(pe, g, 0)

        def moe_tensor(pe):
            pe.wait_ge(s_acc, 2 * BODIES)

            def outof(i):
                pe.wait_ge(s_a, i + 1)
                for h, dst in enumerate((B2, B3)):
                    if i > 0:
                        pe.wait_ge(s_y, (i - 1) * CH + 2 * h + 2)
                    for c in range(2):
                        mm = pe.matmul(dst[:, 256 * c:256 * c + 256], aT[:, i % 2, (2 * h + c) * P:(2 * h + c + 1) * P],
                                       down_of(i % NX), start=True, stop=True)
                    mm.then_inc(s_dnp, 1)

            for g in range(B):
                for e in range(NX):
                    if g + e > 0:
                        into(pe, g, e)
                    if g * NX + e > 0:
                        outof(g * NX + e - 1)
                    if g + 1 < B:
                        for k in AFTER_EXPERT["tensor"].get(e, ()):
                            prepare_tensor(pe, k, g + 1)
            outof(B * NX - 1)

        def prepare_scalar(act, k, g):
            if k == 3:
                act.wait_ge(s_ln1, (g + 1) * NORM)
                for c in range(CH):
                    act.activation(sqx[:, c, :], x1[g % 2][:, c, :], ACT.Square, accum_out=rs[:, 0, c:c + 1]).then_inc(s_sqx, 1)
            elif k == 7:
                act.wait_ge(s_htp, g + 1)
                for t in range(KT):
                    act.activation(hT[g % 2][:, t, :], (F0, F1)[t][:, :], ACT.Copy, scale=rms_sb[:, t:t + 1]).then_inc(s_ht, 1)

        def moe_scalar(act):
            for g in range(B):
                for e in range(NX):
                    i = g * NX + e
                    act.wait_ge(s_gup, 2 * i + 1)
                    if i > 1:
                        act.wait_ge(s_a, i - 1)
                    act.activation(sg[:, i % 2], (F2, B0)[i % 2][:, :], ACT.Silu).then_inc(s_sg, 1)
                    if g + 1 < B:
                        for k in AFTER_EXPERT["scalar"].get(e, ()):
                            prepare_scalar(act, k, g + 1)

        def norm_stats(dve, norm, src, s, base):
            for c in range(CH):
                dve.bn_stats(bn[:, norm, c, :], src[:, c, :]).then_inc(s, 1)
            for c in range(CH):
                dve.wait_ge(s, base + c + 1)
                dve.bn_aggr(mv[:, norm, c, :], bn[:, norm, c, :]).then_inc(s, 1)
            dve.wait_ge(s, base + 2 * CH)
            dve.tensor_scalar(st1[:, norm, 0, :], mv[:, norm, :, 1], 1e-5, None, ALU.add).then_inc(s, 1)

        def normalise(dve, norm, dst, src, s):
            for c in range(CH):
                dve.tensor_scalar(dst[:, c, :], src[:, c, :], mv[:, norm, c, 0:1], st1[:, norm, 1, c:c + 1],
                                  ALU.subtract, ALU.mult).then_inc(s, 1)

        def prepare_vector(dve, k, g):
            if k == 0:
                if g == 0:
                    dve.wait_ge(s_mlo, BODIES)
                dve.wait_ge(s_xg, 16 * (g + 1))
                dve.tensor_tensor(xg, xg, acc[:, g * CH:(g + 1) * CH, :], ALU.add).then_inc(s_x1, 1)
                dve.wait_ge(s_x1, g + 1)
                norm_stats(dve, 0, xg, s_ln1, g * NORM)
            elif k == 2:
                dve.wait_ge(s_pw, 3 * g + 1)
                normalise(dve, 0, x1[g % 2], xg, s_ln1)
            elif k == 4:
                dve.wait_ge(s_sqx, (g + 1) * CH)
                dve.tensor_scalar(rs[:, 1, :], rs[:, 0, :], 1.0 / D, 1e-6, ALU.mult, ALU.add).then_inc(s_h, 1)
            elif k == 6:
                dve.wait_ge(s_pw, 3 * g + 2)
                if g > 0:
                    dve.wait_ge(s_htp, g)
                for c in range(CH):
                    dve.tensor_scalar(hrow[:, c, :], x1[g % 2][:, c, :], rs[:, 2, c:c + 1], None, ALU.mult).then_inc(s_h, 1)
            elif k == 8:
                dve.wait_ge(s_rtp, g + 1)
                r = g * RT
                dve.tensor_copy(lg[:, :, :], F0[:, 0:CH * NE].rearrange("p (c e) -> p c e", e=NE)).then_inc(s_rt, 1)
                dve.wait_ge(s_rt, r + 1)
                for c in range(CH):
                    dve.max(top[:, c, :], lg[:, c, :]).then_inc(s_rt, 1)
                for c in range(CH):
                    dve.wait_ge(s_rt, r + 2 + c)
                    dve.max_index(ti[:, c, :], top[:, c, :], lg[:, c, :]).then_inc(s_rt, 1)
                dve.tensor_tensor(tw[:, 0, :], top[:, :, 1], top[:, :, 0], ALU.subtract).then_inc(s_e2, 1)
                dve.wait_ge(s_rt, r + 1 + 2 * CH)
                dve.tensor_copy(tif[:, :, :], ti[:, :, :]).then_inc(s_rt, 1)
            elif k == 10:
                r = g * RT
                dve.wait_ge(s_pw, 3 * g + 3)
                dve.tensor_scalar(tw[:, 2, :], tw[:, 1, :], 1.0, None, ALU.add).then_inc(s_rt, 1)
                dve.wait_ge(s_rt, r + 3 + 2 * CH)
                dve.reciprocal(tw[:, 2, :], tw[:, 2, :]).then_inc(s_rt, 1)
                dve.wait_ge(s_rt, r + 4 + 2 * CH)
                dve.tensor_tensor(tw[:, 3, :], tw[:, 1, :], tw[:, 2, :], ALU.mult).then_inc(s_rt, 1)
                for j in range(2):
                    dve.tensor_tensor(pick[:, j], iota_sb[:, :].unsqueeze(1).broadcast_to([P, CH, NE]),
                                      tif[:, :, j:j + 1].broadcast_to([P, CH, NE]), ALU.is_equal).then_inc(s_rt, 1)
                dve.wait_ge(s_rt, r + 7 + 2 * CH)
                for j in range(2):
                    dve.tensor_tensor(pick[:, j], pick[:, j], tw[:, 2 + j, :].unsqueeze(2).broadcast_to([P, CH, NE]),
                                      ALU.mult).then_inc(s_rt, 1)
                dve.wait_ge(s_rt, r + 9 + 2 * CH)
                dve.tensor_tensor(wd[:, g % 2], pick[:, 0], pick[:, 1], ALU.add).then_inc(s_rt, 1)

        def moe_vector(dve):
            def gated(i):
                dve.wait_ge(s_sg, i + 1)
                dve.wait_ge(s_gup, 2 * i + 2)
                if i > 1:
                    dve.wait_ge(s_dnp, 2 * (i - 1))
                dve.tensor_tensor(aT[:, i % 2], sg[:, i % 2], (F3, B1)[i % 2][:, :], ALU.mult).then_inc(s_a, 1)

            def added(i):
                g, e = divmod(i, NX)
                if e == 0:
                    dve.wait_ge(s_rt, (g + 1) * RT)
                    if g > 0:
                        dve.wait_ge(s_ln2, g * NORM)
                for c in range(CH):
                    dve.wait_ge(s_dnp, 2 * i + c // 2 + 1)
                    if e > 0:
                        dve.wait_ge(s_y, (i - 1) * CH + c + 1)
                    src = (B2, B3)[c // 2][:, 256 * (c % 2):256 * (c % 2) + 256]
                    dve.scalar_tensor_tensor(y[:, c, :], src, wd[:, g % 2, c, e:e + 1] if e < NE else 1.0,
                                             (y if e else x1[g % 2])[:, c, :], op0=ALU.mult, op1=ALU.add).then_inc(s_y, 1)

            def last_norm(g):
                dve.wait_ge(s_pw2, g + 1)
                if g > 0:
                    dve.wait_ge(s_out, 16 * g)
                normalise(dve, 1, outrow, y, s_ln2)

            for g in range(B):
                for e in range(NX):
                    i = g * NX + e
                    gated(i)
                    if e == 1 and g > 0:
                        last_norm(g - 1)
                    if e > 0:
                        added(i - 1)
                    elif g > 0:
                        added(i - 1)
                        dve.wait_ge(s_y, g * NX * CH)
                        norm_stats(dve, 1, y, s_ln2, (g - 1) * NORM)
                    if g + 1 < B:
                        for k in AFTER_EXPERT["vector"].get(e, ()):
                            prepare_vector(dve, k, g + 1)
            added(B * NX - 1)
            dve.wait_ge(s_y, B * NX * CH)
            norm_stats(dve, 1, y, s_ln2, (B - 1) * NORM)
            last_norm(B - 1)

        block = ctx.enter_context(nc.Block())

        @block.sync
        def _(sp):
            for dst, src in (
                (wab[:, :, :], w_ab.rearrange("(t p) n -> p t n", p=P)), (vec32[:, 0, :], dt_bias), (vec32[:, 1, :], a_log),
                (tri_sb[:, :, :], tri),
            ):
                sp.dma_start(dst, src).then_inc(s_early, 16)
            for b in range(B):
                sp.dma_start(xT[:, :, SEQ * b:SEQ * (b + 1)],
                             x_cols[:, SEQ * b:SEQ * (b + 1)].rearrange("(t p) n -> p t n", p=P)).then_inc(s_xin[b], 16)
            for dst, src in (
                (negm[:, :], neg_mask[:, 0:512]), (identb[:, :], neg_mask[:, 512:640]),
                (lev[:, :, :], levels16), (identh[:, :], ident16), (iota_sb[:, :], iota8),
                (gam[:, :], gamma), (expo[:, :], exponents), (rt_w[:, :, :], router_w), (rms_sb[:, :], rms_w),
                (cw_all[:, :, :], conv_w),
            ):
                sp.dma_start(dst, src).then_inc(s_const, 16)
            sp.dma_start(w_kh[:, :, :], w_heads[0].rearrange("p (t n) -> p t n", t=KT)).then_inc(s_w, 16)
            sp.dma_start(wo_raw[:, :, :], w_out[0]).then_inc(s_wo, 16)

            def weights(kh):
                sp.wait_ge(s_zp, (kh * B + B) * 2)
                sp.dma_start(w_kh[:, :, :], w_heads[bass.ds(kh + 1, 1)].rearrange("o p (t n) -> (o p) t n", t=KT)).then_inc(s_w, 16)
                sp.wait_ge(s_wog, kh + 1)
                sp.dma_start(wo_raw[:, :, :], w_out[bass.ds(kh + 1, 1)].rearrange("o p v n -> (o p) v n")).then_inc(s_wo, 16)

            sp.wait_ge(s_const, CONSTS)
            with sp.Fori(0, KH - 1) as kh:
                weights(kh)
            moe_loads(sp)

        @block.gpsimd
        def _(pool):
            pool.memset(acc[:, :, :], 0.0).then_inc(s_zero, 1)
            pool.wait_ge(s_early, EARLY_LOADS)
            pool.wait_ge(s_const, CONSTS)

            def fill_n():
                for i in range(len(LEVELS)):
                    pool.tensor_copy(N[:, i], identh[:, :].unsqueeze(1).broadcast_to([P, CELLS, P])).then_inc(s_ident, 1)

            def scale_wo(kh):
                pool.wait_ge(s_wo, 16 * (kh + 1))
                pool.tensor_tensor(wo[:, :, :], wo_raw[:, :, :], gam[:, 0:1].unsqueeze(2).broadcast_to([P, VH, D]), ALU.mult).then_inc(s_wog, 1)

            def run(step, n, b, head):
                p = b % 2
                if step[0] == "prepare":
                    prepare_pool(pool, step[1], 0)
                elif step == ("scalars", 0):
                    pool.wait_ge(s_sc, n * 2 + 2)
                    if past_first(n):
                        pool.wait_ge(s_decp, n * 2)
                    for part, what in enumerate((Q_G, Q_G_REST)):
                        pool.tensor_tensor(gseg[:, part], upto.unsqueeze(1).broadcast_to([P, CELLS, P]),
                                           scal(p, what, 0, CELLS).unsqueeze(2).broadcast_to([P, CELLS, P]),
                                           ALU.mult).then_inc(s_seg, 1)
                elif step[0] == "decay":
                    h = step[1]
                    pool.wait_ge(s_dec, n * 2 + h + 1)
                    if h == 0 and past_first(n):
                        pool.wait_ge(s_p, n * 2)
                    pool.tensor_tensor(half(decb, h), half(dec, h),
                                       scal(p, Q_BETA, 4 * h, 4).unsqueeze(2).broadcast_to([P, 4, P]), ALU.mult).then_inc(s_decb, 1)
                elif step == ("norms", 0):
                    pool.wait_ge(s_ss, n * 3 + 3)
                    pool.tensor_tensor(nk[:, :], ss[:, CH:], expo[:, 1:2].broadcast_to([P, CH]), ALU.pow).then_inc(s_small, 1)
                    pool.tensor_tensor(rqs[:, :], ss[:, 0:CH], expo[:, 0:1].broadcast_to([P, CH]), ALU.pow).then_inc(s_small, 1)
                elif step == ("scale", 0):
                    pool.wait_ge(s_zs, n * 2 + 2)
                    pool.wait_ge(s_small, n * 2 + 2)
                    pool.tensor_tensor(zs[:, p, :, :], zs[:, p, :, :],
                                       rqs[:, :].unsqueeze(2).broadcast_to([P, CH, VH * P]), ALU.mult).then_inc(s_zq, 1)
                elif step == ("system", 0):
                    for h in range(2):
                        pool.wait_ge(s_const, CONSTS)
                        pool.wait_ge(s_m, n * 2 + h + 1)
                        pool.affine_select(out=half(mhiT, h), in_=half(m32T, h), compare_op=ALU.not_equal, fill=1.0,
                                           base=0, pattern=[[0, 4], [-1, P]], channel_multiplier=1).then_inc(s_mhi, 1)
                    for h in range(2):
                        pool.wait_ge(s_const, CONSTS)
                        pool.wait_ge(s_mhi, n * 2 + h + 1)
                        pool.affine_select(out=half(m32T, h), in_=half(m32T, h), compare_op=ALU.not_equal, fill=1.0,
                                           base=0, pattern=[[0, 4], [-1, P]], channel_multiplier=1).then_inc(s_fill, 1)
                    pool.wait_ge(s_fill, n * 2 + 2)
                    pool.tensor_tensor(mloT[:, :, :], m32T[:, :, :], mhiT[:, :, :], ALU.subtract).then_inc(s_mlo, 1)
                elif step == ("factor", 0):
                    pool.wait_ge(s_mse, n + 1)
                    pool.tensor_tensor(ms[:, 2, :], ms[:, 1, :], expo[:, 0:1].broadcast_to([P, CELLS]),
                                       ALU.pow).then_inc(s_msl, 1)
                    for h in range(2):
                        pool.wait_ge(s_msl, n + 1)
                        pool.tensor_tensor(half(og, h), half(og, h),
                                           ms[:, 2, 4 * h:4 * h + 4].unsqueeze(2).broadcast_to([P, 4, P]),
                                           ALU.mult).then_inc(s_on, 1)

            fill_n()
            for step in FRONT:
                run(step, 0, 0, 0)

            def key_head(kh, last):
                for step, n, b, head in body_steps(kh, last):
                    run(step, n, b, head)
                    if step == ("project", 3) and b == B - 1 and not last:
                        pool.wait_ge(s_opp, (kh * B + B) * 2)
                        scale_wo(kh + 1)

            scale_wo(0)
            with pool.Fori(0, KH - 1) as kh:
                key_head(kh, False)
            key_head(KH - 1, True)
            moe_pool(pool)

        @block.tensor
        def _(pe):
            pe.wait_ge(s_early, EARLY_LOADS)
            for t in range(TILES):
                if t % CH == 0:
                    pe.wait_ge(s_xin[t // CH], 16)
                for k in range(KT):
                    mm = pe.matmul(bank[t // 8][:, 64 * (t % 8):64 * (t % 8) + 64], xT[:, k, t * P:(t + 1) * P],
                                   wab[:, k, :], start=(k == 0), stop=(k == KT - 1))
                mm.then_inc(s_abp, 1)
            pe.wait_ge(s_gates, GATES)
            for i, m in enumerate((upto, after, ones)):
                pe.matmul(bank[2 + i][:, :], m, gall, start=True, stop=True).then_inc(s_cum, 1)
            pe.wait_ge(s_gact, GACT)
            pe.wait_ge(s_const, CONSTS)

            def run(step, n, b, head):
                p = b % 2
                later = past_first(n)
                name, i = step
                if name == "prepare":
                    prepare_tensor(pe, i, 0)
                elif name == "proj":
                    g, k = divmod(i, KT)
                    if i == 0 and b % B == 0:
                        pe.wait_ge(s_w, 16 * (head + 1))
                    if later and g < 2 and k == 0:
                        pe.wait_ge(s_res, (n - 1) * 2 + g + 1)
                    if later and g >= 2 and k == 0:
                        pe.wait_ge(s_new, (n - 1) * 2 + g - 1)
                    mm = pe.matmul(FB[g][:, :], w_kh[:, k, g * P:(g + 1) * P], xT[:, k, bass.ts(b % B, SEQ)],
                                   start=(k == 0), stop=(k == KT - 1))
                    if k == KT - 1:
                        mm.then_inc(s_proj, 1)
                elif name == "decay":
                    dst = (B2, B3)[i]
                    if i == 0:
                        pe.wait_ge(s_seg, n * 2 + 2)
                    pe.matmul(dst[:, :], identb[:, :], negm[:, :], start=True, stop=False, skip_group_check=True)
                    for part in range(2):
                        mm = pe.matmul(dst[:, :], after_r[:, :], gseg[:, part, 4 * i:4 * i + 4, :], start=False,
                                       stop=(part == 1), skip_group_check=True)
                    mm.then_inc(s_decp, 1)
                elif name == "gate":
                    h, c = divmod(i, 2)
                    if c == 0:
                        if later:
                            pe.wait_ge(s_qs, (n - 1) * 2 + h + 1)
                        else:
                            pe.wait_ge(s_dec, h + 1)
                    t = (b % B) * CH + i
                    for k in range(KT):
                        mm = pe.matmul((B2, B3)[h][:, 256 * c:256 * c + 256], xT[:, k, t * P:(t + 1) * P], w_kh[:, k, 512:768],
                                       start=(k == 0), stop=(k == KT - 1))
                    if c == 1:
                        mm.then_inc(s_zp, 1)
                elif name == "squares":
                    pe.wait_ge(s_silu, n * 4 + 2)
                    for a, dst in ((1, F1), (0, F0)):
                        for c in range(CH):
                            mm = pe.transpose(dst[:, c * P:(c + 1) * P], qkT[:, p, a, c * P:(c + 1) * P], ident)
                        mm.then_inc(s_ktp, 1)
                elif name == "values":
                    if i == 0:
                        pe.wait_ge(s_silu, n * 4 + 4)
                    for c in range(2):
                        for v in range(VH):
                            o = (c * VH + v) * P
                            t = (2 * i + c) * P
                            mm = pe.transpose(FB[2 + i][:, o:o + P], vT[:, v, t:t + P], ident)
                    mm.then_inc(s_vtp, 1)
                elif name == "products":
                    if i == 0:
                        pe.wait_ge(s_sq, (n + 1) * 2 * CH)
                    else:
                        pe.wait_ge(s_keys, n + 1)
                    a, dst = ((1, F0), (0, F1))[i]
                    for c in range(CH):
                        mm = pe.matmul(dst[:, c * P:(c + 1) * P], qkT[:, p, 1, c * P:(c + 1) * P],
                                       qkT[:, p, a, c * P:(c + 1) * P], start=True, stop=True)
                    mm.then_inc(s_kq, 1)
                elif name == "start":
                    pe.wait_ge(s_pair, n * 2 + 2)
                    f0h = F0[:, :].bitcast(F16)
                    for x in range(CELLS):
                        mm = pe.transpose(f0h[:, x * P:(x + 1) * P], XT[:, x, :], identh[:, :])
                    mm.then_inc(s_xp, 1)
                elif name == "join":
                    i, h = divmod(i, 2)
                    if i == 0:
                        if h == 0:
                            pe.wait_ge(s_x0, n + 1)
                            pe.wait_ge(s_p, n * 2 + 2)
                    else:
                        pe.wait_ge(s_x, n * 18 + 3 * (i - 1) + h + 1)
                    for x in range(4):
                        mm = pe.matmul(level_banks(i)[0][h][:, x * 64:(x + 1) * 64], mhiT[:, 4 * h + x, :],
                                       blocks(X[:, 4 * h + x:4 * h + x + 1, :], i, 0), start=True, stop=True)
                    mm.then_inc(s_np, 1)
                elif name == "grow":
                    i, h = divmod(i, 2)
                    mxb, xb = level_banks(i)
                    if i == 0:
                        if h == 0:
                            pe.wait_ge(s_vals, n * CH + CH)
                    elif h == 0:
                        pe.wait_ge(s_xt0, n * 6 + i)
                    else:
                        pe.wait_ge(s_x, n * 18 + 3 * i)
                    pe.wait_ge(s_n, n * 12 + 2 * i + h + 1)
                    for x in range(4):
                        c = 4 * h + x
                        mm = pe.matmul(xb[h][:, x * 64:(x + 1) * 64], XT[:, c, :], blocks(N[:, i, c:c + 1, :], i, 0),
                                       start=True, stop=True)
                    mm.then_inc(s_xp4, 1)
                    for x in range(4):
                        c = 4 * h + x
                        mm = pe.matmul(mxb[h][:, x * 64:(x + 1) * 64], N[:, i, c, :], blocks(XT[:, c:c + 1, :], i, 1),
                                       start=True, stop=True)
                    mm.then_inc(s_xp4, 1)
                elif name == "newton":
                    h = i
                    pe.wait_ge(s_x, n * 18 + 15 + h + 1)
                    if h == 0:
                        pe.wait_ge(s_mlo, n + 1)
                    for x in range(4):
                        c = 4 * h + x
                        pe.matmul(FB[h][:, x * P:(x + 1) * P], mhiT[:, c, :], X[:, c, :], start=True, stop=False)
                        mm = pe.matmul(FB[h][:, x * P:(x + 1) * P], mloT[:, c, :], X[:, c, :], start=False, stop=True)
                    mm.then_inc(s_resp, 1)
                elif name == "finish":
                    h = i
                    if h == 0:
                        pe.wait_ge(s_xt0, n * 6 + 6)
                    else:
                        pe.wait_ge(s_x, n * 18 + 18)
                    pe.wait_ge(s_res, n * 2 + h + 1)
                    for x in range(4):
                        c = 4 * h + x
                        mm = pe.matmul(FB[2 + h][:, x * P:(x + 1) * P], res[:, c, :], XT[:, c, :], start=True, stop=True)
                    mm.then_inc(s_newp, 1)
                elif name == "read":
                    pe.wait_ge(s_st, n * 6 + 2 * i)
                    pe.matmul(B0[:, 0:256], qkT[:, p, 1, i * P:(i + 1) * P], S[:, i, :], start=True, stop=True).then_inc(s_ksp, 1)
                elif name == "recall":
                    c = i
                    if before_last(n) and c < 3:
                        pe.wait_ge(s_dec, (n + 1) * 2 + c)
                    pe.wait_ge(s_st, n * 6 + 2 * c)
                    mm = pe.matmul((B2, B2, B3, B3)[c][:, 256 * (c % 2):256 * (c % 2) + 256], qkT[:, p, 0, c * P:(c + 1) * P],
                                   S[:, c, :], start=True, stop=True)
                    if c % 2:
                        mm.then_inc(s_qsp, 1)
                elif name == "solve":
                    c = i
                    if c == 0:
                        pe.wait_ge(s_new, n * 2 + 2)
                        pe.wait_ge(s_acc, n * 2)
                    for v in range(VH):
                        x = c * VH + v
                        if c > 0:
                            pe.wait_ge(s_r, n * 6 + 2 * c - 2 + v + 1)
                        mm = pe.matmul(B1[:, v * P:(v + 1) * P], TT[:, p, x, :], rhs[:, x, :] if c else vals[:, p, x, :],
                                       start=True, stop=True)
                    mm.then_inc(s_up, 1)
                elif name == "write":
                    c = i
                    pe.wait_ge(s_u, n * 4 + c + 1)
                    if c == 0:
                        pe.wait_ge(s_keys, n + 1)
                    for v in range(VH):
                        x = c * VH + v
                        mm = pe.matmul(B0[:, v * P:(v + 1) * P], keys[:, p, x, :], U[:, x, :], start=True, stop=True)
                    mm.then_inc(s_stp, 1)
                elif name == "out":
                    c = i
                    if c == 0:
                        pe.wait_ge(s_p, n * 2 + 2)
                        pe.wait_ge(s_r, n * 6 + 6)
                    pe.wait_ge(s_u, n * 4 + (4 if c >= 2 else c + 1))
                    for v in range(VH):
                        x = c * VH + v
                        mm = pe.matmul((B0, B1)[c // 2][:, (x % 4) * P:(x % 4 + 1) * P], pT[:, p, x, :], U[:, x, :], start=True, stop=True)
                    if c % 2:
                        mm.then_inc(s_pup, 1)
                elif name == "turn":
                    if before_last(n):
                        pe.wait_ge(s_zs, (n + 1) * 2 + i + 1)
                    pe.wait_ge(s_on, n * 2 + i + 1)
                    for x in range(4):
                        mm = pe.transpose((B2, B3)[i][:, x * P:(x + 1) * P], og[:, 4 * i + x, :], ident)
                    mm.then_inc(s_gtp, 1)
                elif name == "project":
                    if b == 0 and i == 0:
                        pe.wait_ge(s_wog, head + 1)
                    h, c = divmod(i, 2)
                    if c == 0:
                        pe.wait_ge(s_gt, n * 2 + h + 1)
                    for v in range(VH):
                        mm = pe.matmul((B0, B1)[h][:, 256 * c:256 * c + 256], ogT[:, 2 * i + v, :], wo[:, v, :],
                                       start=(v == 0), stop=(v == VH - 1))
                    if c == 1:
                        mm.then_inc(s_opp, 1)

            for step in FRONT:
                run(step, 0, 0, 0)
            with pe.Fori(0, KH - 1) as kh:
                for step, n, b, head in body_steps(kh, False):
                    run(step, n, b, head)
            for step, n, b, head in body_steps(KH - 1, True):
                run(step, n, b, head)
            moe_tensor(pe)

        @block.scalar
        def _(act):
            gates_scalar(act)
            act.wait_ge(s_const, CONSTS)

            def run(step, n, b, head):
                p = b % 2
                later = past_first(n)
                name, i = step
                if name == "prepare":
                    prepare_scalar(act, i, 0)
                elif name == "proj":
                    if i == 0:
                        act.wait_ge(s_sc, n * 2 + 1)
                    g, k = divmod(i, KT)
                    if k == KT - 1:
                        act.wait_ge(s_proj, n * 4 + g + 1)
                        act.activation(conv[:, g, :], FB[g][:, :], ACT.Copy,
                                       scale=cw[:, p, g * TAPS + 3:g * TAPS + 4]).then_inc(s_tap, 1)
                elif name == "silu":
                    for g in (2 * i, 2 * i + 1):
                        act.wait_ge(s_conv, n * 12 + 3 * g + 3)
                        dst = qkT[:, p, g, :] if g < 2 else vT[:, g - 2, :]
                        act.activation(dst, conv[:, g, :], ACT.Silu).then_inc(s_silu, 1)
                elif name == "gate" and i % 2 == 1:
                    act.wait_ge(s_zp, n * 2 + i // 2 + 1)
                    act.activation(zs[:, p, i - 1:i + 1, :], (B2, B3)[i // 2][:, :].rearrange("p (c n) -> p c n", c=2),
                                   ACT.Silu).then_inc(s_zs, 1)
                elif name == "values":
                    act.wait_ge(s_vtp, n * 2 + i + 1)
                    if i == 0:
                        act.wait_ge(s_small, n * 2 + 1)
                    for c in range(2):
                        act.activation(vals[:, p, 4 * i + 2 * c:4 * i + 2 * c + 2, :],
                                       bank4(FB[2 + i])[:, 2 * c:2 * c + 2], ACT.Copy,
                                       scale=nk[:, 2 * i + c:2 * i + c + 1]).then_inc(s_vals, 1)
                elif name == "squares":
                    for t, (a, src) in enumerate(((1, F1), (0, F0))):
                        act.wait_ge(s_ktp, n * 2 + t + 1)
                        for c in range(CH):
                            x = a * CH + c
                            act.activation(og2[:, x, :], src[:, c * P:(c + 1) * P], ACT.Square,
                                           accum_out=ssum[:, x:x + 1]).then_inc(s_sq, 1)
                elif name == "decay":
                    act.wait_ge(s_decp, n * 2 + i + 1)
                    act.activation(half(dec, i), bank4((B2, B3)[i]), ACT.Exp).then_inc(s_dec, 1)
                elif name == "start":
                    act.wait_ge(s_xp, n + 1)
                    act.activation(X[:, :, :], F0[:, :].bitcast(F16).rearrange("p (x n) -> p x n", x=CELLS), ACT.Copy).then_inc(s_x0, 1)
                elif name == "grow":
                    i, h = divmod(i, 2)
                    mxb, xb = level_banks(i)
                    for dst, h, src, t in (((X, 0, xb[0], 1),), ((X, 1, xb[1], 3), (XT, 1, mxb[1], 4)))[h]:
                        act.wait_ge(s_xp4, n * 24 + 4 * i + t)
                        act.activation(blocks(half(dst, h), i, dst is XT), packed(src, i), ACT.Copy).then_inc(s_x, 1)
                elif name == "solve":
                    act.wait_ge(s_up, n * 4 + i + 1)
                    act.activation(U[:, 2 * i:2 * i + 2, :], B1[:, 0:256].rearrange("p (v n) -> p v n", v=VH),
                                   ACT.Copy, scale=-1.0 if i else 1.0).then_inc(s_u, 1)
                elif name == "power":
                    act.wait_ge(s_og, n * 2 + i + 1)
                    for x in range(4 * i, 4 * i + 4):
                        act.activation(og2[:, x, :], og[:, x, :], ACT.Square, accum_out=ms[:, 0, x:x + 1]).then_inc(s_ms, 1)
                elif name == "turn":
                    act.wait_ge(s_gtp, n * 2 + i + 1)
                    act.activation(half(ogT, i), bank4((B2, B3)[i]), ACT.Copy).then_inc(s_gt, 1)

            for step in FRONT:
                run(step, 0, 0, 0)
            with act.Fori(0, KH - 1) as kh:
                for step, n, b, head in body_steps(kh, False):
                    run(step, n, b, head)
            for step, n, b, head in body_steps(KH - 1, True):
                run(step, n, b, head)
            moe_scalar(act)

        @block.vector
        def _(dve):
            dve.wait_ge(s_early, EARLY_LOADS)
            gates_vector(dve)
            dve.wait_ge(s_const, CONSTS)

            def run(step, n, b, head):
                p = b % 2
                later = past_first(n)
                name, i = step
                if name == "prepare":
                    prepare_vector(dve, i, 0)
                elif name == "scalars":
                    if later:
                        dve.wait_ge(s_tap, (n - 1) * GROUPS)
                        dve.wait_ge(s_seg, n * 2)
                    else:
                        dve.wait_ge(s_scall, 3)
                        dve.wait_ge(s_gact, GACT)
                    dve.tensor_scalar(cw[:, p, :], cw_all[:, bass.ds(head, 1), :].rearrange("p o n -> p (o n)"),
                                      1.0, None, ALU.mult).then_inc(s_sc, 1)
                    dve.tensor_scalar(sc[:, p, :], sc_all[:, bass.ds(n, 1), :].rearrange("p o n -> p (o n)"),
                                      1.0, None, ALU.mult).then_inc(s_sc, 1)
                elif name == "conv":
                    g, j = i // 3, i % 3 + 1
                    if j == 1:
                        dve.wait_ge(s_tap, n * 4 + g + 1)
                    else:
                        dve.wait_ge(s_conv, n * 12 + i)
                    dve.scalar_tensor_tensor(conv[:, g, j:], FB[g][:, 0:SEQ - j], cw[:, p, g * TAPS + 3 - j:g * TAPS + 4 - j],
                                             conv[:, g, j:], op0=ALU.mult, op1=ALU.add).then_inc(s_conv, 1)
                elif name == "norms":
                    dve.wait_ge(s_sq, n * 2 * CH + CH)
                    dve.tensor_scalar(ss[:, CH:], ssum[:, CH:], 1e-6, None, ALU.add).then_inc(s_ss, 1)
                    dve.wait_ge(s_ss, n * 3 + 1)
                    dve.reciprocal(rk2[:, :], ss[:, CH:]).then_inc(s_ss, 1)
                    dve.wait_ge(s_ss, n * 3 + 2)
                    dve.tensor_tensor(kfac[:, :].rearrange("p (c v) -> p c v", v=VH),
                                      scal(p, Q_KEYS, 0, CELLS).rearrange("p (c v) -> p c v", v=VH),
                                      rk2[:, :].unsqueeze(2).broadcast_to([P, CH, VH]), ALU.mult).then_inc(s_kfac, 1)
                    dve.wait_ge(s_sq, (n + 1) * 2 * CH)
                    dve.tensor_scalar(ss[:, 0:CH], ssum[:, 0:CH], float(P), P * 1e-6, ALU.mult, ALU.add).then_inc(s_ss, 1)
                elif name == "keys":
                    dve.wait_ge(s_ktp, n * 2 + 1)
                    dve.wait_ge(s_kfac, n + 1)
                    dve.tensor_tensor(keys[:, p].rearrange("p (c v) n -> p c v n", v=VH),
                                      F1[:, :].rearrange("p (c n) -> p c n", c=CH).unsqueeze(2).broadcast_to([P, CH, VH, P]),
                                      kfac[:, :].rearrange("p (c v) -> p c v", v=VH).unsqueeze(3).broadcast_to([P, CH, VH, P]),
                                      ALU.mult).then_inc(s_keys, 1)
                elif name == "system":
                    dst, src, done = ((m32T[:, :, :], F0, s_m), (pT[:, p], F1, s_p))[i]
                    dve.wait_ge(s_kq, n * 2 + i + 1)
                    for c in range(CH):
                        if i == 0 and c % 2 == 0:
                            dve.wait_ge(s_decb, n * 2 + c // 2 + 1)
                            if c == 0 and later:
                                dve.wait_ge(s_mlo, n)
                        op = dve.scalar_tensor_tensor(dst[:, 2 * c:2 * c + 2, :],
                                                      src[:, c * P:(c + 1) * P].unsqueeze(1).broadcast_to([P, VH, P]),
                                                      rk2[:, c:c + 1], decb[:, 2 * c:2 * c + 2, :],
                                                      op0=ALU.mult, op1=ALU.mult)
                        if c % 2 == 1:
                            op.then_inc(done, 1)
                elif name == "pairs":
                    for h in range(2):
                        dve.wait_ge(s_mhi, n * 2 + h + 1)
                        dve.tensor_tensor(half(XT, h), half(mhiT, h), lev[:, 0, :].unsqueeze(1).broadcast_to([P, 4, P]),
                                          ALU.mult).then_inc(s_pair, 1)
                elif name == "join":
                    i, h = divmod(i, 2)
                    dve.wait_ge(s_np, n * 12 + 2 * i + h + 1)
                    if i == 0 and h == 0:
                        dve.wait_ge(s_ident, len(LEVELS))
                    shape = [P, 4, P // (2 * LEVELS[i]), LEVELS[i]]
                    dve.tensor_tensor(blocks(half(N[:, i], h), i, 0), packed(level_banks(i)[0][h], i),
                                      blocks(lev[:, 1 + i:2 + i, :], i, 0).broadcast_to(shape), ALU.mult).then_inc(s_n, 1)
                elif name == "grow" and i % 2 == 0:
                    i = i // 2
                    dve.wait_ge(s_xp4, n * 24 + 4 * i + 2)
                    dve.tensor_copy(blocks(half(XT, 0), i, 1), packed(level_banks(i)[0][0], i)).then_inc(s_xt0, 1)
                elif name == "newton":
                    h = i
                    dve.wait_ge(s_resp, n * 2 + h + 1)
                    dve.tensor_tensor(half(res, h), ident.unsqueeze(1).broadcast_to([P, 4, P]), bank4(FB[h]),
                                      ALU.subtract).then_inc(s_res, 1)
                elif name == "finish":
                    h = i
                    dve.wait_ge(s_newp, n * 2 + h + 1)
                    dve.tensor_tensor(half(TT[:, p], h), bank4(FB[2 + h]), half(XT, h), ALU.add).then_inc(s_new, 1)
                elif name == "read":
                    dve.wait_ge(s_ksp, n * 3 + i)
                    for v in range(VH):
                        x = i * VH + v
                        dve.scalar_tensor_tensor(rhs[:, x, :], B0[:, v * P:(v + 1) * P], scal(p, Q_EG, x),
                                                 vals[:, p, x, :], op0=ALU.mult, op1=ALU.subtract).then_inc(s_r, 1)
                elif name == "write":
                    dve.wait_ge(s_stp, n * 3 + i + 1)
                    for v in range(VH):
                        x = i * VH + v
                        new, got = S[:, i + 1, v * P:(v + 1) * P], B0[:, v * P:(v + 1) * P]
                        if i == 0:
                            dve.tensor_copy(new, got).then_inc(s_st, 1)
                        else:
                            dve.scalar_tensor_tensor(new, S[:, i, v * P:(v + 1) * P], scal(p, Q_EEND, x), got,
                                                     op0=ALU.mult, op1=ALU.add).then_inc(s_st, 1)
                elif name == "recalled":
                    h = i
                    dve.wait_ge(s_qsp, n * 2 + h + 1)
                    a = 2 if h == 0 else 0
                    dve.tensor_tensor(qs[:, 4 * h + a:4 * h + 4, :], bank4((B2, B3)[h])[:, a:4],
                                      scal(p, Q_EG, 4 * h + a, 4 - a).unsqueeze(2).broadcast_to([P, 4 - a, P]),
                                      ALU.mult).then_inc(s_qs, 1)
                elif name == "gated":
                    dve.wait_ge(s_pup, n * 2 + i + 1)
                    dve.wait_ge(s_qs, n * 2 + i + 1)
                    src = bank4((B0, B1)[i])
                    a = 2 if i == 0 else 0
                    if i == 0:
                        dve.wait_ge(s_zq, n + 1)
                        dve.tensor_tensor(og[:, 0:2, :], src[:, 0:2], zs[:, p, 0, :].rearrange("p (v n) -> p v n", v=VH),
                                          ALU.mult).then_inc(s_o, 1)
                    x = slice(4 * i + a, 4 * i + 4)
                    dve.tensor_tensor(qs[:, x, :], src[:, a:4], qs[:, x, :], ALU.add).then_inc(s_o, 1)
                    dve.wait_ge(s_o, n * 3 + 2 + i)
                    dve.tensor_tensor(og[:, x, :], qs[:, x, :],
                                      zs[:, p, 2 * i + a // 2:2 * i + 2, :].rearrange("p c (v n) -> p (c v) n", v=VH),
                                      ALU.mult).then_inc(s_og, 1)
                elif name == "factor":
                    dve.wait_ge(s_ms, (n + 1) * CELLS)
                    dve.tensor_scalar(ms[:, 1, :], ms[:, 0, :], 1.0 / P, 1e-6, ALU.mult, ALU.add).then_inc(s_mse, 1)
                elif name == "project" and i % 2 == 1:
                    dve.wait_ge(s_opp, n * 2 + i // 2 + 1)
                    a = acc[:, b * CH + i - 1:b * CH + i + 1, :]
                    dve.tensor_tensor(a, (B0, B1)[i // 2][:, :].rearrange("p (c n) -> p c n", c=2), a,
                                      ALU.add).then_inc(s_acc, 1)

            dve.wait_ge(s_zero, 1)
            for step in FRONT:
                run(step, 0, 0, 0)
            with dve.Fori(0, KH - 1) as kh:
                for step, n, b, head in body_steps(kh, False):
                    run(step, n, b, head)
            for step, n, b, head in body_steps(KH - 1, True):
                run(step, n, b, head)
            moe_vector(dve)


def kernel(**inputs):
    import ml_dtypes
    import numpy as np
    import concourse.bacc as bacc
    from concourse.bass_utils import run_bass_kernel_spmd

    def arr(name):
        return np.asarray(inputs["L0_" + name])

    x = arr("attn_hidden_states").reshape(TILES * P, D)
    w_qkv, w_z = arr("attn_w_qkv"), arr("attn_w_z")
    kdim = KH * P
    q, k = (w_qkv[:, i * kdim:(i + 1) * kdim].reshape(KT, P, KH, P) for i in range(2))
    v, z = (w.reshape(KT, P, KH, VH * P) for w in (w_qkv[:, 2 * kdim:], w_z))
    heads = np.concatenate([q, k, v, z], axis=3).transpose(2, 1, 0, 3).reshape(KH, P, -1)
    cw = arr("attn_conv_w")
    cq, ck = (cw[i * kdim:(i + 1) * kdim].reshape(KH, 1, P, TAPS) for i in range(2))
    cv = cw[2 * kdim:].reshape(KH, VH, P, TAPS)
    conv_w = np.concatenate([cq, ck, cv], axis=1).transpose(2, 0, 1, 3).reshape(P, KH, GROUPS * TAPS)
    i, j = np.arange(P)[:, None], np.arange(P)[None, :]
    eye = np.eye(P, dtype=np.float32)
    levels = [eye - ((j == i + 1) & (i % 2 == 0))]
    levels += [eye - ((i // (2 * s) == j // (2 * s)) & (i // s == j // s + 1)) for s in LEVELS]
    late = np.where(j < i, -30000.0, 0.0)
    gate, up = (np.concatenate([arr("ffn_w_" + n), arr("ffn_sw_" + n)[None]]) for n in ("gate", "up"))
    down = np.concatenate([arr("ffn_w_down"), arr("ffn_sw_down")[None]])
    arrays = {
        "x_rows": x,
        "x_cols": x.T,
        "w_heads": heads,
        "w_ab": np.concatenate([arr("attn_w_a"), arr("attn_w_b")], axis=1),
        "conv_w": conv_w,
        "dt_bias": np.broadcast_to(arr("attn_dt_bias"), (P, KH * VH)),
        "a_log": np.broadcast_to(arr("attn_A_log"), (P, KH * VH)),
        "gamma": arr("attn_norm_gamma").reshape(P, 1),
        "w_out": arr("attn_w_out").reshape(KH, VH, P, D).transpose(0, 2, 1, 3),
        "rms_w": arr("ffn_rms_weight").reshape(KT, P).T,
        "router_w": arr("ffn_router_w").reshape(KT, P, NE).transpose(1, 0, 2),
        "gate_up": np.concatenate([gate, up], axis=2).reshape(NX, KT, P, 2 * P).transpose(2, 0, 1, 3),
        "down": down.transpose(1, 0, 2),
        "tri": np.stack([i <= j, i > j, i == j, i == i + 0 * j], axis=1).astype(np.float32),
        "levels16": np.stack(levels, axis=1).astype(np.float16),
        "neg_mask": np.concatenate([late] * 4 + [eye], axis=1).astype(ml_dtypes.bfloat16),
        "ident16": eye.astype(np.float16),
        "iota8": np.broadcast_to(np.arange(NE, dtype=np.float32), (P, NE)),
        "exponents": np.broadcast_to(np.array([-0.5, 0.5, np.e], np.float32), (P, 3)),
    }
    nc = bacc.Bacc("TRN2", target_bir_lowering=False, num_devices=1)
    args, data = [], {}
    for name, a in arrays.items():
        data[name] = np.ascontiguousarray(a)
        args.append(nc.dram_tensor(name, a.shape, mybir.dt.from_np(a.dtype), kind="ExternalInput").ap())
    args.append(nc.dram_tensor("out", (TILES * P, D), F32, kind="ExternalOutput").ap())
    build_kernel(nc, *args)
    r = run_bass_kernel_spmd(nc, [data], core_ids=[0])
    return r.results[0]["out"].reshape(B, SEQ, D)
```
